# Optimizing a Trainium2 kernel written in Bass

```python
import numpy as np
import jax
import jax.numpy as jnp

def _softmax(x, axis=-1):
    return jax.nn.softmax(x, axis=axis)

def _gelu(x):
    return jax.nn.gelu(x, approximate=True)

def _silu(x):
    return jax.nn.silu(x)

def _sigmoid(x):
    return jax.nn.sigmoid(x)

def _layernorm(x, axis=-1, eps=1e-05):
    m = jnp.mean(x, axis=axis, keepdims=True)
    v = jnp.var(x, axis=axis, keepdims=True)
    return (x - m) / jnp.sqrt(v + eps)

def _scatter_add(tgt, idx, src, axis=0):
    return tgt.at[idx].add(src)

def _segment_sum(src, seg, n):
    return jax.ops.segment_sum(src, seg, n)
kernel_name = 'mk_seq_postln_d1_jaxref_r2_d9e247'

def setup_inputs(seed: int=0):
    np.random.seed(seed)
    _w = jnp.asarray

    def _L0_attn_setup():
        import jax, jax.numpy as jnp
        import numpy as np
        from jax import lax
        B, T, C, H = (4, 1024, 512, 16)
        K = C // H
        E_MIX, E_DEC = (32, 64)
        EPS = 1e-05 * 8 ** 2

        def _rwkv6_tmix(x, time_maa_x, time_maa_w, time_maa_k, time_maa_v, time_maa_r, time_maa_g, maa_w1, maa_w2, time_decay, td_w1, td_w2, u, Wr, Wk, Wv, Wg, Wo, ln_g, ln_b):
            b, t, c = x.shape
            x_prev = jnp.pad(x, ((0, 0), (1, 0), (0, 0)))[:, :t]
            xx = x_prev - x
            mix = jnp.tanh((x + xx * time_maa_x) @ maa_w1).reshape(b, t, 5, E_MIX)
            mix = jnp.einsum('btfe,fec->fbtc', mix, maa_w2)
            mw, mk, mv, mr, mg = mix
            xw = x + xx * (time_maa_w + mw)
            xk = x + xx * (time_maa_k + mk)
            xv = x + xx * (time_maa_v + mv)
            xr = x + xx * (time_maa_r + mr)
            xg = x + xx * (time_maa_g + mg)
            r = xr @ Wr.T
            k = xk @ Wk.T
            v = xv @ Wv.T
            g = jax.nn.silu(xg @ Wg.T)
            w = time_decay + jnp.tanh(xw @ td_w1) @ td_w2
            decay = jnp.exp(-jnp.exp(w))
            to_tbhk = lambda a: a.reshape(b, t, H, K).transpose(1, 0, 2, 3)
            rs, ks_, vs, ds = map(to_tbhk, (r, k, v, decay))

            def step(S, inp):
                r_t, k_t, v_t, d_t = inp
                kv = k_t[..., :, None] * v_t[..., None, :]
                y = jnp.einsum('bhk,bhkj->bhj', r_t, S + u[None, :, :, None] * kv)
                S = d_t[..., None] * S + kv
                return (S, y)
            S0 = jnp.zeros((b, H, K, K), x.dtype)
            _, y = lax.scan(step, S0, (rs, ks_, vs, ds))
            y = y.transpose(1, 0, 2, 3)
            mu = y.mean(-1, keepdims=True)
            var = y.var(-1, keepdims=True)
            y = ((y - mu) / jnp.sqrt(var + EPS)).reshape(b, t, c) * ln_g + ln_b
            return y * g @ Wo.T
        key = jax.random.key(seed)
        ks = jax.random.split(key, 24)
        u01 = lambda k, s: jax.random.uniform(k, s, jnp.float32, -0.01, 0.01)
        nrm = lambda k, s, sc: jax.random.normal(k, s, jnp.float32) * sc
        return {'x': jax.random.normal(ks[0], (B, T, C), jnp.float32), 'time_maa_x': jax.random.uniform(ks[1], (1, 1, C)), 'time_maa_w': jax.random.uniform(ks[2], (1, 1, C)), 'time_maa_k': jax.random.uniform(ks[3], (1, 1, C)), 'time_maa_v': jax.random.uniform(ks[4], (1, 1, C)), 'time_maa_r': jax.random.uniform(ks[5], (1, 1, C)), 'time_maa_g': jax.random.uniform(ks[6], (1, 1, C)), 'maa_w1': u01(ks[7], (C, 5 * E_MIX)), 'maa_w2': u01(ks[8], (5, E_MIX, C)), 'time_decay': jax.random.uniform(ks[9], (1, 1, C), jnp.float32, -6.0, -1.0), 'td_w1': u01(ks[10], (C, E_DEC)), 'td_w2': u01(ks[11], (E_DEC, C)), 'u': nrm(ks[12], (H, K), 0.1), 'Wr': nrm(ks[13], (C, C), 0.02), 'Wk': nrm(ks[14], (C, C), 0.02), 'Wv': nrm(ks[15], (C, C), 0.02), 'Wg': nrm(ks[16], (C, C), 0.02), 'Wo': nrm(ks[17], (C, C), 0.02), 'ln_g': jnp.ones((C,), jnp.float32), 'ln_b': jnp.zeros((C,), jnp.float32)}
    _L0_attn_in = _L0_attn_setup()

    def _L0_ffn_setup():
        import jax, jax.numpy as jnp
        import numpy as np
        EPS = 1e-06
        LN_EPS = 1e-05

        def _absmean_core(W):
            gamma = jnp.mean(jnp.abs(W)) + EPS
            Ws = W / gamma
            Wq = jnp.sign(Ws) * jnp.minimum(jnp.round(jnp.abs(Ws)), 1.0)
            return (Wq, gamma)

        @jax.custom_vjp
        def absmean(W):
            return _absmean_core(W)[0]

        def _absmean_fwd(W):
            Wq, gamma = _absmean_core(W)
            return (Wq, gamma)

        def _absmean_bwd(gamma, g):
            return (g / gamma,)
        absmean.defvjp(_absmean_fwd, _absmean_bwd)

        def layernorm(x, w, b, eps=LN_EPS):
            mu = jnp.mean(x, axis=-1, keepdims=True)
            var = jnp.mean((x - mu) ** 2, axis=-1, keepdims=True)
            return (x - mu) * jax.lax.rsqrt(var + eps) * w + b
        key = jax.random.key(seed)
        k1, k2, k3 = jax.random.split(key, 3)
        d, h = (512, 2048)
        B, T = (8, 1024)
        return {'x': jax.random.normal(k1, (B, T, d), jnp.float32), 'W_fc': jax.random.normal(k2, (h, d), jnp.float32), 'ln_w': jnp.ones((h,), jnp.float32), 'ln_b': jnp.zeros((h,), jnp.float32), 'W_proj': jax.random.normal(k3, (d, h), jnp.float32)}
    _L0_ffn_in = _L0_ffn_setup()
    _d = {'L0_attn_x': _L0_attn_in['x'], 'L0_attn_time_maa_x': _L0_attn_in['time_maa_x'], 'L0_attn_time_maa_w': _L0_attn_in['time_maa_w'], 'L0_attn_time_maa_k': _L0_attn_in['time_maa_k'], 'L0_attn_time_maa_v': _L0_attn_in['time_maa_v'], 'L0_attn_time_maa_r': _L0_attn_in['time_maa_r'], 'L0_attn_time_maa_g': _L0_attn_in['time_maa_g'], 'L0_attn_maa_w1': _L0_attn_in['maa_w1'], 'L0_attn_maa_w2': _L0_attn_in['maa_w2'], 'L0_attn_time_decay': _L0_attn_in['time_decay'], 'L0_attn_td_w1': _L0_attn_in['td_w1'], 'L0_attn_td_w2': _L0_attn_in['td_w2'], 'L0_attn_u': _L0_attn_in['u'], 'L0_attn_Wr': _L0_attn_in['Wr'], 'L0_attn_Wk': _L0_attn_in['Wk'], 'L0_attn_Wv': _L0_attn_in['Wv'], 'L0_attn_Wg': _L0_attn_in['Wg'], 'L0_attn_Wo': _L0_attn_in['Wo'], 'L0_attn_ln_g': _L0_attn_in['ln_g'], 'L0_attn_ln_b': _L0_attn_in['ln_b'], 'L0_ffn_W_fc': _L0_ffn_in['W_fc'], 'L0_ffn_ln_w': _L0_ffn_in['ln_w'], 'L0_ffn_ln_b': _L0_ffn_in['ln_b'], 'L0_ffn_W_proj': _L0_ffn_in['W_proj']}
    _x0 = _d['L0_attn_x']
    _d['L0_attn_x'] = jax.random.normal(jax.random.fold_in(jax.random.key(seed), 1), (4, 2048, 512), dtype=_x0.dtype)
    del _x0
    return _d

def reference(L0_attn_x, L0_attn_time_maa_x, L0_attn_time_maa_w, L0_attn_time_maa_k, L0_attn_time_maa_v, L0_attn_time_maa_r, L0_attn_time_maa_g, L0_attn_maa_w1, L0_attn_maa_w2, L0_attn_time_decay, L0_attn_td_w1, L0_attn_td_w2, L0_attn_u, L0_attn_Wr, L0_attn_Wk, L0_attn_Wv, L0_attn_Wg, L0_attn_Wo, L0_attn_ln_g, L0_attn_ln_b, L0_ffn_W_fc, L0_ffn_ln_w, L0_ffn_ln_b, L0_ffn_W_proj):

    def _L0_attn_ref(x, time_maa_x, time_maa_w, time_maa_k, time_maa_v, time_maa_r, time_maa_g, maa_w1, maa_w2, time_decay, td_w1, td_w2, u, Wr, Wk, Wv, Wg, Wo, ln_g, ln_b):
        import jax, jax.numpy as jnp
        import numpy as np
        from jax import lax
        B, T, C, H = (4, 1024, 512, 16)
        K = C // H
        E_MIX, E_DEC = (32, 64)
        EPS = 1e-05 * 8 ** 2

        def _rwkv6_tmix(x, time_maa_x, time_maa_w, time_maa_k, time_maa_v, time_maa_r, time_maa_g, maa_w1, maa_w2, time_decay, td_w1, td_w2, u, Wr, Wk, Wv, Wg, Wo, ln_g, ln_b):
            b, t, c = x.shape
            x_prev = jnp.pad(x, ((0, 0), (1, 0), (0, 0)))[:, :t]
            xx = x_prev - x
            mix = jnp.tanh((x + xx * time_maa_x) @ maa_w1).reshape(b, t, 5, E_MIX)
            mix = jnp.einsum('btfe,fec->fbtc', mix, maa_w2)
            mw, mk, mv, mr, mg = mix
            xw = x + xx * (time_maa_w + mw)
            xk = x + xx * (time_maa_k + mk)
            xv = x + xx * (time_maa_v + mv)
            xr = x + xx * (time_maa_r + mr)
            xg = x + xx * (time_maa_g + mg)
            r = xr @ Wr.T
            k = xk @ Wk.T
            v = xv @ Wv.T
            g = jax.nn.silu(xg @ Wg.T)
            w = time_decay + jnp.tanh(xw @ td_w1) @ td_w2
            decay = jnp.exp(-jnp.exp(w))
            to_tbhk = lambda a: a.reshape(b, t, H, K).transpose(1, 0, 2, 3)
            rs, ks_, vs, ds = map(to_tbhk, (r, k, v, decay))

            def step(S, inp):
                r_t, k_t, v_t, d_t = inp
                kv = k_t[..., :, None] * v_t[..., None, :]
                y = jnp.einsum('bhk,bhkj->bhj', r_t, S + u[None, :, :, None] * kv)
                S = d_t[..., None] * S + kv
                return (S, y)
            S0 = jnp.zeros((b, H, K, K), x.dtype)
            _, y = lax.scan(step, S0, (rs, ks_, vs, ds))
            y = y.transpose(1, 0, 2, 3)
            mu = y.mean(-1, keepdims=True)
            var = y.var(-1, keepdims=True)
            y = ((y - mu) / jnp.sqrt(var + EPS)).reshape(b, t, c) * ln_g + ln_b
            return y * g @ Wo.T
        return _rwkv6_tmix(x, time_maa_x, time_maa_w, time_maa_k, time_maa_v, time_maa_r, time_maa_g, maa_w1, maa_w2, time_decay, td_w1, td_w2, u, Wr, Wk, Wv, Wg, Wo, ln_g, ln_b)

    def _L0_ffn_ref(x, W_fc, ln_w, ln_b, W_proj):
        import jax, jax.numpy as jnp
        import numpy as np
        EPS = 1e-06
        LN_EPS = 1e-05

        def _absmean_core(W):
            gamma = jnp.mean(jnp.abs(W)) + EPS
            Ws = W / gamma
            Wq = jnp.sign(Ws) * jnp.minimum(jnp.round(jnp.abs(Ws)), 1.0)
            return (Wq, gamma)

        @jax.custom_vjp
        def absmean(W):
            return _absmean_core(W)[0]

        def _absmean_fwd(W):
            Wq, gamma = _absmean_core(W)
            return (Wq, gamma)

        def _absmean_bwd(gamma, g):
            return (g / gamma,)
        absmean.defvjp(_absmean_fwd, _absmean_bwd)

        def layernorm(x, w, b, eps=LN_EPS):
            mu = jnp.mean(x, axis=-1, keepdims=True)
            var = jnp.mean((x - mu) ** 2, axis=-1, keepdims=True)
            return (x - mu) * jax.lax.rsqrt(var + eps) * w + b
        h = jnp.einsum('btd,hd->bth', x, absmean(W_fc))
        h = jax.nn.gelu(h, approximate=False)
        h = layernorm(h, ln_w, ln_b)
        return jnp.einsum('bth,dh->btd', h, absmean(W_proj))
    x = L0_attn_x
    x = _layernorm(x + _L0_attn_ref(x, L0_attn_time_maa_x, L0_attn_time_maa_w, L0_attn_time_maa_k, L0_attn_time_maa_v, L0_attn_time_maa_r, L0_attn_time_maa_g, L0_attn_maa_w1, L0_attn_maa_w2, L0_attn_time_decay, L0_attn_td_w1, L0_attn_td_w2, L0_attn_u, L0_attn_Wr, L0_attn_Wk, L0_attn_Wv, L0_attn_Wg, L0_attn_Wo, L0_attn_ln_g, L0_attn_ln_b), axis=-1)
    x = _layernorm(x + _L0_ffn_ref(x, L0_ffn_W_fc, L0_ffn_ln_w, L0_ffn_ln_b, L0_ffn_W_proj), axis=-1)
    return x

_drawn_inputs = setup_inputs


def setup_inputs(seed=0):
    import zlib

    import numpy as np

    out = dict(_drawn_inputs(seed))
    spreads = {'L0_attn_ln_g': (1.0, 0.6),
     'L0_attn_ln_b': (0.0, 0.777),
     'L0_ffn_ln_w': (1.0, 0.2),
     'L0_ffn_ln_b': (0.0, 0.1)}
    factors = {'L0_attn_time_maa_x': 8.0,
     'L0_attn_time_maa_w': 64.0,
     'L0_attn_maa_w1': 8.0,
     'L0_attn_maa_w2': 8.0,
     'L0_attn_td_w1': 64.0,
     'L0_attn_td_w2': 64.0,
     'L0_attn_u': 22.225}
    for name, (base, spread) in spreads.items():
        noise = np.random.default_rng([zlib.crc32(name.encode()), seed]).standard_normal(out[name].shape)
        drawn = base * np.exp(spread * noise) if base else spread * noise
        out[name] = jnp.asarray(drawn.astype(out[name].dtype))
    for name, factor in factors.items():
        out[name] = (out[name] * factor).astype(out[name].dtype)
    return out
```

```python
from contextlib import ExitStack

import numpy as np

import concourse.bass as bass
from concourse import mybir

F32 = mybir.dt.float32
F16 = mybir.dt.float16
U32 = mybir.dt.uint32
ALU = mybir.AluOpType
ACT = mybir.ActivationFunctionType
AX = mybir.AxisListType

B, T, C = 4, 2048, 512
HEADS, HD = 16, 32
HID = 2048
MIXR, DECR = 32, 64
CH = 64
COLS = B * CH
KC = C // 128
HPG = 128 // HD
MH = HID // 128
TILES = T // CH
PAIRS = B // 2
BLK = 32
GN_EPS = 1e-5 * 8 ** 2
LN_EPS = 1e-5
GAMMA_EPS = 1e-6
LEVELS = (2, 4, 8, 16)

MAA_X, MAA_W, MAA_K, MAA_V, MAA_R, MAA_G, DECAY, U, LN_G, LN_B = range(10)
NPAR = 10
MIX_PAR = (MAA_W, MAA_K, MAA_V, MAA_R, MAA_G)
W_R, W_K, W_V, W_G, W_O = range(5)

P_SEQ = [("w1a", "act"), ("w1b", "act"), ("mw0", "dve"), ("mw1", "dve"), ("mk0", "dve"), ("mk1", "dve"),
         ("td1", "act"), ("mv0", "dve"), ("mv1", "dve"), ("td20", "act"), ("td21", "act"), ("k0", "act"),
         ("k1", "act"), ("mr0", "dve"), ("mr1", "dve"), ("v0", "act"), ("v1", "act"), ("mg0", "dve"),
         ("mg1", "dve"), ("r0", "act"), ("r1", "act"), ("g0", "dve"), ("g1", "dve"), ("var", "act"),
         ("rb0", "dve"), ("rb1", "dve"), ("wo0", "dve"), ("wo1", "dve"), ("xt0", "dve"), ("xt1", "dve")]
W_SEQ = [("l1_0", "dve"), ("l1_1", "dve"), ("l2", "dve"), ("l4", "dve"), ("l8", "dve"), ("l16", "dve"),
         ("l32_0", "act"), ("l32_1", "act")]
X_SEQ = [("kt0", "act"), ("kt1", "act"), ("kv0", "dve"), ("kv1", "dve"), ("kv2", "dve"), ("kv3", "dve")]
F_SEQ = [(f"{n}_{p}", e) for p in range(PAIRS)
         for n, e in (("fc0", "act"), ("fc1", "act"), ("fc2", "act"), ("fc3", "act"), ("st", "dve"), ("pj", "dve"))]
RB_SEQ = {"l1_0": 0, "l1_1": 1, "l2": 0, "l4": 1, "l8": 0, "l16": 1, "l32": 0}


class Ring:

    def __init__(self, seq, depth, filled, emptied):
        self.names = [n for n, _ in seq]
        self.by = [e for _, e in seq]
        self.n, self.depth, self.filled, self.emptied = len(seq), depth, filled, emptied
        assert self.n % depth == 0

    def bank(self, name):
        return self.names.index(name) % self.depth

    def full(self, it, name):
        return it * self.n + self.names.index(name) + 1

    def read(self, it, name):
        i = self.names.index(name)
        return it * self.by.count(self.by[i]) + self.by[:i + 1].count(self.by[i])

    def wait_free(self, eng, it, name, first):
        i = self.names.index(name) - self.depth
        if i < 0 and first:
            return
        before = self.names[i % self.n]
        eng.wait_ge(self.emptied[self.by[i % self.n]], self.read(it if i >= 0 else it - 1, before))


class FeedForward:

    def __init__(self, alone, up=None, stats=None, down=None, roots=None, centre=None, finish=None):
        self.alone, self.up, self.stats, self.down = alone, up, stats, down
        self.roots, self.centre, self.finish = roots, centre, finish


def rwkv_ffn_kernel(nc, x_ch, x_tok, w_all, w1, w2a, w2b, td1, td2, par, wfc, wpj, ffn_wb, c_f32, c_mask, out,
                    tiles=TILES):
    with ExitStack() as ctx:
        def sb(name, shape, dt=F32):
            return ctx.enter_context(nc.sbuf_tensor(name, shape, dt))

        def sem(name):
            return ctx.enter_context(nc.semaphore(name))

        WALL = sb("WALL", [128, 5, KC, C])
        W1 = sb("W1", [128, KC, 5 * MIXR])
        W2A = sb("W2A", [128, C])
        TD1 = sb("TD1", [128, KC, DECR])
        TD2W2 = sb("TD2W2", [DECR + MIXR, C])
        TD2, W2B = TD2W2[0:DECR, :], TD2W2[DECR:DECR + MIXR, :]
        PAR = sb("PAR", [128, KC, NPAR])
        WFC = sb("WFC", [128, KC, HID], F16)
        WPJ = sb("WPJ", [128, MH, C], F16)
        FWB = sb("FWB", [128, 2, MH])
        WSUM = sb("WSUM", [128, C])
        BSUM = sb("BSUM", [128, C])
        CF = sb("CF", [128, c_f32.shape[1]])
        CM = sb("CM", [128, c_mask.shape[1]], U32)
        o = 0
        IDENT = CF[:, o:o + 128]; o += 128
        BLKMASK = CF[:, o:o + 128]; o += 128
        ONES = CF[:, o:o + 128]; o += 128
        SEL = CF[:, o:o + KC * HEADS].rearrange("p (c h) -> p c h", c=KC); o += KC * HEADS
        SPREAD = CF[:, o:o + KC * 128].rearrange("p (c n) -> p c n", c=KC); o += KC * 128
        MASK1 = CF[:, o:o + BLK]; o += BLK
        EPS = CF[:, o:o + 2]; o += 2
        ZERO = CF[:, o:o + 1]; o += 1

        ARENA1 = sb("ARENA1", [128, 8192])
        ARENA2 = sb("ARENA2", [128, 8192])
        RB = [ARENA1[:, 2048 * i:2048 * (i + 1)].rearrange("p (c h t) -> p c h t", c=KC, h=HPG) for i in range(2)]
        AB = ARENA1[:, 4096:6144].rearrange("p (h t) -> p h t", h=HEADS)
        A = ARENA1[:, 6144:7168]
        K1 = ARENA1[:, 7168:8192]
        KT = ARENA1[:, 7168:8192].rearrange("p (q n) -> p q n", q=PAIRS)
        S = ARENA2[:, 0:2048].rearrange("p (b c n) -> p b c n", b=B, c=KC)
        XF = [ARENA2[:, 2048 + 1024 * i:3072 + 1024 * i] for i in range(2)]
        YSB, YSQ = XF
        KM = ARENA2[:, 4096:5120]
        RM = ARENA2[:, 5120:6144]
        D = ARENA2[:, 6144:7168]
        G = ARENA2[:, 7168:8192]

        XT = sb("XT", [128, KC * B, CH + 1])
        XX = sb("XX", [128, KC * B, CH])
        XTOK = XX[:, :, :].rearrange("p q t -> p (q t)").rearrange("p (h c) -> p h c", h=PAIRS)
        TMA = sb("TMA", [128, COLS])
        TZTM = sb("TZTM", [DECR + MIXR, COLS])
        TZ, TMB = TZTM[0:DECR, :], TZTM[DECR:DECR + MIXR, :]
        TOT = {1: D}
        for n in (2, 4, 8, 16, 32, 64):
            TOT[n] = sb(f"TOT{n}", [128, KC * COLS // n])[:, :]
        V = sb("V", [128, PAIRS, C])
        KVM = D.rearrange("p (i n) -> p i n", i=2)
        RS = sb("RS", [HEADS, COLS])
        X1 = sb("X1", [128, PAIRS, C])
        BNS = sb("BNS", [128, PAIRS, 6])
        MV = sb("MV", [128, PAIRS, 2])
        RSTD = sb("RSTD", [128, PAIRS])
        XHI = sb("XHI", [128, PAIRS, KC, 128], F16)
        XLO = sb("XLO", [128, PAIRS, KC, 128], F16)
        GF = sb("GF", [128, 2, 512])
        GSQ = sb("GSQ", [128, 2, 512])
        GW = sb("GW", [128, 512])
        HHI = sb("HHI", [128, MH, 128], F16)
        HLO = sb("HLO", [128, MH, 128], F16)
        GA = sb("GA", [128, 512])
        QA = sb("QA", [128, 512])
        GR = sb("GR", [128, 2, 128])
        ST = sb("ST", [128, PAIRS, 4])
        FV, FSD, FSC = sb("FV", [128, PAIRS]), sb("FSD", [128, PAIRS]), sb("FSC", [128, PAIRS])
        FBN = sb("FBN", [128, PAIRS, 6])
        FMV = sb("FMV", [128, PAIRS, 2])
        OSD = sb("OSD", [128, PAIRS])
        OUT = sb("OUT", [128, PAIRS, C])
        PAUSE = sb("PAUSE", [1, 8])
        SC = sb("SC", [128, 32])
        AMAX = SC[:, 0:2]
        RED = GF[:, 0, 0:256]
        VMEAN = GF[:, 1, 0:KC * HEADS]

        psP = ctx.enter_context(nc.psum_tensor("psP", [128, 2, 512], F32))
        psW = ctx.enter_context(nc.psum_tensor("psW", [128, 2, 512], F32))
        psX = ctx.enter_context(nc.psum_tensor("psX", [128, 512], F32))
        psY = ctx.enter_context(nc.psum_tensor("psY", [128, 512], F32))
        psF = ctx.enter_context(nc.psum_tensor("psF", [128, 2, 512], F32))

        const_in, weights_in, wfc_in, wpj_in = sem("const_in"), sem("weights_in"), sem("wfc_in"), sem("wpj_in")
        xt_in, xtok_in, out_stored = sem("xt_in"), sem("xtok_in"), sem("out_stored")
        quantised = sem("quantised")
        su_dve, su_pe, su_act, su_pool = sem("setup_dve"), sem("setup_pe"), sem("setup_act"), sem("setup_pool")
        p_full, p_act, p_dve = sem("p_full"), sem("p_read_act"), sem("p_read_dve")
        w_full, w_act, w_dve = sem("w_full"), sem("w_read_act"), sem("w_read_dve")
        x_full, x_act, x_dve = sem("x_full"), sem("x_read_act"), sem("x_read_dve")
        f_full, f_act, f_dve = sem("f_full"), sem("f_read_act"), sem("f_read_dve")
        y_full, y_copied, y_squared = sem("y_full"), sem("y_copied"), sem("y_squared")
        xx_ready, xm_ready, xf_ready = sem("xx_ready"), sem("xm_ready"), sem("xf_ready")
        gate_tanh, ew_ready, d_ready = sem("gate_tanh"), sem("ew_ready"), sem("d_ready")
        km_ready, k1_even, k1_odd = sem("km_ready"), sem("k1_even"), sem("k1_odd")
        rb_act, rb_dve = sem("rb_act"), sem("rb_dve")
        r_scaled, k_scaled, tot_ready = sem("r_scaled"), sem("k_scaled"), sem("tot_ready")
        a_l1, ab_diag = sem("a_l1"), sem("ab_diag")
        kvm_ready, s_decayed, s_ready = sem("kvm_ready"), sem("s_decayed"), sem("s_ready")
        rs_inv, y_affine, z_ready = sem("rs_inv"), sem("y_affine"), sem("z_ready")
        bn_done, mv_ready, sd_ready, rstd_ready = sem("bn_done"), sem("mv_ready"), sem("sd_ready"), sem("rstd_ready")
        x1_ready, xhi_ready, x1_biased = sem("x1_ready"), sem("xhi_ready"), sem("x1_biased")
        g_squared, gw_ready = sem("g_squared"), sem("gw_ready")
        hhi_ready, hlo_ready, sums_added, sums_folded = sem("hhi_ready"), sem("hlo_ready"), sem("sums_added"), sem("sums_folded")
        setup_step, st_step, fsd_ready, fsc_step = sem("setup_step"), sem("st_step"), sem("fsd_ready"), sem("fsc_step")
        o_step, osd_ready, osd_inv, out_ready = sem("o_step"), sem("osd_ready"), sem("osd_inv"), sem("out_ready")

        P = Ring(P_SEQ, 2, p_full, {"act": p_act, "dve": p_dve})
        W = Ring(W_SEQ, 2, w_full, {"act": w_act, "dve": w_dve})
        X = Ring(X_SEQ, 1, x_full, {"act": x_act, "dve": x_dve})
        F = Ring(F_SEQ, 2, f_full, {"act": f_act, "dve": f_dve})

        xprev, xcur = XT[:, :, 0:CH], XT[:, :, 1:CH + 1]

        def cc(buf, c):
            return buf[:, c * COLS:(c + 1) * COLS]

        def halves(buf, n):
            v = buf.rearrange("p (q two n) -> p q two n", two=2, n=n)
            return v[:, :, 0, :], v[:, :, 1, :]

        def grow(v, n):
            return v.unsqueeze(2).broadcast_to([v.shape[0], v.shape[1], n])

        def rows(h):
            return slice(HD * h, HD * (h + 1))

        NPL = len(LEVELS) + 2
        NWEIGHTS = 7

        def over_tiles(eng, attention, feed_forward):
            attention(0, True, None)
            if tiles > 1:
                attention(1, False, feed_forward(0, True))
            if tiles > 2:
                with eng.Fori(2, tiles) as it:
                    attention(it, False, feed_forward(eng.snap(it - 1), False))
            feed_forward(tiles - 1, tiles == 1).alone()

        block = ctx.enter_context(nc.Block())

        @block.sync
        def _(sp):
            for dst, src in ((CF[:, :], c_f32), (CM[:, :], c_mask), (PAR[:, :, :], par), (FWB[:, :, :], ffn_wb)):
                sp.dma_start(dst, src).then_inc(const_in, 16)
            for k in range(4):
                sp.dma_start(ARENA1[:, 2048 * k:2048 * (k + 1)], wfc[:, 2048 * k:2048 * (k + 1)]).then_inc(wfc_in, 16)
            for k in range(4):
                sp.dma_start(ARENA2[:, 2048 * k:2048 * (k + 1)], wpj[:, 2048 * k:2048 * (k + 1)]).then_inc(wpj_in, 16)
            for dst, src in ((W1[:, :, :], w1), (W2A[:, :], w2a), (W2B[:, :], w2b), (TD1[:, :, :], td1),
                             (TD2[:, :], td2), (WALL[:, 1:4, :, :], w_all[:, 1:4, :, :])):
                sp.dma_start(dst, src).then_inc(weights_in, 16)
            sp.dma_start(WALL[:, 0:5:4, :, :], w_all[:, 0:5:4, :, :]).then_inc(weights_in, 16)

            def loads(it, first):
                if not first:
                    sp.wait_ge(xf_ready, 5 * it)
                sp.dma_start(XT[:, :, :], x_ch[it]).then_inc(xt_in, 16)
                sp.wait_ge(p_dve, P.read(it, "mg1"))
                sp.dma_start(XTOK[:, :, :], x_tok[it]).then_inc(xtok_in, 16)

            def tile(it, first, ffn):
                loads(it, first)
                if ffn:
                    ffn.alone()

            def feed_forward(j, first):
                def stores():
                    for p in range(PAIRS):
                        sp.wait_ge(out_ready, PAIRS * j + p + 1)
                        sp.dma_start(out[j, :, p, :], OUT[:, p, :]).then_inc(out_stored, 16)
                return FeedForward(alone=stores)

            over_tiles(sp, tile, feed_forward)
            sp.wait_ge(out_stored, 16 * PAIRS * tiles)

        @block.tensor
        def _(pe):
            pe.wait_ge(su_dve, 1)
            pe.wait_ge(const_in, 16 * 4)
            pe.matmul(psP[:, 0, 0:1], ONES, SC[:, 8:9], start=True, stop=True).then_inc(su_pe, 1)
            pe.wait_ge(su_dve, 2)
            pe.matmul(psP[:, 1, 0:1], ONES, SC[:, 9:10], start=True, stop=True).then_inc(su_pe, 1)
            pe.wait_ge(su_dve, 3)
            pe.transpose(psX[0:2, 0:128], SC[:, 10:12], IDENT).then_inc(su_pe, 1)
            pe.wait_ge(su_dve, 4)
            pe.matmul(psY[:, 0:1], ONES[0:2, :], SC[0:2, 14:15], start=True, stop=True)
            pe.matmul(psY[:, 1:2], ONES[0:2, :], SC[0:2, 15:16], start=True, stop=True).then_inc(su_pe, 1)
            for v in range(2):
                pe.wait_ge(su_dve, 5 + v)
                for m in range(MH):
                    for part, h in enumerate((HHI, HLO)):
                        mm = pe.matmul(psW[:, v, :], h[:, m, :], WPJ[:, m, :], start=(m == 0 and part == 0),
                                       stop=(m == MH - 1 and part == 1))
                mm.then_inc(su_pe, 1)
            pe.wait_ge(su_dve, 8)
            pe.wait_ge(su_pool, 1)
            pe.wait_ge(weights_in, 16 * NWEIGHTS)

            def tile(it, first, ffn):
                pe.wait_ge(xm_ready, it + 1)
                for name, lo, n in (("w1a", 0, 4 * MIXR), ("w1b", 4 * MIXR, MIXR)):
                    P.wait_free(pe, it, name, first)
                    for k in range(KC):
                        mm = pe.matmul(psP[0:n, P.bank(name), 0:COLS], W1[:, k, lo:lo + n], cc(XF[1], k),
                                       start=(k == 0), stop=(k == KC - 1))
                    mm.then_inc(p_full, 1)

                def mix(f, name):
                    pe.wait_ge(p_act, P.read(it, "w1a" if f < 4 else "w1b"))
                    lhs, rhs = (W2A[rows(f), :], TMA[rows(f), :]) if f < 4 else (W2B[:, :], TMB[:, :])
                    for g in range(2):
                        P.wait_free(pe, it, f"{name}{g}", first)
                        for c in range(2):
                            mm = pe.matmul(psP[:, P.bank(f"{name}{g}"), COLS * c:COLS * (c + 1)],
                                           lhs[:, 128 * (2 * g + c):128 * (2 * g + c + 1)], rhs, start=True, stop=True)
                        mm.then_inc(p_full, 1)

                def channels(name, w, f, slot):
                    pe.wait_ge(xf_ready, 5 * it + f + 1)
                    for g in range(2):
                        P.wait_free(pe, it, f"{name}{g}", first)
                        for c in range(2):
                            for k in range(KC):
                                mm = pe.matmul(psP[:, P.bank(f"{name}{g}"), COLS * c:COLS * (c + 1)],
                                               WALL[:, w, k, 128 * (2 * g + c):128 * (2 * g + c + 1)], cc(XF[slot], k),
                                               start=(k == 0), stop=(k == KC - 1))
                        mm.then_inc(p_full, 1)

                mix(0, "mw")
                mix(1, "mk")
                pe.wait_ge(xf_ready, 5 * it + 1)
                P.wait_free(pe, it, "td1", first)
                for k in range(KC):
                    mm = pe.matmul(psP[0:DECR, P.bank("td1"), 0:COLS], TD1[:, k, :], cc(XF[0], k),
                                   start=(k == 0), stop=(k == KC - 1))
                mm.then_inc(p_full, 1)
                mix(2, "mv")
                pe.wait_ge(p_act, P.read(it, "td1"))
                for g in range(2):
                    P.wait_free(pe, it, f"td2{g}", first)
                    for c in range(2):
                        mm = pe.matmul(psP[:, P.bank(f"td2{g}"), COLS * c:COLS * (c + 1)],
                                       TD2[:, 128 * (2 * g + c):128 * (2 * g + c + 1)], TZ[:, :], start=True, stop=True)
                    mm.then_inc(p_full, 1)
                channels("k", W_K, 1, 1)
                mix(3, "mr")
                pe.wait_ge(xf_ready, 5 * it + 3)
                for p in range(PAIRS):
                    P.wait_free(pe, it, f"v{p}", first)
                    for k in range(KC):
                        mm = pe.matmul(psP[:, P.bank(f"v{p}"), :], cc(XF[0], k)[:, 128 * p:128 * (p + 1)],
                                       WALL[:, W_V, k, :], start=(k == 0), stop=(k == KC - 1))
                    mm.then_inc(p_full, 1)
                mix(4, "mg")
                channels("r", W_R, 3, 1)
                channels("g", W_G, 4, 0)

                pe.wait_ge(k1_odd, it + 1)
                pe.wait_ge(k1_even, 2 * it + 2)
                for p in range(PAIRS):
                    name = f"l1_{p}"
                    W.wait_free(pe, it, name, first)
                    pe.wait_ge(rb_dve, 2 * it + p + 1)
                    pe.wait_ge(rb_act, 7 * it + p + 1)
                    for q in range(4):
                        for c in range(KC):
                            o = 128 * p + BLK * q
                            mm = pe.matmul(psW[BLK * q:BLK * (q + 1), W.bank(name), 128 * c:128 * (c + 1)],
                                           cc(K1, c)[:, o:o + BLK], RB[p][:, c, :, BLK * q:BLK * (q + 1)],
                                           start=True, stop=True, skip_group_check=True)
                    mm.then_inc(w_full, 1)
                    if ffn:
                        ffn.up(0, p)
                for i, n in enumerate(LEVELS):
                    name = f"l{n}"
                    W.wait_free(pe, it, name, first)
                    pe.wait_ge(k_scaled, NPL * it + i + 1)
                    pe.wait_ge(rb_act, 7 * it + i + 3)
                    for q in range(8):
                        for c in range(KC):
                            o = 256 * (q // 4) + 64 * c
                            mm = pe.matmul(psW[BLK * (q % 4):BLK * (q % 4 + 1), W.bank(name), o:o + 64],
                                           cc(KM, c)[:, BLK * q:BLK * (q + 1)],
                                           RB[RB_SEQ[name]][:, c, :, 16 * q:16 * (q + 1)],
                                           start=True, stop=True, skip_group_check=True)
                    mm.then_inc(w_full, 1)
                    if ffn and i < 2:
                        ffn.up(0, 2 + i)
                pe.wait_ge(k_scaled, NPL * it + 5)
                pe.wait_ge(rb_act, 7 * it + 7)
                for p in range(PAIRS):
                    name = f"l32_{p}"
                    W.wait_free(pe, it, name, first)
                    for h in range(2):
                        b = 2 * p + h
                        for c in range(KC):
                            mm = pe.matmul(psW[64 * h:64 * h + BLK, W.bank(name), 128 * c:128 * (c + 1)],
                                           cc(KM, c)[:, CH * b:CH * b + BLK], RB[0][:, c, :, BLK * b:BLK * (b + 1)],
                                           start=True, stop=True, skip_group_check=True)
                    mm.then_inc(w_full, 1)
                pe.wait_ge(k_scaled, NPL * it + 6)
                for p in range(PAIRS):
                    X.wait_free(pe, it, f"kt{p}", first)
                    for c in range(KC):
                        mm = pe.transpose(psX[:, 128 * c:128 * (c + 1)], cc(KM, c)[:, 128 * p:128 * (p + 1)], IDENT)
                    mm.then_inc(x_full, 1)
                if ffn:
                    ffn.stats(0)
                    ffn.down(0, 0)
                    ffn.down(0, 1)
                pe.wait_ge(r_scaled, NPL * it + 6)
                pe.wait_ge(p_act, P.read(it, "v1"))
                pe.wait_ge(su_pool, 2)
                if not first:
                    pe.wait_ge(s_ready, B * it)
                for p in range(PAIRS):
                    if p or not first:
                        pe.wait_ge(y_copied, 2 * it + p)
                    for c in range(KC):
                        for h in range(2):
                            b = 2 * p + h
                            pe.matmul(psY[:, 128 * c + CH * h:128 * c + CH * (h + 1)], S[:, b, c, :],
                                      cc(RM, c)[:, CH * b:CH * (b + 1)], start=(c == 0 and h == 0), stop=False,
                                      skip_group_check=True)
                    pe.wait_ge(ab_diag, 2 * it + p + 1)
                    pe.wait_ge(w_act, W.read(it, f"l32_{p}"))
                    for c in range(KC):
                        for h in range(HPG):
                            mm = pe.matmul(psY[rows(h), 128 * c:128 * (c + 1)], V[:, p, 128 * c + HD * h:128 * c + HD * (h + 1)],
                                           AB[:, HPG * c + h, :], start=False, stop=True, skip_group_check=True)
                    mm.then_inc(y_full, 1)
                    if ffn:
                        ffn.up(1, p)
                pe.wait_ge(x_act, X.read(it, "kt1"))
                for b in range(B):
                    X.wait_free(pe, it, f"kv{b}", first)
                    r = slice(CH * (b % 2), CH * (b % 2 + 1))
                    for c in range(KC):
                        mm = pe.matmul(psX[:, 128 * c:128 * (c + 1)], KT[r, b // 2, 128 * c:128 * (c + 1)],
                                       V[r, b // 2, 128 * c:128 * (c + 1)], start=True, stop=True, skip_group_check=True)
                    mm.then_inc(x_full, 1)
                if ffn:
                    ffn.up(1, 2)
                    ffn.up(1, 3)
                pe.wait_ge(y_squared, 2 * it + 2)
                P.wait_free(pe, it, "var", first)
                for k in range(KC):
                    mm = pe.matmul(psP[0:HEADS, P.bank("var"), 0:COLS], SEL[:, k, :], cc(YSQ, k), start=(k == 0), stop=(k == KC - 1))
                mm.then_inc(p_full, 1)
                if ffn:
                    ffn.stats(1)
                    ffn.down(1, 0)
                pe.wait_ge(rs_inv, it + 1)
                for g in range(2):
                    P.wait_free(pe, it, f"rb{g}", first)
                    for c in range(2):
                        mm = pe.matmul(psP[:, P.bank(f"rb{g}"), COLS * c:COLS * (c + 1)], SPREAD[0:HEADS, 2 * g + c, :],
                                       RS[:, :], start=True, stop=True)
                    mm.then_inc(p_full, 1)
                if ffn:
                    ffn.down(1, 1)
                pe.wait_ge(z_ready, it + 1)
                for p in range(PAIRS):
                    P.wait_free(pe, it, f"wo{p}", first)
                    for k in range(KC):
                        mm = pe.matmul(psP[:, P.bank(f"wo{p}"), :], cc(YSB, k)[:, 128 * p:128 * (p + 1)], WALL[:, W_O, k, :],
                                       start=(k == 0), stop=(k == KC - 1))
                    mm.then_inc(p_full, 1)
                for p in range(PAIRS):
                    pe.wait_ge(x1_ready, 2 * it + p + 1)
                    P.wait_free(pe, it, f"xt{p}", first)
                    for c in range(KC):
                        mm = pe.transpose(psP[:, P.bank(f"xt{p}"), 128 * c:128 * (c + 1)], X1[:, p, 128 * c:128 * (c + 1)], IDENT)
                    mm.then_inc(p_full, 1)

            def feed_forward(j, first):
                def up(p, g):
                    if g == 0:
                        pe.wait_ge(p_dve, P.read(j, f"xt{p}"))
                    name = f"fc{g}_{p}"
                    F.wait_free(pe, j, name, first)
                    for m in range(4):
                        for k in range(KC):
                            for part, x in enumerate((XHI, XLO)):
                                mm = pe.matmul(psF[:, F.bank(name), 128 * m:128 * (m + 1)],
                                               WFC[:, k, 128 * (4 * g + m):128 * (4 * g + m + 1)], x[:, p, k, :],
                                               start=(k == 0 and part == 0), stop=(k == KC - 1 and part == 1))
                    mm.then_inc(f_full, 1)

                def stats(p):
                    pe.wait_ge(sums_folded, 2 * j + p + 1)
                    F.wait_free(pe, j, f"st_{p}", first)
                    for i in range(2):
                        mm = pe.matmul(psF[:, F.bank(f"st_{p}"), i:i + 1], GR[:, i, :], ONES[:, 0:1], start=True, stop=True)
                    mm.then_inc(f_full, 1)

                def down(p, part):
                    if part == 0:
                        pe.wait_ge(hlo_ready, 8 * j + 4 * p + 4)
                        F.wait_free(pe, j, f"pj_{p}", first)
                    for m in range(MH // 2 * part, MH // 2 * (part + 1)):
                        for h in (HHI, HLO):
                            mm = pe.matmul(psF[:, F.bank(f"pj_{p}"), :], h[:, m, :], WPJ[:, m, :],
                                           start=(m == 0 and h is HHI), stop=(m == MH - 1 and h is HLO))
                    if part == 1:
                        mm.then_inc(f_full, 1)

                def alone():
                    for p in range(PAIRS):
                        for g in range(4):
                            up(p, g)
                        stats(p)
                        down(p, 0)
                        down(p, 1)
                return FeedForward(up=up, stats=stats, down=down, alone=alone)

            over_tiles(pe, tile, feed_forward)

        @block.scalar
        def _(act):
            act.wait_ge(su_dve, 8)
            act.wait_ge(su_pool, 2)
            act.wait_ge(weights_in, 16 * NWEIGHTS)

            def copy(o, i):
                return act.activation(o, i, ACT.Copy)

            def tile(it, first, ffn):
                act.wait_ge(p_full, P.full(it, "w1a"))
                act.activation(TMA[:, :], psP[:, P.bank("w1a"), 0:COLS], ACT.Tanh).then_inc(p_act, 1)
                act.wait_ge(p_full, P.full(it, "w1b"))
                act.activation(TMB[:, :], psP[0:MIXR, P.bank("w1b"), 0:COLS], ACT.Tanh).then_inc(p_act, 1)
                act.wait_ge(p_full, P.full(it, "td1"))
                act.activation(TZ[:, :], psP[0:DECR, P.bank("td1"), 0:COLS], ACT.Tanh).then_inc(p_act, 1)
                if not first:
                    act.wait_ge(tot_ready, NPL * it)
                    act.wait_ge(r_scaled, NPL * it)
                    act.wait_ge(k_scaled, NPL * it)
                    act.wait_ge(s_ready, B * it)
                for g in range(2):
                    act.wait_ge(p_full, P.full(it, f"td2{g}"))
                    for c in range(2):
                        k = 2 * g + c
                        e = act.activation(cc(D, k), psP[:, P.bank(f"td2{g}"), COLS * c:COLS * (c + 1)], ACT.Exp,
                                           bias=PAR[:, k, DECAY:DECAY + 1])
                    e.then_inc(p_act, 1)
                act.wait_ge(p_act, P.read(it, "td21"))
                act.activation(D, D, ACT.Exp, scale=-1.0).then_inc(d_ready, 1)
                if not first:
                    act.wait_ge(x_full, X.full(it - 1, "kv3"))
                for g in range(2):
                    act.wait_ge(p_full, P.full(it, f"k{g}"))
                    src = psP[:, P.bank(f"k{g}"), :]
                    copy(halves(K1[:, 512 * g:512 * (g + 1)], 1)[0], halves(src, 1)[0]).then_inc(k1_even, 1)
                    copy(KM[:, 512 * g:512 * (g + 1)], src).then_inc(p_act, 1)
                for p in range(PAIRS):
                    act.wait_ge(p_full, P.full(it, f"v{p}"))
                    copy(V[:, p, :], psP[:, P.bank(f"v{p}"), :]).then_inc(p_act, 1)
                for g in range(2):
                    act.wait_ge(p_full, P.full(it, f"r{g}"))
                    copy(RM[:, 512 * g:512 * (g + 1)], psP[:, P.bank(f"r{g}"), :]).then_inc(p_act, 1)
                if not first:
                    act.wait_ge(z_ready, it)
                for g in range(2):
                    act.wait_ge(p_full, P.full(it, f"g{g}"))
                    act.activation(G[:, 512 * g:512 * (g + 1)], psP[:, P.bank(f"g{g}"), :], ACT.Tanh, scale=0.5).then_inc(gate_tanh, 1)

                act.wait_ge(p_act, P.read(it, "r1"))
                for p in range(PAIRS):
                    if not first:
                        act.wait_ge(w_full, W.full(it - 1, "l32_1" if p == 0 else "l16"))
                    for h in range(HPG):
                        e = copy(RB[p][rows(h), :, h, 1:128:2],
                                 RM[rows(h), :].rearrange("p (c t) -> p c t", c=KC)[:, :, 128 * p + 1:128 * (p + 1):2])
                    e.then_inc(rb_act, 1)
                for i, n in enumerate(LEVELS + (BLK,)):
                    act.wait_ge(r_scaled, NPL * it + i + 1)
                    act.wait_ge(w_full, W.full(it, W_SEQ[i][0]))
                    for h in range(HPG):
                        src = halves(RM[rows(h), :], n)[1].rearrange("p (c q) n -> p c q n", c=KC)
                        dst = RB[i % 2][rows(h), :, h, :].rearrange("p c (q n) -> p c q n", n=n)
                        e = copy(dst, src)
                    e.then_inc(rb_act, 1)
                    if ffn and i < 4:
                        ffn.up(0, i)
                for p in range(PAIRS):
                    if not first or p:
                        act.wait_ge(y_full, 2 * it + p)
                    if p == 0:
                        act.wait_ge(w_dve, W.read(it, "l16"))
                    for q in range(4):
                        r = slice(BLK * q, BLK * (q + 1))
                        e = copy(AB[r, :, BLK * q:BLK * (q + 1)],
                                 A[r, 512 * p:512 * (p + 1)].rearrange("p (h t) -> p h t", h=HEADS))
                    e.then_inc(ab_diag, 1)
                    act.wait_ge(w_full, W.full(it, f"l32_{p}"))
                    for h in range(2):
                        r = slice(64 * h, 64 * h + BLK)
                        e = copy(AB[r, :, 64 * h + BLK:64 * h + 2 * BLK],
                                 psW[r, W.bank(f"l32_{p}"), :].rearrange("p (h t) -> p h t", h=HEADS))
                    e.then_inc(w_act, 1)
                    if p == 0:
                        for q in range(PAIRS):
                            act.wait_ge(x_full, X.full(it, f"kt{q}"))
                            copy(KT[:, q, :], psX[:, :]).then_inc(x_act, 1)
                    act.wait_ge(y_copied, 2 * it + p + 1)
                    act.activation(YSQ.rearrange("p (c t) -> p c t", c=KC)[:, :, 128 * p:128 * (p + 1)],
                                   YSB.rearrange("p (c t) -> p c t", c=KC)[:, :, 128 * p:128 * (p + 1)], ACT.Square).then_inc(y_squared, 1)
                    if ffn:
                        ffn.up(1, p)
                if ffn:
                    ffn.up(1, 2)
                    ffn.up(1, 3)
                act.wait_ge(p_full, P.full(it, "var"))
                act.activation(RS[:, :], psP[0:HEADS, P.bank("var"), 0:COLS], ACT.Sqrt, bias=EPS[0:HEADS, 0:1]).then_inc(p_act, 1)
                if ffn:
                    ffn.roots()
                act.wait_ge(mv_ready, it + 1)
                act.activation(RSTD[:, :], MV[:, :, 1], ACT.Sqrt, bias=EPS[:, 1:2]).then_inc(sd_ready, 1)
                for p in range(PAIRS):
                    act.wait_ge(p_full, P.full(it, f"xt{p}"))
                    copy(XHI[:, p, :, :], psP[:, P.bank(f"xt{p}"), :].rearrange("p (c t) -> p c t", c=KC)).then_inc(xhi_ready, 1)

            def feed_forward(j, first):
                def up(p, g):
                    u = 4 * p + g
                    act.wait_ge(f_full, F.full(j, f"fc{g}_{p}"))
                    if u >= 2 or not first:
                        act.wait_ge(gw_ready, 8 * j + u - 1)
                        act.wait_ge(sums_added, 8 * j + u - 1)
                    act.activation(GF[:, u % 2, :], psF[:, F.bank(f"fc{g}_{p}"), :], ACT.Gelu).then_inc(f_act, 1)
                    act.wait_ge(f_act, 8 * j + u + 1)
                    act.activation(GSQ[:, u % 2, :], GF[:, u % 2, :], ACT.Square).then_inc(g_squared, 1)

                def roots():
                    act.wait_ge(st_step, 6 * j + 6)
                    act.activation(FSD[:, :], FV[:, :], ACT.Sqrt, bias=EPS[:, 1:2]).then_inc(fsd_ready, 1)
                    act.wait_ge(o_step, 6 * j + 6)
                    act.activation(OSD[:, :], FMV[:, :, 1], ACT.Sqrt, bias=EPS[:, 1:2]).then_inc(osd_ready, 1)

                def alone():
                    for p in range(PAIRS):
                        for g in range(4):
                            up(p, g)
                    roots()
                return FeedForward(up=up, roots=roots, alone=alone)

            over_tiles(act, tile, feed_forward)

        @block.gpsimd
        def _(pool):
            pool.wait_ge(quantised, 8)
            pool.memset(ARENA1[:, 0:6144], 0.0).then_inc(su_pool, 1)
            pool.memset(ARENA2[:, 0:2048], 0.0).then_inc(su_pool, 1)
            pool.wait_ge(su_dve, 8)
            pool.wait_ge(su_pool, 2)

            def tile(it, first, ffn):
                pool.wait_ge(xt_in, 16 * (it + 1))
                for f, name in enumerate(("mw1", "mk1", "mv1", "mr1", "mg1")):
                    pool.wait_ge(p_dve, P.read(it, name))
                    v = XF[f % 2].rearrange("p (q t) -> p q t", t=CH)
                    pool.tensor_tensor(v, v, xcur, ALU.add).then_inc(xf_ready, 1)
                    if f == 3:
                        pool.wait_ge(p_act, P.read(it, "k1"))
                        pool.tensor_tensor(halves(K1, 1)[1].rearrange("p (c q) n -> p c (q n)", c=KC),
                                           halves(KM, 1)[1].rearrange("p (c q) n -> p c (q n)", c=KC),
                                           PAR[:, :, U:U + 1].broadcast_to([128, KC, COLS // 2]), ALU.mult).then_inc(k1_odd, 1)
                if ffn:
                    for u in range(6):
                        ffn.up(u // 4, u % 4)
                pool.wait_ge(tot_ready, NPL * it + 6)
                for b in range(B):
                    pool.wait_ge(y_full, 2 * it + b // 2 + 1)
                    tot = TOT[64].rearrange("p (c b) -> p b c", b=B)[:, b, :]
                    pool.tensor_tensor(S[:, b, :, :], S[:, b, :, :], grow(tot, 128), ALU.mult).then_inc(s_decayed, 1)
                    pool.wait_ge(s_decayed, B * it + b + 1)
                    pool.wait_ge(x_dve, X.read(it, f"kv{b}"))
                    pool.tensor_tensor(S[:, b, :, :], S[:, b, :, :], KVM[:, b % 2, :].rearrange("p (c n) -> p c n", c=KC),
                                       ALU.add).then_inc(s_ready, 1)
                if ffn:
                    ffn.up(1, 2)
                    ffn.up(1, 3)
                pool.wait_ge(y_affine, KC * (it + 1))
                pool.wait_ge(p_dve, P.read(it, "g1"))
                pool.tensor_tensor(YSB, YSB, G, ALU.mult).then_inc(z_ready, 1)
                for p in range(PAIRS):
                    pool.wait_ge(p_full, P.full(it, f"xt{p}"))
                    pool.tensor_tensor(X1[:, p, :], X1[:, p, :], BSUM[:, :], ALU.add).then_inc(x1_biased, 1)

            def feed_forward(j, first):
                def up(p, g):
                    u = 4 * p + g
                    for acc, src, ready, n in ((GA, GF, f_act, 1), (QA, GSQ, g_squared, 2)):
                        pool.wait_ge(ready, 8 * j + u + 1)
                        if g == 0:
                            if p or not first:
                                pool.wait_ge(sums_folded, 2 * j + p)
                            e = pool.tensor_tensor(acc[:, :], src[:, u % 2, :], ZERO.broadcast_to([128, 512]), ALU.add)
                        else:
                            if n == 1:
                                pool.wait_ge(sums_added, 8 * j + u)
                            e = pool.tensor_tensor(acc[:, :], acc[:, :], src[:, u % 2, :], ALU.add)
                    e.then_inc(sums_added, 1)

                def alone():
                    for p in range(PAIRS):
                        for g in range(4):
                            up(p, g)
                return FeedForward(up=up, alone=alone)

            over_tiles(pool, tile, feed_forward)

        @block.vector
        def _(dve):
            def after_wait(i):
                dve.memset(PAUSE[:, i:i + 1], 0.0)

            dve.wait_ge(const_in, 16 * 4)
            for i, (arena, here) in enumerate(((ARENA1, wfc_in), (ARENA2, wpj_in))):
                dve.wait_ge(here, 64)
                dve.tensor_reduce(RED[:, 128 * i:128 * (i + 1)], arena[:, :].rearrange("p (q n) -> p q n", n=64), AX.X, ALU.add,
                                  apply_absolute_value=True).then_inc(setup_step, 1)
                dve.wait_ge(setup_step, i + 1)
                dve.tensor_reduce(SC[:, 8 + i:9 + i], RED[:, 128 * i:128 * (i + 1)], AX.X, ALU.add).then_inc(su_dve, 1)
            dve.tensor_reduce(SC[:, 10:12], FWB[:, :, :], AX.X, ALU.max, apply_absolute_value=True).then_inc(su_dve, 1)
            dve.wait_ge(su_pe, 3)
            dve.tensor_reduce(SC[0:2, 12:13], psX[0:2, 0:128], AX.X, ALU.max).then_inc(setup_step, 1)
            dve.wait_ge(setup_step, 3)
            dve.tensor_scalar(SC[0:2, 14:16], IDENT[0:2, 0:2], SC[0:2, 12:13], None, ALU.mult).then_inc(su_dve, 1)
            dve.wait_ge(su_pe, 4)
            dve.tensor_scalar(AMAX, psY[:, 0:2], 1e-30, None, ALU.max).then_inc(setup_step, 1)
            dve.wait_ge(setup_step, 4)
            dve.reciprocal(SC[:, 2:4], AMAX).then_inc(setup_step, 1)
            dve.wait_ge(setup_step, 5)
            dve.tensor_scalar(FWB[:, 0, :], FWB[:, 0, :], SC[:, 2:3], None, ALU.mult)
            dve.tensor_scalar(FWB[:, 1, :], FWB[:, 1, :], SC[:, 3:4], None, ALU.mult).then_inc(setup_step, 1)
            for i in range(2):
                dve.wait_ge(su_pe, i + 1)
                dve.tensor_scalar(SC[:, 16 + i:17 + i], psP[:, i, 0:1], 1.0 / (C * HID), GAMMA_EPS, ALU.mult, ALU.add).then_inc(setup_step, 1)
            dve.wait_ge(setup_step, 8)
            dve.tensor_scalar(SC[:, 18:20], SC[:, 16:18], 0.5, None, ALU.mult)
            dve.tensor_scalar(SC[:, 20:22], SC[:, 16:18], -0.5, None, ALU.mult).then_inc(setup_step, 1)
            dve.wait_ge(setup_step, 9)
            neg = HHI[:, :, :].rearrange("p m t -> p (m t)")
            n = 9
            for i, (arena, dst) in enumerate(((ARENA1, WFC), (ARENA2, WPJ))):
                flat = dst[:, :, :].rearrange("p a n -> p (a n)")
                for k in range(4):
                    src = arena[:, 2048 * k:2048 * (k + 1)]
                    dve.tensor_scalar(neg, src, SC[:, 20 + i:21 + i], None, ALU.is_lt).then_inc(setup_step, 1)
                    n += 1
                    dve.wait_ge(setup_step, n)
                    dve.scalar_tensor_tensor(out=flat[:, 2048 * k:2048 * (k + 1)], in0=src, scalar=SC[:, 18 + i:19 + i],
                                             in1=neg, op0=ALU.is_gt, op1=ALU.subtract).then_inc(quantised, 1)
                    dve.wait_ge(quantised, 4 * i + k + 1)
            for v in range(2):
                src = grow(FWB[:, v, :], 128)
                if v:
                    dve.wait_ge(su_pe, 5)
                dve.tensor_copy(HHI[:, :, :], src).then_inc(setup_step, 1)
                n += 1
                dve.wait_ge(setup_step, n)
                dve.tensor_tensor(HLO[:, :, :], src, HHI[:, :, :], ALU.subtract).then_inc(su_dve, 1)
            dve.wait_ge(su_pe, 6)
            dve.tensor_copy(WSUM[:, :], psW[:, 0, :])
            dve.tensor_scalar(BSUM[:, :], psW[:, 1, :], AMAX[:, 1:2], None, ALU.mult).then_inc(su_dve, 1)
            dve.wait_ge(weights_in, 16 * NWEIGHTS)
            wv = WALL[:, W_V, :, :].rearrange("p k (h j) -> p (k h) j", j=HD)
            dve.tensor_reduce(VMEAN, wv, AX.X, ALU.add).then_inc(setup_step, 1)
            n += 1
            dve.wait_ge(setup_step, n)
            dve.tensor_scalar(VMEAN, VMEAN, 1.0 / HD, None, ALU.mult).then_inc(setup_step, 1)
            n += 1
            dve.wait_ge(setup_step, n)
            dve.tensor_tensor(wv, wv, grow(VMEAN, HD), ALU.subtract)
            dve.tensor_scalar(PAR[:, :, LN_G:LN_B + 1], PAR[:, :, LN_G:LN_B + 1], 0.5, None, ALU.mult).then_inc(su_dve, 1)
            dve.wait_ge(su_dve, 8)
            dve.wait_ge(su_pool, 2)

            def tile(it, first, ffn):
                dve.wait_ge(xt_in, 16 * (it + 1))
                dve.tensor_tensor(XX[:, :, :], xprev, xcur, ALU.subtract).then_inc(xx_ready, 1)
                dve.wait_ge(xx_ready, it + 1)
                if not first:
                    dve.wait_ge(p_full, P.full(it - 1, "wo1"))
                for k in range(KC):
                    q = slice(B * k, B * (k + 1))
                    e = dve.scalar_tensor_tensor(out=cc(XF[1], k).rearrange("p (q t) -> p q t", t=CH), in0=XX[:, q, :],
                                                 scalar=PAR[:, k, MAA_X:MAA_X + 1], in1=xcur[:, q, :], op0=ALU.mult, op1=ALU.add)
                e.then_inc(xm_ready, 1)

                def mix(f, name, before):
                    if before:
                        dve.wait_ge(p_full, P.full(it, before))
                    for g in range(2):
                        dve.wait_ge(p_full, P.full(it, f"{name}{g}"))
                        for c in range(2):
                            k = 2 * g + c
                            e = dve.scalar_tensor_tensor(
                                out=cc(XF[f % 2], k), in0=psP[:, P.bank(f"{name}{g}"), COLS * c:COLS * (c + 1)],
                                scalar=PAR[:, k, MIX_PAR[f]:MIX_PAR[f] + 1],
                                in1=XX[:, B * k:B * (k + 1), :].rearrange("p q t -> p (q t)"), op0=ALU.add, op1=ALU.mult)
                        e.then_inc(p_dve, 1)

                mix(0, "mw", None)
                mix(1, "mk", "w1b")
                mix(2, "mv", "td1")
                mix(3, "mr", "k1")
                mix(4, "mg", "v1")
                for g in range(2):
                    dve.wait_ge(gate_tanh, 2 * it + g + 1)
                    dve.scalar_tensor_tensor(out=G[:, 512 * g:512 * (g + 1)], in0=G[:, 512 * g:512 * (g + 1)], scalar=1.0,
                                             in1=psP[:, P.bank(f"g{g}"), :], op0=ALU.add, op1=ALU.mult).then_inc(p_dve, 1)

                def scale(i, n):
                    tl, tr = TOT[n].rearrange("p (q two) -> p two q", two=2)[:, 0, :], TOT[n].rearrange("p (q two) -> p two q", two=2)[:, 1, :]
                    right = halves(RM, n)[1]
                    dve.wait_ge(rb_act, 7 * it + i + 2)
                    dve.tensor_tensor(right, right, grow(tl, n), ALU.mult).then_inc(r_scaled, 1)
                    if i == 0:
                        dve.wait_ge(k1_odd, it + 1)
                    else:
                        dve.wait_ge(w_full, W.full(it, f"l{n}" if n < 32 else "l32_1"))
                    left = halves(KM, n)[0]
                    dve.tensor_tensor(left, left, grow(tr, n), ALU.mult).then_inc(k_scaled, 1)
                    dve.tensor_tensor(TOT[2 * n], tl, tr, ALU.mult).then_inc(tot_ready, 1)
                    dve.wait_ge(tot_ready, NPL * it + i + 1)
                    dve.wait_ge(r_scaled, NPL * it + i + 1)
                    dve.wait_ge(k_scaled, NPL * it + i + 1)

                dve.wait_ge(p_act, P.read(it, "r1"))
                for p in range(PAIRS):
                    if not first:
                        dve.wait_ge(w_full, W.full(it - 1, "l32_1" if p == 0 else "l16"))
                    for h in range(HPG):
                        e = dve.tensor_tensor(RB[p][rows(h), :, h, 0:128:2],
                                               RM[rows(h), :].rearrange("p (c t) -> p c t", c=KC)[:, :, 128 * p:128 * (p + 1):2],
                                               PAR[rows(h), :, U:U + 1].broadcast_to([HD, KC, 64]), ALU.mult)
                    e.then_inc(rb_dve, 1)
                dve.wait_ge(d_ready, it + 1)
                scale(0, 1)
                if not first:
                    dve.wait_ge(ab_diag, 2 * it)
                for p in range(PAIRS):
                    dve.wait_ge(w_full, W.full(it, f"l1_{p}"))
                    dve.tensor_tensor(A[:, 512 * p:512 * (p + 1)].rearrange("p (h t) -> p h t", t=BLK),
                                      psW[:, W.bank(f"l1_{p}"), :].rearrange("p (h t) -> p h t", t=BLK),
                                      MASK1.unsqueeze(1).broadcast_to([128, HEADS, BLK]), ALU.mult).then_inc(w_dve, 1)
                dve.wait_ge(w_dve, W.read(it, "l1_1"))
                for i, n in enumerate(LEVELS):
                    scale(i + 1, n)
                    av = A.rearrange("p (h q two n) -> p h q two n", two=2, n=n, h=2 * HEADS)[:, :, :, 1, :]
                    nq = 16 // n
                    data = psW[:, W.bank(f"l{n}"), :].rearrange("p (h q n) -> p h q n", h=2 * HEADS, n=n)
                    mask = CM[:, 16 * i:16 * (i + 1)].rearrange("p (q n) -> p q n", n=n).unsqueeze(1).broadcast_to([128, 2 * HEADS, nq, n])
                    after_wait(i)
                    dve.copy_predicated(av, mask, data).then_inc(w_dve, 1)
                    dve.wait_ge(w_dve, W.read(it, f"l{n}"))
                    if ffn:
                        ffn.up(0, i)
                scale(5, 32)
                if ffn:
                    ffn.stats(0)
                    ffn.centre(0)
                for p in range(PAIRS):
                    dve.wait_ge(y_full, 2 * it + p + 1)
                    dve.tensor_copy(YSB.rearrange("p (c t) -> p c t", c=KC)[:, :, 128 * p:128 * (p + 1)],
                                    psY[:, :].rearrange("p (c t) -> p c t", c=KC)).then_inc(y_copied, 1)
                    if ffn:
                        ffn.up(1, p)
                for b in range(B):
                    dve.wait_ge(x_full, X.full(it, f"kv{b}"))
                    if b >= 2 or not first:
                        dve.wait_ge(s_ready, B * it + b - 1)
                    dve.tensor_tensor(KVM[:, b % 2, :].rearrange("p (c n) -> p c n", c=KC), psX[:, :].rearrange("p (c n) -> p c n", c=KC),
                                      BLKMASK.unsqueeze(1).broadcast_to([128, KC, 128]), ALU.mult).then_inc(x_dve, 1)
                if ffn:
                    ffn.up(1, 2)
                    ffn.up(1, 3)
                dve.wait_ge(p_act, P.read(it, "var"))
                dve.reciprocal(RS[:, :], RS[:, :]).then_inc(rs_inv, 1)
                if ffn:
                    ffn.stats(1)
                dve.wait_ge(y_copied, 2 * it + 2)
                for g in range(2):
                    dve.wait_ge(p_full, P.full(it, f"rb{g}"))
                    v = YSB[:, 512 * g:512 * (g + 1)]
                    dve.tensor_tensor(v, v, psP[:, P.bank(f"rb{g}"), :], ALU.mult).then_inc(p_dve, 1)
                for k in range(KC):
                    dve.wait_ge(p_dve, P.read(it, f"rb{k // 2}"))
                    dve.tensor_scalar(cc(YSB, k), cc(YSB, k), PAR[:, k, LN_G:LN_G + 1], PAR[:, k, LN_B:LN_B + 1],
                                      ALU.mult, ALU.add).then_inc(y_affine, 1)
                if ffn:
                    ffn.centre(1)
                    ffn.finish()
                dve.wait_ge(xtok_in, 16 * (it + 1))
                for p in range(PAIRS):
                    dve.wait_ge(p_full, P.full(it, f"wo{p}"))
                    dve.tensor_tensor(X1[:, p, :], psP[:, P.bank(f"wo{p}"), :], XTOK[:, p, :], ALU.add).then_inc(p_dve, 1)
                    dve.wait_ge(p_dve, P.read(it, f"wo{p}"))
                    dve.bn_stats(BNS[:, p, :], X1[:, p, :]).then_inc(bn_done, 1)
                dve.wait_ge(bn_done, 2 * it + 2)
                after_wait(4)
                dve.bn_aggr(MV[:, 0, :], BNS[:, 0, :])
                dve.bn_aggr(MV[:, 1, :], BNS[:, 1, :]).then_inc(mv_ready, 1)
                dve.wait_ge(mv_ready, it + 1)
                dve.wait_ge(sd_ready, it + 1)
                dve.reciprocal(RSTD[:, :], RSTD[:, :]).then_inc(rstd_ready, 1)
                dve.wait_ge(rstd_ready, it + 1)
                for p in range(PAIRS):
                    dve.tensor_scalar(X1[:, p, :], X1[:, p, :], MV[:, p, 0:1], RSTD[:, p:p + 1], ALU.subtract, ALU.mult).then_inc(x1_ready, 1)
                for p in range(PAIRS):
                    dve.wait_ge(xhi_ready, 2 * it + p + 1)
                    dve.tensor_tensor(XLO[:, p, :, :], psP[:, P.bank(f"xt{p}"), :].rearrange("p (c t) -> p c t", c=KC),
                                      XHI[:, p, :, :], ALU.subtract).then_inc(p_dve, 1)

            def feed_forward(j, first):
                def up(p, g):
                    u = 4 * p + g
                    dve.wait_ge(f_act, 8 * j + u + 1)
                    if g == 0 and (p or not first):
                        dve.wait_ge(f_full, F.full(j if p else j - 1, f"pj_{1 - p}"))
                    if u or not first:
                        dve.wait_ge(hlo_ready, 8 * j + u)
                    dve.tensor_tensor(GW[:, :].rearrange("p (m t) -> p m t", m=4), GF[:, u % 2, :].rearrange("p (m t) -> p m t", m=4),
                                      grow(FWB[:, 0, 4 * g:4 * (g + 1)], 128), ALU.mult).then_inc(gw_ready, 1)
                    dve.wait_ge(gw_ready, 8 * j + u + 1)
                    gw = GW[:, :].rearrange("p (m t) -> p m t", m=4)
                    dve.tensor_copy(HHI[:, 4 * g:4 * (g + 1), :], gw).then_inc(hhi_ready, 1)
                    dve.wait_ge(hhi_ready, 8 * j + u + 1)
                    dve.tensor_tensor(HLO[:, 4 * g:4 * (g + 1), :], gw, HHI[:, 4 * g:4 * (g + 1), :], ALU.subtract).then_inc(hlo_ready, 1)

                def stats(p):
                    dve.wait_ge(sums_added, 8 * j + 4 * p + 4)
                    dve.tensor_reduce(GR[:, 0, :], GA[:, :].rearrange("p (m t) -> p t m", m=4), AX.X, ALU.add)
                    dve.tensor_reduce(GR[:, 1, :], QA[:, :].rearrange("p (m t) -> p t m", m=4), AX.X, ALU.add).then_inc(sums_folded, 1)

                def centre(p):
                    st = ST[:, p, :]
                    s = 6 * j + 3 * p
                    dve.wait_ge(f_full, F.full(j, f"st_{p}"))
                    dve.tensor_scalar(st[:, 0:2], psF[:, F.bank(f"st_{p}"), 0:2], 1.0 / HID, None, ALU.mult).then_inc(f_dve, 1)
                    dve.wait_ge(f_dve, F.read(j, f"st_{p}"))
                    dve.tensor_scalar(st[:, 2:3], st[:, 0:1], -1.0, None, ALU.mult).then_inc(st_step, 1)
                    dve.wait_ge(st_step, s + 1)
                    dve.scalar_tensor_tensor(out=st[:, 3:4], in0=st[:, 0:1], scalar=st[:, 2:3], in1=st[:, 1:2],
                                             op0=ALU.mult, op1=ALU.add).then_inc(st_step, 1)
                    dve.wait_ge(st_step, s + 2)
                    dve.tensor_scalar(FV[:, p:p + 1], st[:, 3:4], 0.0, None, ALU.max).then_inc(st_step, 1)
                    if not first:
                        dve.wait_ge(out_stored, 16 * PAIRS * j)
                    dve.wait_ge(f_full, F.full(j, f"pj_{p}"))
                    dve.scalar_tensor_tensor(out=OUT[:, p, :], in0=WSUM[:, :], scalar=st[:, 2:3], in1=psF[:, F.bank(f"pj_{p}"), :],
                                             op0=ALU.mult, op1=ALU.add).then_inc(f_dve, 1)

                def finish():
                    dve.wait_ge(fsd_ready, j + 1)
                    dve.reciprocal(FSD[:, :], FSD[:, :]).then_inc(fsc_step, 1)
                    dve.wait_ge(fsc_step, 2 * j + 1)
                    dve.tensor_scalar(FSC[:, :], FSD[:, :], AMAX[:, 0:1], None, ALU.mult).then_inc(fsc_step, 1)
                    dve.wait_ge(fsc_step, 2 * j + 2)
                    dve.wait_ge(f_dve, F.read(j, "pj_1"))
                    for p in range(PAIRS):
                        dve.wait_ge(x1_biased, 2 * j + p + 1)
                        dve.scalar_tensor_tensor(out=OUT[:, p, :], in0=OUT[:, p, :], scalar=FSC[:, p:p + 1], in1=X1[:, p, :],
                                                 op0=ALU.mult, op1=ALU.add).then_inc(o_step, 1)
                    for p in range(PAIRS):
                        dve.wait_ge(o_step, 6 * j + p + 1)
                        dve.bn_stats(FBN[:, p, :], OUT[:, p, :]).then_inc(o_step, 1)
                    for p in range(PAIRS):
                        dve.wait_ge(o_step, 6 * j + p + 3)
                        after_wait(5 + p)
                        dve.bn_aggr(FMV[:, p, :], FBN[:, p, :]).then_inc(o_step, 1)
                    dve.wait_ge(osd_ready, j + 1)
                    dve.reciprocal(OSD[:, :], OSD[:, :]).then_inc(osd_inv, 1)
                    dve.wait_ge(osd_inv, j + 1)
                    for p in range(PAIRS):
                        dve.tensor_scalar(OUT[:, p, :], OUT[:, p, :], FMV[:, p, 0:1], OSD[:, p:p + 1],
                                          ALU.subtract, ALU.mult).then_inc(out_ready, 1)

                def alone():
                    for p in range(PAIRS):
                        for g in range(4):
                            up(p, g)
                        stats(p)
                        centre(p)
                    finish()
                return FeedForward(up=up, stats=stats, centre=centre, finish=finish, alone=alone)

            over_tiles(dve, tile, feed_forward)


def _constants():
    p = np.arange(128)
    ident = np.eye(128)
    blk = (p[:, None] // HD == p[None, :] // HD) * 1.0
    ones = np.ones((128, 128))
    sel = np.zeros((128, KC, HEADS))
    spread = np.zeros((128, KC, 128))
    for c in range(KC):
        sel[p, c, HPG * c + p // HD] = 1.0 / HD
        spread[HPG * c + p // HD, c, p] = 1.0
    s, t = p[:, None] % BLK, np.arange(BLK)[None, :]
    mask1 = ((s == t) | ((s % 2 == 0) & (t == s + 1))) * 1.0
    eps = np.tile(np.array([[GN_EPS, LN_EPS, 0.0]]), (128, 1))
    f = np.concatenate([ident, blk, ones, sel.reshape(128, -1), spread.reshape(128, -1), mask1, eps], 1).astype(np.float32)
    masks = []
    for n in LEVELS:
        r = np.arange(16)[None, :]
        masks.append((s // (2 * n) == r // n) & (s % (2 * n) < n))
    return f, np.concatenate(masks, 1).astype(np.uint32)


def kernel(**inputs):
    import concourse.bacc as _bacc
    from concourse.bass_utils import run_bass_kernel_spmd as _run

    g = {k.replace("L0_attn_", "a_").replace("L0_ffn_", "f_"): np.asarray(v) for k, v in inputs.items()}

    def by_part(w):
        return w.reshape(-1, 128, w.shape[-1]).transpose(1, 0, 2)

    x = g["a_x"]
    padded = np.pad(x, ((0, 0), (1, 0), (0, 0)))
    cuts = np.stack([padded[:, i * CH:i * CH + CH + 1] for i in range(TILES)])
    x_ch = cuts.reshape(TILES, B, CH + 1, KC, 128).transpose(0, 4, 3, 1, 2).reshape(TILES, 128, KC * B, CH + 1)
    x_tok = x.reshape(PAIRS, 2, TILES, CH, C).transpose(2, 1, 3, 0, 4).reshape(TILES, 128, PAIRS, C)
    w_all = np.stack([by_part(g[n].T) for n in ("a_Wr", "a_Wk", "a_Wv", "a_Wg", "a_Wo")], 1)
    par = np.stack([g[n].reshape(KC, 128).T for n in
                    ("a_time_maa_x", "a_time_maa_w", "a_time_maa_k", "a_time_maa_v", "a_time_maa_r", "a_time_maa_g",
                     "a_time_decay", "a_u", "a_ln_g", "a_ln_b")], 2)
    c_f32, c_mask = _constants()
    arrays = {
        "x_ch": x_ch, "x_tok": x_tok, "w_all": w_all,
        "w1": by_part(g["a_maa_w1"]), "w2a": g["a_maa_w2"][0:4].reshape(128, C), "w2b": g["a_maa_w2"][4],
        "td1": by_part(g["a_td_w1"]), "td2": g["a_td_w2"], "par": par,
        "wfc": by_part(g["f_W_fc"].T).reshape(128, -1), "wpj": by_part(g["f_W_proj"].T).reshape(128, -1),
        "ffn_wb": np.stack([g["f_ln_w"].reshape(MH, 128).T, g["f_ln_b"].reshape(MH, 128).T], 1),
        "c_f32": c_f32, "c_mask": c_mask,
    }
    arrays = {k: np.ascontiguousarray(v) for k, v in arrays.items()}
    nc = _bacc.Bacc("TRN2", target_bir_lowering=False, num_devices=1)
    args = [nc.dram_tensor(k, a.shape, mybir.dt.from_np(a.dtype), kind="ExternalInput").ap() for k, a in arrays.items()]
    args.append(nc.dram_tensor("out", (TILES, 128, PAIRS, C), F32, kind="ExternalOutput").ap())
    rwkv_ffn_kernel(nc, *args)
    r = _run(nc, [arrays], core_ids=[0])
    out = r.results[0]["out"]
    return np.ascontiguousarray(out.reshape(TILES, 2, CH, PAIRS, C).transpose(3, 1, 0, 2, 4).reshape(B, T, C))
```

```python
from contextlib import ExitStack

import numpy as np

import concourse.bass as bass
from concourse import mybir

F32 = mybir.dt.float32
F16 = mybir.dt.float16
U32 = mybir.dt.uint32
ALU = mybir.AluOpType
ACT = mybir.ActivationFunctionType
AX = mybir.AxisListType

B, T, C = 4, 2048, 512
HEADS, HD = 16, 32
HID = 2048
MIXR, DECR = 32, 64
CH = 64
COLS = B * CH
KC = C // 128
HPG = 128 // HD
MH = HID // 128
TILES = T // CH
PAIRS = B // 2
BLK = 32
GN_EPS = 1e-5 * 8 ** 2
LN_EPS = 1e-5
GAMMA_EPS = 1e-6
LEVELS = (2, 4, 8, 16)

MAA_X, MAA_W, MAA_K, MAA_V, MAA_R, MAA_G, DECAY, U, LN_G, LN_B = range(10)
NPAR = 10
MIX_PAR = (MAA_W, MAA_K, MAA_V, MAA_R, MAA_G)
W_R, W_K, W_V, W_G, W_O = range(5)

P_SEQ = [("mw0", "dve"), ("mw1", "dve"), ("mk0", "dve"), ("mk1", "dve"),
         ("td1", "act"), ("mv0", "dve"), ("mv1", "dve"), ("td20", "act"), ("td21", "act"), ("k0", "act"),
         ("k1", "act"), ("mr0", "dve"), ("mr1", "dve"), ("v0", "act"), ("v1", "act"), ("mg0", "dve"),
         ("mg1", "dve"), ("r0", "act"), ("r1", "act"), ("g0", "dve"), ("g1", "dve"), ("var", "act"),
         ("rb0", "dve"), ("rb1", "dve"), ("w1a", "tanh"), ("w1b", "tanh"), ("wo0", "dve"), ("wo1", "dve"), ("xt0", "dve"), ("xt1", "dve")]
W_SEQ = [("l1_0", "dve"), ("l1_1", "dve"), ("l2", "dve"), ("l4", "dve"), ("l8", "dve"), ("l16", "dve"),
         ("l32_0", "act"), ("l32_1", "act")]
X_SEQ = [("kt0", "act"), ("kt1", "act"), ("kv0", "dve"), ("kv1", "dve"), ("kv2", "dve"), ("kv3", "dve")]
F_SEQ = [(f"{n}_{p}", e) for p in range(PAIRS)
         for n, e in (("fc0", "act"), ("fc1", "act"), ("fc2", "act"), ("fc3", "act"), ("pj", "product"), ("st", "stats"))]
RB_SEQ = {"l1_0": 0, "l1_1": 1, "l2": 0, "l4": 1, "l8": 0, "l16": 1, "l32": 0}


class Ring:

    def __init__(self, seq, depth, filled, emptied, before={}):
        self.names = [n for n, _ in seq]
        self.by = [e for _, e in seq]
        self.n, self.depth, self.filled, self.emptied = len(seq), depth, filled, emptied
        self.before = before
        assert self.n % depth == 0

    def bank(self, name):
        return self.names.index(name) % self.depth

    def full(self, it, name):
        return it * self.n + self.names.index(name) + 1

    def read(self, it, name):
        i = self.names.index(name)
        return it * self.by.count(self.by[i]) + self.by[:i + 1].count(self.by[i]) + self.before.get(self.by[i], 0)

    def wait_free(self, eng, it, name, first):
        i = self.names.index(name) - self.depth
        if i < 0 and first:
            return
        before = self.names[i % self.n]
        eng.wait_ge(self.emptied[self.by[i % self.n]], self.read(it if i >= 0 else it - 1, before))


class FeedForward:

    def __init__(self, alone, up=None, stats=None, down=None, finish=None):
        self.alone, self.up, self.stats, self.down, self.finish = alone, up, stats, down, finish


def rwkv_ffn_kernel(nc, x_ch, x_tok, w_all, w1, w2a, w2b, td1, td2, par, wfc, wpj, ffn_wb, c_f32, c_mask, out,
                    tiles=TILES):
    with ExitStack() as ctx:
        def sb(name, shape, dt=F32):
            return ctx.enter_context(nc.sbuf_tensor(name, shape, dt))

        def sem(name):
            return ctx.enter_context(nc.semaphore(name))

        WALL = sb("WALL", [128, 5, KC, C])
        W1 = sb("W1", [128, KC, 5 * MIXR])
        W2A = sb("W2A", [128, C])
        TD1 = sb("TD1", [128, KC, DECR])
        TD2W2 = sb("TD2W2", [DECR + MIXR, C])
        TD2, W2B = TD2W2[0:DECR, :], TD2W2[DECR:DECR + MIXR, :]
        PAR = sb("PAR", [128, KC, NPAR])
        WFC = sb("WFC", [128, KC, HID], F16)
        WPJ = sb("WPJ", [128, MH, C], F16)
        FWB = sb("FWB", [128, 2, MH])
        WSUM = sb("WSUM", [128, C])
        BSUM = sb("BSUM", [128, C])
        CF = sb("CF", [128, c_f32.shape[1]])
        CM = sb("CM", [128, c_mask.shape[1]], U32)
        o = 0
        IDENT = CF[:, o:o + 128]; o += 128
        BLKMASK = CF[:, o:o + 128]; o += 128
        ONES = CF[:, o:o + 128]; o += 128
        SEL = CF[:, o:o + KC * HEADS].rearrange("p (c h) -> p c h", c=KC); o += KC * HEADS
        SPREAD = CF[:, o:o + KC * 128].rearrange("p (c n) -> p c n", c=KC); o += KC * 128
        MASK1 = CF[:, o:o + BLK]; o += BLK
        EPS = CF[:, o:o + 2]; o += 2
        ZERO = CF[:, o:o + 1]; o += 1
        MINUS_HALF = CF[:, o:o + 1]; o += 1

        ARENA1 = sb("ARENA1", [128, 8192])
        ARENA2 = sb("ARENA2", [128, 8192])
        RB = [ARENA1[:, 2048 * i:2048 * (i + 1)].rearrange("p (c h t) -> p c h t", c=KC, h=HPG) for i in range(2)]
        AB = ARENA1[:, 4096:6144].rearrange("p (h t) -> p h t", h=HEADS)
        A = ARENA1[:, 6144:7168]
        K1 = ARENA1[:, 7168:8192]
        KT = ARENA1[:, 7168:8192].rearrange("p (q n) -> p q n", q=PAIRS)
        S = ARENA2[:, 0:2048].rearrange("p (b c n) -> p b c n", b=B, c=KC)
        XF = [ARENA2[:, 2048 + 1024 * i:3072 + 1024 * i] for i in range(2)]
        YSB, YSQ = XF
        KM = ARENA2[:, 4096:5120]
        RM = ARENA2[:, 5120:6144]
        XTOK = KM.rearrange("p (h c) -> p h c", h=PAIRS)
        D = ARENA2[:, 6144:7168]
        G = ARENA2[:, 7168:8192]

        XT = sb("XT", [128, KC * B, CH + 1])
        XX = sb("XX", [128, KC * B, CH])
        TMA = sb("TMA", [128, COLS])
        TZTM = sb("TZTM", [DECR + MIXR, COLS])
        TZ, TMB = TZTM[0:DECR, :], TZTM[DECR:DECR + MIXR, :]
        TOT = {1: D}
        for n in (2, 4, 8, 16, 32, 64):
            TOT[n] = sb(f"TOT{n}", [128, KC * COLS // n])[:, :]
        V = sb("V", [128, PAIRS, C])
        KVM = D.rearrange("p (i n) -> p i n", i=2)
        RS = sb("RS", [HEADS, COLS])
        X1 = sb("X1", [128, PAIRS, C])
        BNS = sb("BNS", [128, PAIRS, 6])
        MV = sb("MV", [128, PAIRS, 2])
        RSTD = sb("RSTD", [128, PAIRS])
        XHI = sb("XHI", [128, PAIRS, KC, 128], F16)
        XLO = sb("XLO", [128, PAIRS, KC, 128], F16)
        GF = sb("GF", [128, 2, 512])
        GSQ = sb("GSQ", [128, 2, 512])
        GW = sb("GW", [128, 512])
        HHI = sb("HHI", [128, MH, 128], F16)
        HLO = sb("HLO", [128, MH, 128], F16)
        GA = sb("GA", [128, 512])
        QA = sb("QA", [128, 512])
        GR = sb("GR", [128, 2, 128])
        ST = sb("ST", [128, PAIRS, 4])
        FV, FSC = sb("FV", [128, PAIRS]), sb("FSC", [128, PAIRS])
        FBN = sb("FBN", [128, PAIRS, 6])
        FMV = sb("FMV", [128, PAIRS, 2])
        OSD = sb("OSD", [128, PAIRS])
        OUT = sb("OUT", [128, PAIRS, C])
        PAUSE = sb("PAUSE", [1, 8])
        SC = sb("SC", [128, 32])
        AMAX = SC[:, 0:2]
        RED = GF[:, 0, 0:256]
        VMEAN = GF[:, 1, 0:KC * HEADS]

        psP = ctx.enter_context(nc.psum_tensor("psP", [128, 2, 512], F32))
        psW = ctx.enter_context(nc.psum_tensor("psW", [128, 2, 512], F32))
        psX = ctx.enter_context(nc.psum_tensor("psX", [128, 512], F32))
        psY = ctx.enter_context(nc.psum_tensor("psY", [128, 512], F32))
        psF = ctx.enter_context(nc.psum_tensor("psF", [128, 2, 512], F32))

        const_in, weights_in, wfc_in, wpj_in = sem("const_in"), sem("weights_in"), sem("wfc_in"), sem("wpj_in")
        xt_in, xtok_in, out_stored = sem("xt_in"), sem("xtok_in"), sem("out_stored")
        quantised = sem("quantised")
        su_dve, su_pe, su_act, su_pool = sem("setup_dve"), sem("setup_pe"), sem("setup_act"), sem("setup_pool")
        p_full, p_act, p_dve = sem("p_full"), sem("p_read_act"), sem("p_read_dve")
        w_full, w_act, w_dve = sem("w_full"), sem("w_read_act"), sem("w_read_dve")
        x_full, x_act, x_dve = sem("x_full"), sem("x_read_act"), sem("x_read_dve")
        tm_first, tm_ready, down_step = sem("tm_first"), sem("tm_ready"), sem("down_step")
        f_full, f_act = sem("f_full"), sem("f_read_act")
        f_stats, f_product = sem("f_read_stats"), sem("f_read_product")
        y_full, y_copied, y_squared = sem("y_full"), sem("y_copied"), sem("y_squared")
        xx_ready, xm_ready, xf_ready = sem("xx_ready"), sem("xm_ready"), sem("xf_ready")
        gate_tanh, ew_ready, d_ready = sem("gate_tanh"), sem("ew_ready"), sem("d_ready")
        km_ready, k1_even, k1_odd = sem("km_ready"), sem("k1_even"), sem("k1_odd")
        rb_act, rb_dve = sem("rb_act"), sem("rb_dve")
        r_scaled, k_scaled, tot_ready = sem("r_scaled"), sem("k_scaled"), sem("tot_ready")
        a_l1, ab_diag = sem("a_l1"), sem("ab_diag")
        kvm_ready, s_decayed, s_ready = sem("kvm_ready"), sem("s_decayed"), sem("s_ready")
        rs_inv, y_affine, z_ready = sem("rs_inv"), sem("y_affine"), sem("z_ready")
        bn_done, mv_ready, rstd_ready = sem("bn_done"), sem("mv_ready"), sem("rstd_ready")
        x1_ready, xhi_ready, x1_biased = sem("x1_ready"), sem("xhi_ready"), sem("x1_biased")
        g_squared, gw_ready = sem("g_squared"), sem("gw_ready")
        hhi_ready, hlo_ready, sums_added, sums_folded = sem("hhi_ready"), sem("hlo_ready"), sem("sums_added"), sem("sums_folded")
        root_taken = sem("root_taken")
        setup_step, st_step, o_step, out_ready = sem("setup_step"), sem("st_step"), sem("o_step"), sem("out_ready")

        P = Ring(P_SEQ, 2, p_full, {"act": p_act, "dve": p_dve, "tanh": tm_ready}, {"tanh": 2})
        W = Ring(W_SEQ, 2, w_full, {"act": w_act, "dve": w_dve})
        X = Ring(X_SEQ, 1, x_full, {"act": x_act, "dve": x_dve})
        F = Ring(F_SEQ, 2, f_full, {"act": f_act, "stats": f_stats, "product": f_product})

        xprev, xcur = XT[:, :, 0:CH], XT[:, :, 1:CH + 1]

        def cc(buf, c):
            return buf[:, c * COLS:(c + 1) * COLS]

        def halves(buf, n):
            v = buf.rearrange("p (q two n) -> p q two n", two=2, n=n)
            return v[:, :, 0, :], v[:, :, 1, :]

        def grow(v, n):
            return v.unsqueeze(2).broadcast_to([v.shape[0], v.shape[1], n])

        def rows(h):
            return slice(HD * h, HD * (h + 1))

        NPL = len(LEVELS) + 2
        NWEIGHTS = 7

        def over_tiles(eng, attention, feed_forward):
            attention(0, True, None)
            if tiles > 1:
                attention(1, False, feed_forward(0, True))
            if tiles > 2:
                with eng.Fori(2, tiles) as it:
                    attention(it, False, feed_forward(eng.snap(it - 1), False))
            feed_forward(tiles - 1, tiles == 1).alone()

        block = ctx.enter_context(nc.Block())

        @block.sync
        def _(sp):
            for dst, src in ((CF[:, :], c_f32), (CM[:, :], c_mask), (PAR[:, :, :], par), (FWB[:, :, :], ffn_wb)):
                sp.dma_start(dst, src).then_inc(const_in, 16)
            for k in range(4):
                sp.dma_start(ARENA1[:, 2048 * k:2048 * (k + 1)], wfc[:, 2048 * k:2048 * (k + 1)]).then_inc(wfc_in, 16)
            for k in range(4):
                sp.dma_start(ARENA2[:, 2048 * k:2048 * (k + 1)], wpj[:, 2048 * k:2048 * (k + 1)]).then_inc(wpj_in, 16)
            for dst, src in ((W1[:, :, :], w1), (W2A[:, :], w2a), (W2B[:, :], w2b), (TD1[:, :, :], td1),
                             (TD2[:, :], td2), (WALL[:, 1:4, :, :], w_all[:, 1:4, :, :])):
                sp.dma_start(dst, src).then_inc(weights_in, 16)
            sp.dma_start(WALL[:, 0:5:4, :, :], w_all[:, 0:5:4, :, :]).then_inc(weights_in, 16)

            sp.dma_start(XT[:, :, :], x_ch[0]).then_inc(xt_in, 16)

            def tile(it, first, ffn):
                sp.wait_ge(xf_ready, 5 * (it + 1))
                nxt = sp.snap(it + 1) if not isinstance(it, int) else it + 1
                sp.dma_start(XT[:, :, :], x_ch[nxt]).then_inc(xt_in, 16)
                sp.wait_ge(x_full, X.full(it, "kt1"))
                sp.dma_start(XTOK[:, :, :], x_tok[it]).then_inc(xtok_in, 16)
                if ffn:
                    ffn.finish(0)
                    ffn.finish(1)

            def feed_forward(j, first):
                def store(p):
                    sp.wait_ge(out_ready, PAIRS * j + p + 1)
                    sp.dma_start(out[j, :, p, :], OUT[:, p, :]).then_inc(out_stored, 16)

                def alone():
                    for p in range(PAIRS):
                        store(p)
                return FeedForward(finish=store, alone=alone)

            over_tiles(sp, tile, feed_forward)
            sp.wait_ge(out_stored, 16 * PAIRS * tiles)

        @block.tensor
        def _(pe):
            pe.wait_ge(su_dve, 1)
            pe.wait_ge(const_in, 16 * 4)
            pe.matmul(psP[:, 0, 0:1], ONES, SC[:, 8:9], start=True, stop=True).then_inc(su_pe, 1)
            pe.wait_ge(su_dve, 2)
            pe.matmul(psP[:, 1, 0:1], ONES, SC[:, 9:10], start=True, stop=True).then_inc(su_pe, 1)
            pe.wait_ge(su_dve, 3)
            pe.transpose(psX[0:2, 0:128], SC[:, 10:12], IDENT).then_inc(su_pe, 1)
            pe.wait_ge(su_dve, 4)
            pe.matmul(psY[:, 0:1], ONES[0:2, :], SC[0:2, 14:15], start=True, stop=True)
            pe.matmul(psY[:, 1:2], ONES[0:2, :], SC[0:2, 15:16], start=True, stop=True).then_inc(su_pe, 1)
            for v in range(2):
                pe.wait_ge(su_dve, 5 + v)
                for m in range(MH):
                    for part, h in enumerate((HHI, HLO)):
                        mm = pe.matmul(psW[:, v, :], h[:, m, :], WPJ[:, m, :], start=(m == 0 and part == 0),
                                       stop=(m == MH - 1 and part == 1))
                mm.then_inc(su_pe, 1)
            pe.wait_ge(su_dve, 8)
            pe.wait_ge(su_pool, 1)
            pe.wait_ge(weights_in, 16 * NWEIGHTS)

            def tanh_argument(ps, lo, n):
                for k in range(KC):
                    mm = pe.matmul(ps, W1[:, k, lo:lo + n], cc(XF[1], k), start=(k == 0), stop=(k == KC - 1))
                return mm

            pe.wait_ge(xm_ready, 1)
            tanh_argument(psX[:, 0:COLS], 0, 4 * MIXR).then_inc(tm_first, 1)
            tanh_argument(psY[0:MIXR, 0:COLS], 4 * MIXR, MIXR).then_inc(tm_first, 1)

            def tile(it, first, ffn):
                def mix(f, name):
                    pe.wait_ge(tm_ready, P.read(it - 1, "w1a" if f < 4 else "w1b"))
                    lhs, rhs = (W2A[rows(f), :], TMA[rows(f), :]) if f < 4 else (W2B[:, :], TMB[:, :])
                    for g in range(2):
                        P.wait_free(pe, it, f"{name}{g}", first)
                        for c in range(2):
                            mm = pe.matmul(psP[:, P.bank(f"{name}{g}"), COLS * c:COLS * (c + 1)],
                                           lhs[:, 128 * (2 * g + c):128 * (2 * g + c + 1)], rhs, start=True, stop=True)
                        mm.then_inc(p_full, 1)

                def channels(name, w, f, slot):
                    pe.wait_ge(xf_ready, 5 * it + f + 1)
                    for g in range(2):
                        P.wait_free(pe, it, f"{name}{g}", first)
                        for c in range(2):
                            for k in range(KC):
                                mm = pe.matmul(psP[:, P.bank(f"{name}{g}"), COLS * c:COLS * (c + 1)],
                                               WALL[:, w, k, 128 * (2 * g + c):128 * (2 * g + c + 1)], cc(XF[slot], k),
                                               start=(k == 0), stop=(k == KC - 1))
                        mm.then_inc(p_full, 1)

                mix(0, "mw")
                mix(1, "mk")
                pe.wait_ge(xf_ready, 5 * it + 1)
                P.wait_free(pe, it, "td1", first)
                for k in range(KC):
                    mm = pe.matmul(psP[0:DECR, P.bank("td1"), 0:COLS], TD1[:, k, :], cc(XF[0], k),
                                   start=(k == 0), stop=(k == KC - 1))
                mm.then_inc(p_full, 1)
                mix(2, "mv")
                pe.wait_ge(p_act, P.read(it, "td1"))
                for g in range(2):
                    P.wait_free(pe, it, f"td2{g}", first)
                    for c in range(2):
                        mm = pe.matmul(psP[:, P.bank(f"td2{g}"), COLS * c:COLS * (c + 1)],
                                       TD2[:, 128 * (2 * g + c):128 * (2 * g + c + 1)], TZ[:, :], start=True, stop=True)
                    mm.then_inc(p_full, 1)
                channels("k", W_K, 1, 1)
                mix(3, "mr")
                pe.wait_ge(xf_ready, 5 * it + 3)
                for p in range(PAIRS):
                    P.wait_free(pe, it, f"v{p}", first)
                    for k in range(KC):
                        mm = pe.matmul(psP[:, P.bank(f"v{p}"), :], cc(XF[0], k)[:, 128 * p:128 * (p + 1)],
                                       WALL[:, W_V, k, :], start=(k == 0), stop=(k == KC - 1))
                    mm.then_inc(p_full, 1)
                mix(4, "mg")
                channels("r", W_R, 3, 1)
                channels("g", W_G, 4, 0)
                if ffn:
                    ffn.up(0, 0)

                pe.wait_ge(k1_odd, it + 1)
                pe.wait_ge(k1_even, 2 * it + 2)
                for p in range(PAIRS):
                    name = f"l1_{p}"
                    W.wait_free(pe, it, name, first)
                    pe.wait_ge(rb_dve, 2 * it + p + 1)
                    pe.wait_ge(rb_act, 7 * it + p + 1)
                    for q in range(4):
                        for c in range(KC):
                            o = 128 * p + BLK * q
                            mm = pe.matmul(psW[BLK * q:BLK * (q + 1), W.bank(name), 128 * c:128 * (c + 1)],
                                           cc(K1, c)[:, o:o + BLK], RB[p][:, c, :, BLK * q:BLK * (q + 1)],
                                           start=True, stop=True, skip_group_check=True)
                    mm.then_inc(w_full, 1)
                    if ffn:
                        ffn.up(0, 1 + p)
                for i, n in enumerate(LEVELS):
                    name = f"l{n}"
                    W.wait_free(pe, it, name, first)
                    pe.wait_ge(k_scaled, NPL * it + i + 1)
                    pe.wait_ge(rb_act, 7 * it + i + 3)
                    for q in range(8):
                        for c in range(KC):
                            o = 256 * (q // 4) + 64 * c
                            mm = pe.matmul(psW[BLK * (q % 4):BLK * (q % 4 + 1), W.bank(name), o:o + 64],
                                           cc(KM, c)[:, BLK * q:BLK * (q + 1)],
                                           RB[RB_SEQ[name]][:, c, :, 16 * q:16 * (q + 1)],
                                           start=True, stop=True, skip_group_check=True)
                    mm.then_inc(w_full, 1)
                    if ffn and i == 0:
                        ffn.up(0, 3)
                    elif ffn:
                        ffn.down(0, i - 1)
                pe.wait_ge(k_scaled, NPL * it + 5)
                pe.wait_ge(rb_act, 7 * it + 7)
                for p in range(PAIRS):
                    name = f"l32_{p}"
                    W.wait_free(pe, it, name, first)
                    for h in range(2):
                        b = 2 * p + h
                        for c in range(KC):
                            mm = pe.matmul(psW[64 * h:64 * h + BLK, W.bank(name), 128 * c:128 * (c + 1)],
                                           cc(KM, c)[:, CH * b:CH * b + BLK], RB[0][:, c, :, BLK * b:BLK * (b + 1)],
                                           start=True, stop=True, skip_group_check=True)
                    mm.then_inc(w_full, 1)
                if ffn:
                    ffn.down(0, 3)
                    ffn.stats(0)
                pe.wait_ge(k_scaled, NPL * it + 6)
                for p in range(PAIRS):
                    X.wait_free(pe, it, f"kt{p}", first)
                    for c in range(KC):
                        mm = pe.transpose(psX[:, 128 * c:128 * (c + 1)], cc(KM, c)[:, 128 * p:128 * (p + 1)], IDENT)
                    mm.then_inc(x_full, 1)
                pe.wait_ge(r_scaled, NPL * it + 6)
                pe.wait_ge(p_act, P.read(it, "v1"))
                pe.wait_ge(su_pool, 2)
                if not first:
                    pe.wait_ge(s_ready, B * it)
                for p in range(PAIRS):
                    if p or not first:
                        pe.wait_ge(y_copied, 2 * it + p)
                    for c in range(KC):
                        for h in range(2):
                            b = 2 * p + h
                            pe.matmul(psY[:, 128 * c + CH * h:128 * c + CH * (h + 1)], S[:, b, c, :],
                                      cc(RM, c)[:, CH * b:CH * (b + 1)], start=(c == 0 and h == 0), stop=False,
                                      skip_group_check=True)
                    if ffn and p:
                        ffn.up(1, 1)
                    pe.wait_ge(ab_diag, 2 * it + p + 1)
                    pe.wait_ge(w_act, W.read(it, f"l32_{p}"))
                    for c in range(KC):
                        for h in range(HPG):
                            mm = pe.matmul(psY[rows(h), 128 * c:128 * (c + 1)], V[:, p, 128 * c + HD * h:128 * c + HD * (h + 1)],
                                           AB[:, HPG * c + h, :], start=False, stop=True, skip_group_check=True)
                    mm.then_inc(y_full, 1)
                    if ffn and p == 0:
                        ffn.up(1, 0)
                pe.wait_ge(x_act, X.read(it, "kt1"))
                for b in range(B):
                    X.wait_free(pe, it, f"kv{b}", first)
                    r = slice(CH * (b % 2), CH * (b % 2 + 1))
                    for c in range(KC):
                        mm = pe.matmul(psX[:, 128 * c:128 * (c + 1)], KT[r, b // 2, 128 * c:128 * (c + 1)],
                                       V[r, b // 2, 128 * c:128 * (c + 1)], start=True, stop=True, skip_group_check=True)
                    mm.then_inc(x_full, 1)
                    if ffn and b < 2:
                        ffn.up(1, 2 + b)
                    elif ffn:
                        ffn.down(1, b - 2)
                pe.wait_ge(y_squared, 2 * it + 2)
                P.wait_free(pe, it, "var", first)
                for k in range(KC):
                    mm = pe.matmul(psP[0:HEADS, P.bank("var"), 0:COLS], SEL[:, k, :], cc(YSQ, k), start=(k == 0), stop=(k == KC - 1))
                mm.then_inc(p_full, 1)
                if ffn:
                    ffn.down(1, 2)
                pe.wait_ge(rs_inv, it + 1)
                for g in range(2):
                    P.wait_free(pe, it, f"rb{g}", first)
                    for c in range(2):
                        mm = pe.matmul(psP[:, P.bank(f"rb{g}"), COLS * c:COLS * (c + 1)], SPREAD[0:HEADS, 2 * g + c, :],
                                       RS[:, :], start=True, stop=True)
                    mm.then_inc(p_full, 1)
                pe.wait_ge(xm_ready, it + 2)
                for name, lo, n in (("w1a", 0, 4 * MIXR), ("w1b", 4 * MIXR, MIXR)):
                    P.wait_free(pe, it, name, first)
                    tanh_argument(psP[0:n, P.bank(name), 0:COLS], lo, n).then_inc(p_full, 1)
                pe.wait_ge(z_ready, 2 * it + 2)
                for p in range(PAIRS):
                    P.wait_free(pe, it, f"wo{p}", first)
                    for k in range(KC):
                        mm = pe.matmul(psP[:, P.bank(f"wo{p}"), :], cc(YSB, k)[:, 128 * p:128 * (p + 1)], WALL[:, W_O, k, :],
                                       start=(k == 0), stop=(k == KC - 1))
                    mm.then_inc(p_full, 1)
                if ffn:
                    ffn.down(1, 3)
                    ffn.stats(1)
                for p in range(PAIRS):
                    pe.wait_ge(x1_ready, 2 * it + p + 1)
                    P.wait_free(pe, it, f"xt{p}", first)
                    for c in range(KC):
                        mm = pe.transpose(psP[:, P.bank(f"xt{p}"), 128 * c:128 * (c + 1)], X1[:, p, 128 * c:128 * (c + 1)], IDENT)
                    mm.then_inc(p_full, 1)

            def feed_forward(j, first):
                def up(p, g):
                    if g == 0:
                        pe.wait_ge(p_dve, P.read(j, f"xt{p}"))
                    name = f"fc{g}_{p}"
                    F.wait_free(pe, j, name, first)
                    for m in range(4):
                        for k in range(KC):
                            for part, x in enumerate((XHI, XLO)):
                                mm = pe.matmul(psF[:, F.bank(name), 128 * m:128 * (m + 1)],
                                               WFC[:, k, 128 * (4 * g + m):128 * (4 * g + m + 1)], x[:, p, k, :],
                                               start=(k == 0 and part == 0), stop=(k == KC - 1 and part == 1))
                    mm.then_inc(f_full, 1)

                def stats(p):
                    pe.wait_ge(sums_folded, 2 * j + p + 1)
                    F.wait_free(pe, j, f"st_{p}", first)
                    for i in range(2):
                        mm = pe.matmul(psF[:, F.bank(f"st_{p}"), i:i + 1], GR[:, i, :], ONES[:, 0:1], start=True, stop=True)
                    mm.then_inc(f_full, 1)

                def down(p, part):
                    pe.wait_ge(hlo_ready, 8 * j + 4 * p + part + 1)
                    if part == 0:
                        F.wait_free(pe, j, f"pj_{p}", first)
                    for m in range(MH // 4 * part, MH // 4 * (part + 1)):
                        for h in (HHI, HLO):
                            mm = pe.matmul(psF[:, F.bank(f"pj_{p}"), :], h[:, m, :], WPJ[:, m, :],
                                           start=(m == 0 and h is HHI), stop=(m == MH - 1 and h is HLO))
                    mm.then_inc(f_full if part == 3 else down_step, 1)

                def alone():
                    for p in range(PAIRS):
                        for g in range(4):
                            up(p, g)
                        for part in range(4):
                            down(p, part)
                        stats(p)
                return FeedForward(up=up, stats=stats, down=down, alone=alone)

            over_tiles(pe, tile, feed_forward)

        @block.scalar
        def _(act):
            act.wait_ge(su_dve, 8)
            act.wait_ge(su_pool, 2)
            act.wait_ge(weights_in, 16 * NWEIGHTS)
            act.wait_ge(tm_first, 1)
            act.activation(TMA[:, :], psX[:, 0:COLS], ACT.Tanh).then_inc(tm_ready, 1)
            act.wait_ge(tm_first, 2)
            act.activation(TMB[:, :], psY[0:MIXR, 0:COLS], ACT.Tanh).then_inc(tm_ready, 1)

            def copy(o, i):
                return act.activation(o, i, ACT.Copy)

            def tile(it, first, ffn):
                act.wait_ge(p_full, P.full(it, "td1"))
                act.activation(TZ[:, :], psP[0:DECR, P.bank("td1"), 0:COLS], ACT.Tanh).then_inc(p_act, 1)
                if not first:
                    act.wait_ge(tot_ready, NPL * it)
                    act.wait_ge(r_scaled, NPL * it)
                    act.wait_ge(k_scaled, NPL * it)
                    act.wait_ge(s_ready, B * it)
                for g in range(2):
                    act.wait_ge(p_full, P.full(it, f"td2{g}"))
                    for c in range(2):
                        k = 2 * g + c
                        e = act.activation(cc(D, k), psP[:, P.bank(f"td2{g}"), COLS * c:COLS * (c + 1)], ACT.Exp,
                                           bias=PAR[:, k, DECAY:DECAY + 1])
                    e.then_inc(p_act, 1)
                act.wait_ge(p_act, P.read(it, "td21"))
                act.activation(D, D, ACT.Exp, scale=-1.0).then_inc(d_ready, 1)
                if not first:
                    act.wait_ge(x_full, X.full(it - 1, "kv3"))
                    act.wait_ge(p_dve, P.read(it - 1, "wo1"))
                for g in range(2):
                    act.wait_ge(p_full, P.full(it, f"k{g}"))
                    src = psP[:, P.bank(f"k{g}"), :]
                    copy(halves(K1[:, 512 * g:512 * (g + 1)], 1)[0], halves(src, 1)[0]).then_inc(k1_even, 1)
                    copy(KM[:, 512 * g:512 * (g + 1)], src).then_inc(p_act, 1)
                for p in range(PAIRS):
                    act.wait_ge(p_full, P.full(it, f"v{p}"))
                    copy(V[:, p, :], psP[:, P.bank(f"v{p}"), :]).then_inc(p_act, 1)
                for g in range(2):
                    act.wait_ge(p_full, P.full(it, f"r{g}"))
                    copy(RM[:, 512 * g:512 * (g + 1)], psP[:, P.bank(f"r{g}"), :]).then_inc(p_act, 1)
                act.wait_ge(p_act, P.read(it, "r1"))
                for p in range(PAIRS):
                    if not first:
                        act.wait_ge(w_full, W.full(it - 1, "l32_1" if p == 0 else "l16"))
                    for h in range(HPG):
                        e = copy(RB[p][rows(h), :, h, 1:128:2],
                                 RM[rows(h), :].rearrange("p (c t) -> p c t", c=KC)[:, :, 128 * p + 1:128 * (p + 1):2])
                    e.then_inc(rb_act, 1)
                if not first:
                    act.wait_ge(z_ready, 2 * it)
                for g in range(2):
                    act.wait_ge(p_full, P.full(it, f"g{g}"))
                    act.activation(G[:, 512 * g:512 * (g + 1)], psP[:, P.bank(f"g{g}"), :], ACT.Tanh, scale=0.5).then_inc(gate_tanh, 1)
                if ffn:
                    ffn.up(0, 0)
                for i, n in enumerate(LEVELS + (BLK,)):
                    act.wait_ge(r_scaled, NPL * it + i + 1)
                    act.wait_ge(w_full, W.full(it, W_SEQ[i][0]))
                    for h in range(HPG):
                        src = halves(RM[rows(h), :], n)[1].rearrange("p (c q) n -> p c q n", c=KC)
                        dst = RB[i % 2][rows(h), :, h, :].rearrange("p c (q n) -> p c q n", n=n)
                        e = copy(dst, src)
                    e.then_inc(rb_act, 1)
                    if ffn and i < 3:
                        ffn.up(0, i + 1)
                for p in range(PAIRS):
                    if not first or p:
                        act.wait_ge(y_full, 2 * it + p)
                    if p == 0:
                        act.wait_ge(w_dve, W.read(it, "l16"))
                    for q in range(4):
                        r = slice(BLK * q, BLK * (q + 1))
                        e = copy(AB[r, :, BLK * q:BLK * (q + 1)],
                                 A[r, 512 * p:512 * (p + 1)].rearrange("p (h t) -> p h t", h=HEADS))
                    e.then_inc(ab_diag, 1)
                    act.wait_ge(w_full, W.full(it, f"l32_{p}"))
                    for h in range(2):
                        r = slice(64 * h, 64 * h + BLK)
                        e = copy(AB[r, :, 64 * h + BLK:64 * h + 2 * BLK],
                                 psW[r, W.bank(f"l32_{p}"), :].rearrange("p (h t) -> p h t", h=HEADS))
                    e.then_inc(w_act, 1)
                    if p == 0:
                        for q in range(PAIRS):
                            act.wait_ge(x_full, X.full(it, f"kt{q}"))
                            copy(KT[:, q, :], psX[:, :]).then_inc(x_act, 1)
                    if ffn and p:
                        ffn.up(1, 0)
                    act.wait_ge(y_copied, 2 * it + p + 1)
                    act.activation(YSQ.rearrange("p (c t) -> p c t", c=KC)[:, :, 128 * p:128 * (p + 1)],
                                   YSB.rearrange("p (c t) -> p c t", c=KC)[:, :, 128 * p:128 * (p + 1)], ACT.Square).then_inc(y_squared, 1)
                if ffn:
                    for g in range(1, 4):
                        ffn.up(1, g)
                act.wait_ge(p_full, P.full(it, "var"))
                act.activation(RS[:, :], psP[0:HEADS, P.bank("var"), 0:COLS], ACT.Sqrt, bias=EPS[0:HEADS, 0:1]).then_inc(p_act, 1)
                act.wait_ge(p_full, P.full(it, "w1a"))
                act.activation(TMA[:, :], psP[:, P.bank("w1a"), 0:COLS], ACT.Tanh).then_inc(tm_ready, 1)
                act.wait_ge(p_full, P.full(it, "w1b"))
                act.activation(TMB[:, :], psP[0:MIXR, P.bank("w1b"), 0:COLS], ACT.Tanh).then_inc(tm_ready, 1)
                for p in range(PAIRS):
                    act.wait_ge(p_full, P.full(it, f"xt{p}"))
                    copy(XHI[:, p, :, :], psP[:, P.bank(f"xt{p}"), :].rearrange("p (c t) -> p c t", c=KC)).then_inc(xhi_ready, 1)

            def feed_forward(j, first):
                def up(p, g):
                    u = 4 * p + g
                    act.wait_ge(f_full, F.full(j, f"fc{g}_{p}"))
                    if u >= 2 or not first:
                        act.wait_ge(gw_ready, 8 * j + u - 1)
                        act.wait_ge(sums_added, 8 * j + u - 1)
                    act.activation(GF[:, u % 2, :], psF[:, F.bank(f"fc{g}_{p}"), :], ACT.Gelu).then_inc(f_act, 1)
                    act.wait_ge(f_act, 8 * j + u + 1)
                    act.activation(GSQ[:, u % 2, :], GF[:, u % 2, :], ACT.Square).then_inc(g_squared, 1)

                def alone():
                    for p in range(PAIRS):
                        for g in range(4):
                            up(p, g)
                return FeedForward(up=up, alone=alone)

            over_tiles(act, tile, feed_forward)

        @block.gpsimd
        def _(pool):
            pool.wait_ge(quantised, 8)
            pool.memset(ARENA1[:, 0:6144], 0.0).then_inc(su_pool, 1)
            pool.memset(ARENA2[:, 0:2048], 0.0).then_inc(su_pool, 1)
            pool.wait_ge(su_dve, 8)
            pool.wait_ge(su_pool, 2)

            def inverse_root(v):
                return pool.tensor_tensor(v, v, MINUS_HALF.broadcast_to([128, v.shape[1]]), ALU.pow)

            def tile(it, first, ffn):
                pool.wait_ge(xt_in, 16 * (it + 1))
                for f, name in enumerate(("mw1", "mk1", "mv1", "mr1", "mg1")):
                    pool.wait_ge(p_dve, P.read(it, name))
                    v = XF[f % 2].rearrange("p (q t) -> p q t", t=CH)
                    pool.tensor_tensor(v, v, xcur, ALU.add).then_inc(xf_ready, 1)
                    if f == 3:
                        pool.wait_ge(p_act, P.read(it, "k1"))
                        pool.tensor_tensor(halves(K1, 1)[1].rearrange("p (c q) n -> p c (q n)", c=KC),
                                           halves(KM, 1)[1].rearrange("p (c q) n -> p c (q n)", c=KC),
                                           PAR[:, :, U:U + 1].broadcast_to([128, KC, COLS // 2]), ALU.mult).then_inc(k1_odd, 1)
                if ffn:
                    for g in range(4):
                        ffn.up(0, g)
                    ffn.finish(0)

                def decay(b):
                    pool.wait_ge(y_full, 2 * it + b // 2 + 1)
                    tot = TOT[64].rearrange("p (c b) -> p b c", b=B)[:, b, :]
                    pool.tensor_tensor(S[:, b, :, :], S[:, b, :, :], grow(tot, 128), ALU.mult).then_inc(s_decayed, 1)

                def update(b):
                    pool.wait_ge(s_decayed, B * it + b + 1)
                    pool.wait_ge(x_dve, X.read(it, f"kv{b}"))
                    pool.tensor_tensor(S[:, b, :, :], S[:, b, :, :], KVM[:, b % 2, :].rearrange("p (c n) -> p c n", c=KC),
                                       ALU.add).then_inc(s_ready, 1)

                pool.wait_ge(tot_ready, NPL * it + 6)
                decay(0)
                decay(1)
                if ffn:
                    ffn.up(1, 0)
                decay(2)
                decay(3)
                for b in range(B):
                    update(b)
                    if ffn and b < 3:
                        ffn.up(1, 1 + b)
                pool.wait_ge(p_dve, P.read(it, "g1"))
                for g in range(2):
                    z = YSB[:, 512 * g:512 * (g + 1)]
                    pool.wait_ge(y_affine, KC * it + 2 * (g + 1))
                    pool.tensor_tensor(z, z, G[:, 512 * g:512 * (g + 1)], ALU.mult).then_inc(z_ready, 1)
                pool.wait_ge(mv_ready, 2 * (it + 1))
                inverse_root(RSTD[:, :]).then_inc(rstd_ready, 1)
                if ffn:
                    ffn.finish(1)
                    pool.wait_ge(out_stored, 16 * PAIRS * it)
                for p in range(PAIRS):
                    pool.wait_ge(x1_ready, 2 * it + p + 1)
                    pool.tensor_tensor(OUT[:, p, :], X1[:, p, :], BSUM[:, :], ALU.add).then_inc(x1_biased, 1)

            def feed_forward(j, first):
                def up(p, g):
                    u = 4 * p + g
                    for acc, src, ready, n in ((GA, GF, f_act, 1), (QA, GSQ, g_squared, 2)):
                        pool.wait_ge(ready, 8 * j + u + 1)
                        if g == 0:
                            if p or not first:
                                pool.wait_ge(sums_folded, 2 * j + p)
                            e = pool.tensor_tensor(acc[:, :], src[:, u % 2, :], ZERO.broadcast_to([128, 512]), ALU.add)
                        else:
                            if n == 1:
                                pool.wait_ge(sums_added, 8 * j + u)
                            e = pool.tensor_tensor(acc[:, :], acc[:, :], src[:, u % 2, :], ALU.add)
                    e.then_inc(sums_added, 1)

                def finish(p):
                    pool.wait_ge(st_step, 4 * (PAIRS * j + p) + 3)
                    inverse_root(FV[:, p:p + 1]).then_inc(root_taken, 1)
                    pool.wait_ge(o_step, 3 * (PAIRS * j + p) + 3)
                    inverse_root(OSD[:, p:p + 1]).then_inc(root_taken, 1)

                def alone():
                    for p in range(PAIRS):
                        for g in range(4):
                            up(p, g)
                        finish(p)
                return FeedForward(up=up, finish=finish, alone=alone)

            over_tiles(pool, tile, feed_forward)

        @block.vector
        def _(dve):
            def after_wait(i):
                dve.memset(PAUSE[:, i:i + 1], 0.0)

            dve.wait_ge(const_in, 16 * 4)
            for i, (arena, here) in enumerate(((ARENA1, wfc_in), (ARENA2, wpj_in))):
                dve.wait_ge(here, 64)
                dve.tensor_reduce(RED[:, 128 * i:128 * (i + 1)], arena[:, :].rearrange("p (q n) -> p q n", n=64), AX.X, ALU.add,
                                  apply_absolute_value=True).then_inc(setup_step, 1)
                dve.wait_ge(setup_step, i + 1)
                dve.tensor_reduce(SC[:, 8 + i:9 + i], RED[:, 128 * i:128 * (i + 1)], AX.X, ALU.add).then_inc(su_dve, 1)
            dve.tensor_reduce(SC[:, 10:12], FWB[:, :, :], AX.X, ALU.max, apply_absolute_value=True).then_inc(su_dve, 1)
            dve.wait_ge(su_pe, 3)
            dve.tensor_reduce(SC[0:2, 12:13], psX[0:2, 0:128], AX.X, ALU.max).then_inc(setup_step, 1)
            dve.wait_ge(setup_step, 3)
            dve.tensor_scalar(SC[0:2, 14:16], IDENT[0:2, 0:2], SC[0:2, 12:13], None, ALU.mult).then_inc(su_dve, 1)
            dve.wait_ge(su_pe, 4)
            dve.tensor_scalar(AMAX, psY[:, 0:2], 1e-30, None, ALU.max).then_inc(setup_step, 1)
            dve.wait_ge(setup_step, 4)
            dve.reciprocal(SC[:, 2:4], AMAX).then_inc(setup_step, 1)
            dve.wait_ge(setup_step, 5)
            dve.tensor_scalar(FWB[:, 0, :], FWB[:, 0, :], SC[:, 2:3], None, ALU.mult)
            dve.tensor_scalar(FWB[:, 1, :], FWB[:, 1, :], SC[:, 3:4], None, ALU.mult).then_inc(setup_step, 1)
            for i in range(2):
                dve.wait_ge(su_pe, i + 1)
                dve.tensor_scalar(SC[:, 16 + i:17 + i], psP[:, i, 0:1], 1.0 / (C * HID), GAMMA_EPS, ALU.mult, ALU.add).then_inc(setup_step, 1)
            dve.wait_ge(setup_step, 8)
            dve.tensor_scalar(SC[:, 18:20], SC[:, 16:18], 0.5, None, ALU.mult)
            dve.tensor_scalar(SC[:, 20:22], SC[:, 16:18], -0.5, None, ALU.mult).then_inc(setup_step, 1)
            dve.wait_ge(setup_step, 9)
            neg = HHI[:, :, :].rearrange("p m t -> p (m t)")
            n = 9
            for i, (arena, dst) in enumerate(((ARENA1, WFC), (ARENA2, WPJ))):
                flat = dst[:, :, :].rearrange("p a n -> p (a n)")
                for k in range(4):
                    src = arena[:, 2048 * k:2048 * (k + 1)]
                    dve.tensor_scalar(neg, src, SC[:, 20 + i:21 + i], None, ALU.is_lt).then_inc(setup_step, 1)
                    n += 1
                    dve.wait_ge(setup_step, n)
                    dve.scalar_tensor_tensor(out=flat[:, 2048 * k:2048 * (k + 1)], in0=src, scalar=SC[:, 18 + i:19 + i],
                                             in1=neg, op0=ALU.is_gt, op1=ALU.subtract).then_inc(quantised, 1)
                    dve.wait_ge(quantised, 4 * i + k + 1)
            for v in range(2):
                src = grow(FWB[:, v, :], 128)
                if v:
                    dve.wait_ge(su_pe, 5)
                dve.tensor_copy(HHI[:, :, :], src).then_inc(setup_step, 1)
                n += 1
                dve.wait_ge(setup_step, n)
                dve.tensor_tensor(HLO[:, :, :], src, HHI[:, :, :], ALU.subtract).then_inc(su_dve, 1)
            dve.wait_ge(su_pe, 6)
            dve.tensor_copy(WSUM[:, :], psW[:, 0, :])
            dve.tensor_scalar(BSUM[:, :], psW[:, 1, :], AMAX[:, 1:2], None, ALU.mult).then_inc(su_dve, 1)
            dve.wait_ge(weights_in, 16 * NWEIGHTS)
            wv = WALL[:, W_V, :, :].rearrange("p k (h j) -> p (k h) j", j=HD)
            dve.tensor_reduce(VMEAN, wv, AX.X, ALU.add).then_inc(setup_step, 1)
            n += 1
            dve.wait_ge(setup_step, n)
            dve.tensor_scalar(VMEAN, VMEAN, 1.0 / HD, None, ALU.mult).then_inc(setup_step, 1)
            n += 1
            dve.wait_ge(setup_step, n)
            dve.tensor_tensor(wv, wv, grow(VMEAN, HD), ALU.subtract)
            dve.tensor_scalar(PAR[:, :, LN_G:LN_B + 1], PAR[:, :, LN_G:LN_B + 1], 0.5, None, ALU.mult).then_inc(su_dve, 1)
            dve.wait_ge(su_dve, 8)
            dve.wait_ge(su_pool, 2)

            def differences(it):
                dve.wait_ge(xt_in, 16 * (it + 1))
                dve.tensor_tensor(XX[:, :, :], xprev, xcur, ALU.subtract).then_inc(xx_ready, 1)

            def mixed_by_x(it):
                dve.wait_ge(xx_ready, it + 1)
                for k in range(KC):
                    q = slice(B * k, B * (k + 1))
                    e = dve.scalar_tensor_tensor(out=cc(XF[1], k).rearrange("p (q t) -> p q t", t=CH), in0=XX[:, q, :],
                                                 scalar=PAR[:, k, MAA_X:MAA_X + 1], in1=xcur[:, q, :], op0=ALU.mult, op1=ALU.add)
                e.then_inc(xm_ready, 1)

            differences(0)
            mixed_by_x(0)

            def tile(it, first, ffn):
                def mix(f, name, before):
                    if before:
                        dve.wait_ge(p_full, P.full(it, before))
                    for g in range(2):
                        dve.wait_ge(p_full, P.full(it, f"{name}{g}"))
                        for c in range(2):
                            k = 2 * g + c
                            e = dve.scalar_tensor_tensor(
                                out=cc(XF[f % 2], k), in0=psP[:, P.bank(f"{name}{g}"), COLS * c:COLS * (c + 1)],
                                scalar=PAR[:, k, MIX_PAR[f]:MIX_PAR[f] + 1],
                                in1=XX[:, B * k:B * (k + 1), :].rearrange("p q t -> p (q t)"), op0=ALU.add, op1=ALU.mult)
                        e.then_inc(p_dve, 1)

                dve.wait_ge(xx_ready, it + 1)
                if not first:
                    dve.wait_ge(p_full, P.full(it - 1, "wo1"))
                mix(0, "mw", None)
                dve.wait_ge(tm_ready, P.read(it - 1, "w1b"))
                mix(1, "mk", None)
                mix(2, "mv", "td1")
                mix(3, "mr", "k1")
                mix(4, "mg", "v1")
                def scale(i, n):
                    tl, tr = TOT[n].rearrange("p (q two) -> p two q", two=2)[:, 0, :], TOT[n].rearrange("p (q two) -> p two q", two=2)[:, 1, :]
                    right = halves(RM, n)[1]
                    dve.wait_ge(rb_act, 7 * it + i + 2)
                    dve.tensor_tensor(right, right, grow(tl, n), ALU.mult).then_inc(r_scaled, 1)
                    if i == 0:
                        dve.wait_ge(k1_odd, it + 1)
                    else:
                        dve.wait_ge(w_full, W.full(it, f"l{n}" if n < 32 else "l32_1"))
                    left = halves(KM, n)[0]
                    dve.tensor_tensor(left, left, grow(tr, n), ALU.mult).then_inc(k_scaled, 1)
                    dve.tensor_tensor(TOT[2 * n], tl, tr, ALU.mult).then_inc(tot_ready, 1)
                    dve.wait_ge(tot_ready, NPL * it + i + 1)
                    dve.wait_ge(r_scaled, NPL * it + i + 1)
                    dve.wait_ge(k_scaled, NPL * it + i + 1)

                dve.wait_ge(p_act, P.read(it, "r1"))
                for p in range(PAIRS):
                    if not first:
                        dve.wait_ge(w_full, W.full(it - 1, "l32_1" if p == 0 else "l16"))
                    for h in range(HPG):
                        e = dve.tensor_tensor(RB[p][rows(h), :, h, 0:128:2],
                                               RM[rows(h), :].rearrange("p (c t) -> p c t", c=KC)[:, :, 128 * p:128 * (p + 1):2],
                                               PAR[rows(h), :, U:U + 1].broadcast_to([HD, KC, 64]), ALU.mult)
                    e.then_inc(rb_dve, 1)
                dve.wait_ge(d_ready, it + 1)
                scale(0, 1)
                for g in range(2):
                    dve.wait_ge(gate_tanh, 2 * it + g + 1)
                    dve.scalar_tensor_tensor(out=G[:, 512 * g:512 * (g + 1)], in0=G[:, 512 * g:512 * (g + 1)], scalar=1.0,
                                             in1=psP[:, P.bank(f"g{g}"), :], op0=ALU.add, op1=ALU.mult).then_inc(p_dve, 1)
                if not first:
                    dve.wait_ge(ab_diag, 2 * it)
                for p in range(PAIRS):
                    dve.wait_ge(w_full, W.full(it, f"l1_{p}"))
                    dve.tensor_tensor(A[:, 512 * p:512 * (p + 1)].rearrange("p (h t) -> p h t", t=BLK),
                                      psW[:, W.bank(f"l1_{p}"), :].rearrange("p (h t) -> p h t", t=BLK),
                                      MASK1.unsqueeze(1).broadcast_to([128, HEADS, BLK]), ALU.mult).then_inc(w_dve, 1)
                dve.wait_ge(w_dve, W.read(it, "l1_1"))
                for i, n in enumerate(LEVELS):
                    scale(i + 1, n)
                    av = A.rearrange("p (h q two n) -> p h q two n", two=2, n=n, h=2 * HEADS)[:, :, :, 1, :]
                    nq = 16 // n
                    data = psW[:, W.bank(f"l{n}"), :].rearrange("p (h q n) -> p h q n", h=2 * HEADS, n=n)
                    mask = CM[:, 16 * i:16 * (i + 1)].rearrange("p (q n) -> p q n", n=n).unsqueeze(1).broadcast_to([128, 2 * HEADS, nq, n])
                    after_wait(i)
                    dve.copy_predicated(av, mask, data).then_inc(w_dve, 1)
                    dve.wait_ge(w_dve, W.read(it, f"l{n}"))
                    if ffn:
                        ffn.up(0, i)
                if ffn:
                    ffn.stats(0)
                scale(5, 32)
                if ffn:
                    ffn.finish(0)
                for p in range(PAIRS):
                    dve.wait_ge(y_full, 2 * it + p + 1)
                    dve.tensor_copy(YSB.rearrange("p (c t) -> p c t", c=KC)[:, :, 128 * p:128 * (p + 1)],
                                    psY[:, :].rearrange("p (c t) -> p c t", c=KC)).then_inc(y_copied, 1)
                    if ffn and p == 0:
                        ffn.up(1, 0)
                for b in range(B):
                    dve.wait_ge(x_full, X.full(it, f"kv{b}"))
                    if b >= 2 or not first:
                        dve.wait_ge(s_ready, B * it + b - 1)
                    dve.tensor_tensor(KVM[:, b % 2, :].rearrange("p (c n) -> p c n", c=KC), psX[:, :].rearrange("p (c n) -> p c n", c=KC),
                                      BLKMASK.unsqueeze(1).broadcast_to([128, KC, 128]), ALU.mult).then_inc(x_dve, 1)
                    if ffn and b < 3:
                        ffn.up(1, 1 + b)
                dve.wait_ge(p_dve, P.read(it, "mg1"))
                differences(it + 1)
                dve.wait_ge(p_full, P.full(it, "var"))
                mixed_by_x(it + 1)
                dve.wait_ge(p_act, P.read(it, "var"))
                dve.reciprocal(RS[:, :], RS[:, :]).then_inc(rs_inv, 1)
                if ffn:
                    ffn.stats(1)
                dve.wait_ge(y_copied, 2 * it + 2)
                for g in range(2):
                    dve.wait_ge(p_full, P.full(it, f"rb{g}"))
                    v = YSB[:, 512 * g:512 * (g + 1)]
                    dve.tensor_tensor(v, v, psP[:, P.bank(f"rb{g}"), :], ALU.mult).then_inc(p_dve, 1)
                    dve.wait_ge(p_dve, P.read(it, f"rb{g}"))
                    for k in (2 * g, 2 * g + 1):
                        dve.tensor_scalar(cc(YSB, k), cc(YSB, k), PAR[:, k, LN_G:LN_G + 1], PAR[:, k, LN_B:LN_B + 1],
                                          ALU.mult, ALU.add).then_inc(y_affine, 1)
                dve.wait_ge(xtok_in, 16 * (it + 1))
                if not first:
                    dve.wait_ge(x1_biased, 2 * it)
                for p in range(PAIRS):
                    dve.wait_ge(p_full, P.full(it, f"wo{p}"))
                    dve.tensor_tensor(X1[:, p, :], psP[:, P.bank(f"wo{p}"), :], XTOK[:, p, :], ALU.add).then_inc(p_dve, 1)
                    dve.wait_ge(p_dve, P.read(it, f"wo{p}"))
                    dve.bn_stats(BNS[:, p, :], X1[:, p, :]).then_inc(bn_done, 1)
                dve.wait_ge(bn_done, 2 * it + 2)
                after_wait(4)
                dve.bn_aggr(MV[:, 0, :], BNS[:, 0, :])
                dve.bn_aggr(MV[:, 1, :], BNS[:, 1, :]).then_inc(mv_ready, 1)
                dve.wait_ge(mv_ready, 2 * it + 1)
                dve.tensor_scalar(RSTD[:, :], MV[:, :, 1], LN_EPS, None, ALU.add).then_inc(mv_ready, 1)
                dve.wait_ge(rstd_ready, it + 1)
                for p in range(PAIRS):
                    dve.tensor_scalar(X1[:, p, :], X1[:, p, :], MV[:, p, 0:1], RSTD[:, p:p + 1], ALU.subtract, ALU.mult).then_inc(x1_ready, 1)
                if ffn:
                    ffn.finish(1)
                for p in range(PAIRS):
                    dve.wait_ge(xhi_ready, 2 * it + p + 1)
                    dve.tensor_tensor(XLO[:, p, :, :], psP[:, P.bank(f"xt{p}"), :].rearrange("p (c t) -> p c t", c=KC),
                                      XHI[:, p, :, :], ALU.subtract).then_inc(p_dve, 1)

            def feed_forward(j, first):
                def up(p, g):
                    u = 4 * p + g
                    dve.wait_ge(f_act, 8 * j + u + 1)
                    if p or not first:
                        if g == 3:
                            dve.wait_ge(f_full, F.full(j if p else j - 1, f"pj_{1 - p}"))
                        else:
                            dve.wait_ge(down_step, 6 * j + 3 * p - 2 + g)
                    if u or not first:
                        dve.wait_ge(hlo_ready, 8 * j + u)
                    dve.tensor_tensor(GW[:, :].rearrange("p (m t) -> p m t", m=4), GF[:, u % 2, :].rearrange("p (m t) -> p m t", m=4),
                                      grow(FWB[:, 0, 4 * g:4 * (g + 1)], 128), ALU.mult).then_inc(gw_ready, 1)
                    dve.wait_ge(gw_ready, 8 * j + u + 1)
                    gw = GW[:, :].rearrange("p (m t) -> p m t", m=4)
                    dve.tensor_copy(HHI[:, 4 * g:4 * (g + 1), :], gw).then_inc(hhi_ready, 1)
                    dve.wait_ge(hhi_ready, 8 * j + u + 1)
                    dve.tensor_tensor(HLO[:, 4 * g:4 * (g + 1), :], gw, HHI[:, 4 * g:4 * (g + 1), :], ALU.subtract).then_inc(hlo_ready, 1)

                def stats(p):
                    dve.wait_ge(sums_added, 8 * j + 4 * p + 4)
                    dve.tensor_reduce(GR[:, 0, :], GA[:, :].rearrange("p (m t) -> p t m", m=4), AX.X, ALU.add)
                    dve.tensor_reduce(GR[:, 1, :], QA[:, :].rearrange("p (m t) -> p t m", m=4), AX.X, ALU.add).then_inc(sums_folded, 1)

                def finish(p):
                    st, s = ST[:, p, :], 4 * (PAIRS * j + p)
                    dve.wait_ge(f_full, F.full(j, f"st_{p}"))
                    dve.tensor_scalar(st[:, 0:2], psF[:, F.bank(f"st_{p}"), 0:2], 1.0 / HID, None, ALU.mult).then_inc(f_stats, 1)
                    dve.wait_ge(f_stats, F.read(j, f"st_{p}"))
                    dve.tensor_scalar(st[:, 2:3], st[:, 0:1], -1.0, None, ALU.mult).then_inc(st_step, 1)
                    dve.wait_ge(st_step, s + 1)
                    pj = psF[:, F.bank(f"pj_{p}"), :]
                    dve.scalar_tensor_tensor(out=pj, in0=WSUM[:, :], scalar=st[:, 2:3], in1=pj, op0=ALU.mult, op1=ALU.add)
                    dve.scalar_tensor_tensor(out=st[:, 3:4], in0=st[:, 0:1], scalar=st[:, 2:3], in1=st[:, 1:2],
                                             op0=ALU.mult, op1=ALU.add).then_inc(st_step, 1)
                    dve.wait_ge(st_step, s + 2)
                    dve.tensor_scalar(FV[:, p:p + 1], st[:, 3:4], 0.0, LN_EPS, ALU.max, ALU.add).then_inc(st_step, 1)
                    dve.wait_ge(root_taken, 2 * (PAIRS * j + p) + 1)
                    dve.tensor_scalar(FSC[:, p:p + 1], FV[:, p:p + 1], AMAX[:, 0:1], None, ALU.mult).then_inc(st_step, 1)
                    dve.wait_ge(st_step, s + 4)
                    dve.wait_ge(x1_biased, PAIRS * j + p + 1)
                    dve.scalar_tensor_tensor(out=OUT[:, p, :], in0=pj, scalar=FSC[:, p:p + 1], in1=OUT[:, p, :],
                                             op0=ALU.mult, op1=ALU.add).then_inc(f_product, 1)
                    dve.wait_ge(f_product, F.read(j, f"pj_{p}"))
                    dve.bn_stats(FBN[:, p, :], OUT[:, p, :]).then_inc(o_step, 1)
                    dve.wait_ge(o_step, 3 * (PAIRS * j + p) + 1)
                    after_wait(5 + p)
                    dve.bn_aggr(FMV[:, p, :], FBN[:, p, :]).then_inc(o_step, 1)
                    dve.wait_ge(o_step, 3 * (PAIRS * j + p) + 2)
                    dve.tensor_scalar(OSD[:, p:p + 1], FMV[:, p, 1:2], LN_EPS, None, ALU.add).then_inc(o_step, 1)
                    dve.wait_ge(root_taken, 2 * (PAIRS * j + p) + 2)
                    dve.tensor_scalar(OUT[:, p, :], OUT[:, p, :], FMV[:, p, 0:1], OSD[:, p:p + 1],
                                      ALU.subtract, ALU.mult).then_inc(out_ready, 1)

                def alone():
                    for p in range(PAIRS):
                        for g in range(4):
                            up(p, g)
                        stats(p)
                        finish(p)
                return FeedForward(up=up, stats=stats, finish=finish, alone=alone)

            over_tiles(dve, tile, feed_forward)


def _constants():
    p = np.arange(128)
    ident = np.eye(128)
    blk = (p[:, None] // HD == p[None, :] // HD) * 1.0
    ones = np.ones((128, 128))
    sel = np.zeros((128, KC, HEADS))
    spread = np.zeros((128, KC, 128))
    for c in range(KC):
        sel[p, c, HPG * c + p // HD] = 1.0 / HD
        spread[HPG * c + p // HD, c, p] = 1.0
    s, t = p[:, None] % BLK, np.arange(BLK)[None, :]
    mask1 = ((s == t) | ((s % 2 == 0) & (t == s + 1))) * 1.0
    eps = np.tile(np.array([[GN_EPS, LN_EPS, 0.0, -0.5]]), (128, 1))
    f = np.concatenate([ident, blk, ones, sel.reshape(128, -1), spread.reshape(128, -1), mask1, eps], 1).astype(np.float32)
    masks = []
    for n in LEVELS:
        r = np.arange(16)[None, :]
        masks.append((s // (2 * n) == r // n) & (s % (2 * n) < n))
    return f, np.concatenate(masks, 1).astype(np.uint32)


def kernel(**inputs):
    import concourse.bacc as _bacc
    from concourse.bass_utils import run_bass_kernel_spmd as _run

    g = {k.replace("L0_attn_", "a_").replace("L0_ffn_", "f_"): np.asarray(v) for k, v in inputs.items()}

    def by_part(w):
        return w.reshape(-1, 128, w.shape[-1]).transpose(1, 0, 2)

    x = g["a_x"]
    padded = np.pad(x, ((0, 0), (1, 0), (0, 0)))
    cuts = np.stack([padded[:, i * CH:i * CH + CH + 1] for i in range(TILES)])
    cuts = np.concatenate([cuts, np.zeros_like(cuts[:1])])
    x_ch = cuts.reshape(TILES + 1, B, CH + 1, KC, 128).transpose(0, 4, 3, 1, 2).reshape(TILES + 1, 128, KC * B, CH + 1)
    x_tok = x.reshape(PAIRS, 2, TILES, CH, C).transpose(2, 1, 3, 0, 4).reshape(TILES, 128, PAIRS, C)
    w_all = np.stack([by_part(g[n].T) for n in ("a_Wr", "a_Wk", "a_Wv", "a_Wg", "a_Wo")], 1)
    par = np.stack([g[n].reshape(KC, 128).T for n in
                    ("a_time_maa_x", "a_time_maa_w", "a_time_maa_k", "a_time_maa_v", "a_time_maa_r", "a_time_maa_g",
                     "a_time_decay", "a_u", "a_ln_g", "a_ln_b")], 2)
    c_f32, c_mask = _constants()
    arrays = {
        "x_ch": x_ch, "x_tok": x_tok, "w_all": w_all,
        "w1": by_part(g["a_maa_w1"]), "w2a": g["a_maa_w2"][0:4].reshape(128, C), "w2b": g["a_maa_w2"][4],
        "td1": by_part(g["a_td_w1"]), "td2": g["a_td_w2"], "par": par,
        "wfc": by_part(g["f_W_fc"].T).reshape(128, -1), "wpj": by_part(g["f_W_proj"].T).reshape(128, -1),
        "ffn_wb": np.stack([g["f_ln_w"].reshape(MH, 128).T, g["f_ln_b"].reshape(MH, 128).T], 1),
        "c_f32": c_f32, "c_mask": c_mask,
    }
    arrays = {k: np.ascontiguousarray(v) for k, v in arrays.items()}
    nc = _bacc.Bacc("TRN2", target_bir_lowering=False, num_devices=1)
    args = [nc.dram_tensor(k, a.shape, mybir.dt.from_np(a.dtype), kind="ExternalInput").ap() for k, a in arrays.items()]
    args.append(nc.dram_tensor("out", (TILES, 128, PAIRS, C), F32, kind="ExternalOutput").ap())
    rwkv_ffn_kernel(nc, *args)
    r = _run(nc, [arrays], core_ids=[0])
    out = r.results[0]["out"]
    return np.ascontiguousarray(out.reshape(TILES, 2, CH, PAIRS, C).transpose(3, 1, 0, 2, 4).reshape(B, T, C))
```

```python
from contextlib import ExitStack

import numpy as np

import concourse.bass as bass
from concourse import mybir

F32 = mybir.dt.float32
F16 = mybir.dt.float16
U32 = mybir.dt.uint32
ALU = mybir.AluOpType
ACT = mybir.ActivationFunctionType
AX = mybir.AxisListType

B, T, C = 4, 2048, 512
HEADS, HD = 16, 32
HID = 2048
MIXR, DECR = 32, 64
CH = 64
COLS = B * CH
KC = C // 128
HPG = 128 // HD
MH = HID // 128
TILES = T // CH
PAIRS = B // 2
BLK = 32
GN_EPS = 1e-5 * 8 ** 2
LN_EPS = 1e-5
GAMMA_EPS = 1e-6
LEVELS = (2, 4, 8, 16)

MAA_X, MAA_W, MAA_K, MAA_V, MAA_R, MAA_G, DECAY, U, LN_G, LN_B = range(10)
NPAR = 10
MIX_PAR = (MAA_W, MAA_K, MAA_V, MAA_R, MAA_G)
W_R, W_K, W_V, W_G, W_O = range(5)

P_SEQ = [("td1", "act"), ("td20", "act"), ("td21", "act"), ("k0", "act"), ("k1", "act"), ("v0", "act"), ("v1", "act"),
         ("r0", "act"), ("r1", "act"), ("g0", "dve"), ("g1", "dve"), ("var", "act"), ("rb0", "dve"), ("rb1", "dve"),
         ("wo0", "dve"), ("wo1", "dve")]
M_SEQ = ([(f"{m}{g}", "dve") for m in ("mk", "mv", "mr", "mg") for g in range(2)]
         + [("w1a", "tanh"), ("w1b", "tanh"), ("mw0", "dve"), ("mw1", "dve")])
W_SEQ = [("l1_0", "dve"), ("l1_1", "dve"), ("l2", "dve"), ("l4", "dve"), ("l8", "dve"), ("l16", "dve"),
         ("l32_0", "act"), ("l32_1", "act"), ("xt0", "dve"), ("xt1", "dve")]
X_SEQ = [("kt0", "act"), ("kt1", "act"), ("kv0", "dve"), ("kv1", "dve"), ("kv2", "dve"), ("kv3", "dve")]
F_SEQ = [(f"{n}_{p}", e) for p in range(PAIRS)
         for n, e in (("fc0", "act"), ("fc1", "act"), ("fc2", "act"), ("fc3", "act"), ("pj", "product"), ("st", "stats"))]
RB_SEQ = {"l1_0": 0, "l1_1": 1, "l2": 0, "l4": 1, "l8": 0, "l16": 1, "l32": 0}


class Ring:

    def __init__(self, seq, depth, filled, emptied, before={}):
        self.names = [n for n, _ in seq]
        self.by = [e for _, e in seq]
        self.n, self.depth, self.filled, self.emptied = len(seq), depth, filled, emptied
        self.before = before
        assert self.n % depth == 0

    def bank(self, name):
        return self.names.index(name) % self.depth

    def full(self, it, name):
        return it * self.n + self.names.index(name) + 1 + self.before.get("filled", 0)

    def read(self, it, name):
        i = self.names.index(name)
        return it * self.by.count(self.by[i]) + self.by[:i + 1].count(self.by[i]) + self.before.get(self.by[i], 0)

    def wait_free(self, eng, it, name, first):
        i = self.names.index(name) - self.depth
        if i < 0 and first and "filled" not in self.before:
            return
        before = self.names[i % self.n]
        eng.wait_ge(self.emptied[self.by[i % self.n]], self.read(it if i >= 0 else it - 1, before))


class FeedForward:

    def __init__(self, alone, normalise=None, tokens=None, up=None, stats=None, down=None, bias=None, finish=None, normed=None, late=None):
        self.alone, self.tokens, self.up, self.stats, self.down = alone, tokens, up, stats, down
        self.normalise, self.bias, self.finish, self.normed = normalise, bias, finish, normed
        self.late = late


def rwkv_ffn_kernel(nc, x_ch, x_tok, w_all, w1, w2a, w2b, td1, td2, par, wfc, wpj, ffn_wb, c_f32, c_mask, out,
                    tiles=TILES):
    with ExitStack() as ctx:
        def sb(name, shape, dt=F32):
            return ctx.enter_context(nc.sbuf_tensor(name, shape, dt))

        def sem(name):
            return ctx.enter_context(nc.semaphore(name))

        WALL = sb("WALL", [128, 5, KC, C])
        W1 = sb("W1", [128, KC, 5 * MIXR])
        W2A = sb("W2A", [128, C])
        TD1 = sb("TD1", [128, KC, DECR])
        TD2W2 = sb("TD2W2", [DECR + MIXR, C])
        TD2, W2B = TD2W2[0:DECR, :], TD2W2[DECR:DECR + MIXR, :]
        PAR = sb("PAR", [128, KC, NPAR])
        WFC = sb("WFC", [128, KC, HID], F16)
        WPJ = sb("WPJ", [128, MH, C], F16)
        FWB = sb("FWB", [128, 2, MH])
        WSUM = sb("WSUM", [128, C])
        BSUM = sb("BSUM", [128, C])
        CF = sb("CF", [128, c_f32.shape[1]])
        CM = sb("CM", [128, c_mask.shape[1]], U32)
        o = 0
        IDENT = CF[:, o:o + 128]; o += 128
        BLKMASK = CF[:, o:o + 128]; o += 128
        ONES = CF[:, o:o + 128]; o += 128
        HEAD_MEAN = CF[:, o:o + HPG]; o += HPG
        MASK1 = CF[:, o:o + BLK]; o += BLK
        EPS = CF[:, o:o + 2]; o += 2
        ZERO = CF[:, o:o + 1]; o += 1
        MINUS_HALF = CF[:, o:o + 1]; o += 1

        ARENA1 = sb("ARENA1", [128, 8192])
        ARENA2 = sb("ARENA2", [128, 8192])
        RB = [ARENA1[:, 2048 * i:2048 * (i + 1)].rearrange("p (c h t) -> p c h t", c=KC, h=HPG) for i in range(2)]
        AB = ARENA1[:, 4096:6144].rearrange("p (h t) -> p h t", h=HEADS)
        A = ARENA1[:, 6144:7168]
        RSX = A.rearrange("p (q n) -> p q n", q=PAIRS)
        K1 = ARENA1[:, 7168:8192]
        KT = ARENA1[:, 7168:8192].rearrange("p (q n) -> p q n", q=PAIRS)
        S = ARENA2[:, 0:2048].rearrange("p (b c n) -> p b c n", b=B, c=KC)
        XF = [ARENA2[:, 2048 + 1024 * i:3072 + 1024 * i] for i in range(2)]
        YSB, YSQ = XF
        KM = ARENA2[:, 4096:5120]
        RM = ARENA2[:, 5120:6144]
        XTOK = KM.rearrange("p (h c) -> p h c", h=PAIRS)
        D = ARENA2[:, 6144:7168]
        G = ARENA2[:, 7168:8192]

        XT = sb("XT", [128, KC * B, CH + 1])
        XX = sb("XX", [128, KC * B, CH])
        TMA = sb("TMA", [128, COLS])
        TZTM = sb("TZTM", [DECR + MIXR, COLS])
        TZ, TMB = TZTM[0:DECR, :], TZTM[DECR:DECR + MIXR, :]
        TOT = {1: D}
        for n in (2, 4, 8, 16, 32, 64):
            TOT[n] = sb(f"TOT{n}", [128, KC * COLS // n])[:, :]
        V = sb("V", [128, PAIRS, C])
        KVM = D.rearrange("p (i n) -> p i n", i=2)
        RS = sb("RS", [128, PAIRS, KC, HPG])
        X1 = sb("X1", [128, PAIRS, C])
        BNS = sb("BNS", [128, PAIRS, 6])
        MV = sb("MV", [128, PAIRS, 2])
        RSTD = sb("RSTD", [128, PAIRS])
        XHI = sb("XHI", [128, PAIRS, KC, 128], F16)
        XLO = sb("XLO", [128, PAIRS, KC, 128], F16)
        GF = sb("GF", [128, 2, 512])
        GSQ = sb("GSQ", [128, 2, 512])
        GW = sb("GW", [128, 512])
        HHI = sb("HHI", [128, MH, 128], F16)
        HLO = sb("HLO", [128, MH, 128], F16)
        GA = sb("GA", [128, 512])
        QA = sb("QA", [128, 512])
        GR = sb("GR", [128, 2, 128])
        ST = sb("ST", [128, PAIRS, 4])
        FV, FSC = sb("FV", [128, PAIRS]), sb("FSC", [128, PAIRS])
        FBN = sb("FBN", [128, PAIRS, 6])
        FMV = sb("FMV", [128, PAIRS, 2])
        OSD = sb("OSD", [128, PAIRS])
        OUT = sb("OUT", [128, PAIRS, C])
        VHI, VLO = sb("VHI", [128, 2, MH], F16), sb("VLO", [128, 2, MH], F16)
        BELOW = [h[:, :, :].rearrange("p m t -> p (m t)") for h in (HHI, HLO)]
        PAUSE = sb("PAUSE", [1, 8])
        SC = sb("SC", [128, 32])
        AMAX = SC[:, 0:2]
        RED = GF[:, 0, 0:256]
        VMEAN = GF[:, 1, 0:KC * HEADS]

        psP = ctx.enter_context(nc.psum_tensor("psP", [128, 2, 512], F32))
        psW = ctx.enter_context(nc.psum_tensor("psW", [128, 2, 512], F32))
        psX = ctx.enter_context(nc.psum_tensor("psX", [128, 512], F32))
        psY = ctx.enter_context(nc.psum_tensor("psY", [128, 512], F32))
        psF = ctx.enter_context(nc.psum_tensor("psF", [128, 2, 512], F32))

        const_in, weights_in, values_in = sem("const_in"), sem("weights_in"), sem("values_in")
        raw_in = [sem(f"raw_in{k}") for k in range(8)]
        below_ready = sem("below_ready")
        xt_in, xtok_in, out_stored = sem("xt_in"), sem("xtok_in"), sem("out_stored")
        quantised = sem("quantised")
        su_dve, su_pe, su_pool = sem("setup_dve"), sem("setup_pe"), sem("setup_pool")
        p_full, p_act, p_dve = sem("p_full"), sem("p_read_act"), sem("p_read_dve")
        m_full, m_dve = sem("m_full"), sem("m_read_dve")
        w_full, w_act, w_dve = sem("w_full"), sem("w_read_act"), sem("w_read_dve")
        x_full, x_act, x_dve = sem("x_full"), sem("x_read_act"), sem("x_read_dve")
        tm_first, tm_ready, down_step = sem("tm_first"), sem("tm_ready"), sem("down_step")
        f_full, f_act = sem("f_full"), sem("f_read_act")
        f_stats, f_product = sem("f_read_stats"), sem("f_read_product")
        y_full, y_copied, y_squared = sem("y_full"), sem("y_copied"), sem("y_squared")
        xx_ready, xm_ready, xf_ready = sem("xx_ready"), sem("xm_ready"), sem("xf_ready")
        gate_tanh, d_ready = sem("gate_tanh"), sem("d_ready")
        k1_even, k1_odd = sem("k1_even"), sem("k1_odd")
        rb_act, rb_dve = sem("rb_act"), sem("rb_dve")
        r_scaled, k_scaled, tot_ready = sem("r_scaled"), sem("k_scaled"), sem("tot_ready")
        ab_diag = sem("ab_diag")
        s_decayed, s_ready = sem("s_decayed"), sem("s_ready")
        rs_inv, y_affine, z_ready = sem("rs_inv"), sem("y_affine"), sem("z_ready")
        bn_done, mv_ready, rstd_ready = sem("bn_done"), sem("mv_ready"), sem("rstd_ready")
        x1_ready, xhi_ready, x1_biased = sem("x1_ready"), sem("xhi_ready"), sem("x1_biased")
        g_squared, gw_ready = sem("g_squared"), sem("gw_ready")
        hhi_ready, hlo_ready, sums_added, sums_folded = sem("hhi_ready"), sem("hlo_ready"), sem("sums_added"), sem("sums_folded")
        root_taken = sem("root_taken")
        setup_step, st_step, o_step, out_ready = sem("setup_step"), sem("st_step"), sem("o_step"), sem("out_ready")

        P = Ring(P_SEQ, 2, p_full, {"act": p_act, "dve": p_dve})
        M = Ring(M_SEQ, 2, m_full, {"dve": m_dve, "tanh": tm_ready}, {"filled": 2, "dve": 2, "tanh": 2})
        M_BANKS = (psX, psY)
        W = Ring(W_SEQ, 2, w_full, {"act": w_act, "dve": w_dve})
        X = Ring(X_SEQ, 1, x_full, {"act": x_act, "dve": x_dve})
        F = Ring(F_SEQ, 2, f_full, {"act": f_act, "stats": f_stats, "product": f_product})

        xprev, xcur = XT[:, :, 0:CH], XT[:, :, 1:CH + 1]

        def cc(buf, c):
            return buf[:, c * COLS:(c + 1) * COLS]

        def halves(buf, n):
            v = buf.rearrange("p (q two n) -> p q two n", two=2, n=n)
            return v[:, :, 0, :], v[:, :, 1, :]

        def grow(v, n):
            return v.unsqueeze(2).broadcast_to([v.shape[0], v.shape[1], n])

        def rows(h):
            return slice(HD * h, HD * (h + 1))

        def level_queries(i, n, h):
            return (RB[i % 2][rows(h), :, h, :].rearrange("p c (q n) -> p c q n", n=n),
                    halves(RM[rows(h), :], n)[1].rearrange("p (c q) n -> p c q n", c=KC))

        NPL = len(LEVELS) + 2
        NWEIGHTS = 9
        POOL_PARTS = (2, 5, 7)

        def over_tiles(eng, attention, feed_forward):
            assert tiles > 2
            attention(0, True, None)
            attention(1, False, feed_forward(0, None))
            with eng.Fori(2, tiles) as it:
                attention(it, False, feed_forward(eng.snap(it - 1), eng.snap(it - 2)))
            feed_forward(tiles - 1, tiles - 2).alone()

        block = ctx.enter_context(nc.Block())

        @block.sync
        def _(sp):
            for dst, src in ((CF[:, :], c_f32), (CM[:, :], c_mask), (PAR[:, :, :], par), (FWB[:, :, :], ffn_wb)):
                sp.dma_start(dst, src).then_inc(const_in, 16)
            for k in range(4):
                sp.dma_start(ARENA1[:, 2048 * k:2048 * (k + 1)], wfc[:, 2048 * k:2048 * (k + 1)]).then_inc(raw_in[k], 16)
            for k in range(4):
                sp.dma_start(ARENA2[:, 2048 * k:2048 * (k + 1)], wpj[:, 2048 * k:2048 * (k + 1)]).then_inc(raw_in[4 + k], 16)
            sp.dma_start(XT[:, :, :], x_ch[0]).then_inc(xt_in, 16)
            sp.dma_start(WALL[:, W_V, :, :], w_all[:, W_V, :, :]).then_inc(values_in, 16)
            for dst, src in ((W1[:, :, :], w1), (W2A[:, :], w2a), (W2B[:, :], w2b), (TD1[:, :, :], td1),
                             (TD2[:, :], td2), (WALL[:, W_K, :, :], w_all[:, W_K, :, :])):
                sp.dma_start(dst, src).then_inc(weights_in, 16)
            for w in (W_R, W_G, W_O):
                sp.dma_start(WALL[:, w, :, :], w_all[:, w, :, :]).then_inc(weights_in, 16)


            def tile(it, first, ffn):
                if ffn:
                    ffn.late()
                sp.wait_ge(xf_ready, 5 * (it + 1))
                nxt = sp.snap(it + 1) if not isinstance(it, int) else it + 1
                sp.dma_start(XT[:, :, :], x_ch[nxt]).then_inc(xt_in, 16)
                sp.wait_ge(x_full, X.full(it, "kt1"))
                sp.dma_start(XTOK[:, :, :], x_tok[it]).then_inc(xtok_in, 16)
                if ffn:
                    ffn.finish()

            def feed_forward(j, before):
                first = before is None
                def store(j, p):
                    sp.wait_ge(out_ready, PAIRS * j + p + 1)
                    sp.dma_start(out[j, :, p, :], OUT[:, p, :]).then_inc(out_stored, 16)

                def late():
                    if not first:
                        store(before, 1)

                def alone():
                    late()
                    store(j, 0)
                    store(j, 1)
                return FeedForward(finish=lambda: store(j, 0), late=late, alone=alone)

            over_tiles(sp, tile, feed_forward)
            sp.wait_ge(out_stored, 16 * PAIRS * tiles)

        @block.tensor
        def _(pe):
            pe.wait_ge(su_dve, 1)
            pe.wait_ge(const_in, 16 * 4)
            pe.matmul(psP[:, 0, 0:1], ONES, SC[:, 8:9], start=True, stop=True).then_inc(su_pe, 1)
            pe.wait_ge(su_dve, 2)
            pe.matmul(psP[:, 1, 0:1], ONES, SC[:, 9:10], start=True, stop=True).then_inc(su_pe, 1)
            pe.wait_ge(su_dve, 3)
            pe.transpose(psX[0:2, 0:128], SC[:, 10:12], IDENT).then_inc(su_pe, 1)
            pe.wait_ge(su_dve, 4)
            pe.matmul(psY[:, 0:1], ONES[0:2, :], SC[0:2, 14:15], start=True, stop=True)
            pe.matmul(psY[:, 1:2], ONES[0:2, :], SC[0:2, 15:16], start=True, stop=True).then_inc(su_pe, 1)

            def against_second(v):
                for m in range(MH):
                    for part, h in enumerate((VHI, VLO)):
                        mm = pe.matmul(psW[:, v, :], h[:, v, m:m + 1].broadcast_to([128, 128]), WPJ[:, m, :],
                                       start=(m == 0 and part == 0), stop=(m == MH - 1 and part == 1))
                mm.then_inc(su_pe, 1)

            pe.wait_ge(su_dve, 5)
            pe.wait_ge(quantised, 8)
            against_second(0)
            pe.wait_ge(weights_in, 16 * NWEIGHTS)
            pe.wait_ge(su_pool, 1)

            def tanh_argument(ps, lo, n):
                for k in range(KC):
                    mm = pe.matmul(ps, W1[:, k, lo:lo + n], cc(XF[1], k), start=(k == 0), stop=(k == KC - 1))
                return mm

            pe.wait_ge(xm_ready, 1)
            tanh_argument(psX[:, 0:COLS], 0, 4 * MIXR).then_inc(tm_first, 1)
            tanh_argument(psY[0:MIXR, 0:COLS], 4 * MIXR, MIXR).then_inc(tm_first, 1)
            against_second(1)

            def mix(t, f, name, wait_free):
                pe.wait_ge(tm_ready, M.read(t, "w1a" if f < 4 else "w1b"))
                lhs, rhs = (W2A[rows(f), :], TMA[rows(f), :]) if f < 4 else (W2B[:, :], TMB[:, :])
                for g in range(2):
                    wait_free(f"{name}{g}")
                    for c in range(2):
                        mm = pe.matmul(M_BANKS[M.bank(f"{name}{g}")][:, COLS * c:COLS * (c + 1)],
                                       lhs[:, 128 * (2 * g + c):128 * (2 * g + c + 1)], rhs, start=True, stop=True)
                    mm.then_inc(m_full, 1)

            pe.wait_ge(tm_ready, 2)
            mix(-1, 0, "mw", lambda name: None)

            def tile(it, first, ffn):
                def wait_free(name):
                    M.wait_free(pe, it, name, first)

                def channels(name, w, f, slot, groups=(0, 1)):
                    pe.wait_ge(xf_ready, 5 * it + f + 1)
                    for g in groups:
                        P.wait_free(pe, it, f"{name}{g}", first)
                        for c in range(2):
                            for k in range(KC):
                                mm = pe.matmul(psP[:, P.bank(f"{name}{g}"), COLS * c:COLS * (c + 1)],
                                               WALL[:, w, k, 128 * (2 * g + c):128 * (2 * g + c + 1)], cc(XF[slot], k),
                                               start=(k == 0), stop=(k == KC - 1))
                        mm.then_inc(p_full, 1)

                mix(it - 1, 1, "mk", wait_free)
                pe.wait_ge(xf_ready, 5 * it + 1)
                P.wait_free(pe, it, "td1", first)
                for k in range(KC):
                    mm = pe.matmul(psP[0:DECR, P.bank("td1"), 0:COLS], TD1[:, k, :], cc(XF[0], k),
                                   start=(k == 0), stop=(k == KC - 1))
                mm.then_inc(p_full, 1)
                mix(it - 1, 2, "mv", wait_free)
                pe.wait_ge(p_act, P.read(it, "td1"))
                for g in range(2):
                    P.wait_free(pe, it, f"td2{g}", first)
                    for c in range(2):
                        mm = pe.matmul(psP[:, P.bank(f"td2{g}"), COLS * c:COLS * (c + 1)],
                                       TD2[:, 128 * (2 * g + c):128 * (2 * g + c + 1)], TZ[:, :], start=True, stop=True)
                    mm.then_inc(p_full, 1)
                if ffn:
                    ffn.tokens()
                channels("k", W_K, 1, 1)
                if ffn:
                    ffn.up(0, 0)
                mix(it - 1, 3, "mr", wait_free)
                pe.wait_ge(xf_ready, 5 * it + 3)
                for p in range(PAIRS):
                    P.wait_free(pe, it, f"v{p}", first)
                    for k in range(KC):
                        mm = pe.matmul(psP[:, P.bank(f"v{p}"), :], cc(XF[0], k)[:, 128 * p:128 * (p + 1)],
                                       WALL[:, W_V, k, :], start=(k == 0), stop=(k == KC - 1))
                    mm.then_inc(p_full, 1)
                if ffn:
                    ffn.up(0, 1)
                mix(it - 1, 4, "mg", wait_free)
                channels("r", W_R, 3, 1)
                if ffn:
                    ffn.up(0, 2)
                channels("g", W_G, 4, 0, (0,))

                pe.wait_ge(k1_odd, it + 1)
                pe.wait_ge(k1_even, 2 * it + 2)
                for p in range(PAIRS):
                    name = f"l1_{p}"
                    W.wait_free(pe, it, name, first)
                    pe.wait_ge(rb_dve, 7 * it + p + 1)
                    pe.wait_ge(rb_act, 7 * it + p + 1)
                    for q in range(4):
                        for c in range(KC):
                            o = 128 * p + BLK * q
                            mm = pe.matmul(psW[BLK * q:BLK * (q + 1), W.bank(name), 128 * c:128 * (c + 1)],
                                           cc(K1, c)[:, o:o + BLK], RB[p][:, c, :, BLK * q:BLK * (q + 1)],
                                           start=True, stop=True, skip_group_check=True)
                    mm.then_inc(w_full, 1)
                if ffn:
                    ffn.up(0, 3)
                channels("g", W_G, 4, 0, (1,))
                for i, n in enumerate(LEVELS):
                    name = f"l{n}"
                    W.wait_free(pe, it, name, first)
                    pe.wait_ge(k_scaled, NPL * it + i + 1)
                    pe.wait_ge(rb_act, 7 * it + i + 3)
                    pe.wait_ge(rb_dve, 7 * it + i + 3)
                    for q in range(8):
                        for c in range(KC):
                            o = 256 * (q // 4) + 64 * c
                            mm = pe.matmul(psW[BLK * (q % 4):BLK * (q % 4 + 1), W.bank(name), o:o + 64],
                                           cc(KM, c)[:, BLK * q:BLK * (q + 1)],
                                           RB[RB_SEQ[name]][:, c, :, 16 * q:16 * (q + 1)],
                                           start=True, stop=True, skip_group_check=True)
                    mm.then_inc(w_full, 1)
                    if ffn:
                        ffn.down(0, i)
                pe.wait_ge(k_scaled, NPL * it + 5)
                pe.wait_ge(rb_act, 7 * it + 7)
                pe.wait_ge(rb_dve, 7 * it + 7)
                for p in range(PAIRS):
                    name = f"l32_{p}"
                    W.wait_free(pe, it, name, first)
                    for h in range(2):
                        b = 2 * p + h
                        for c in range(KC):
                            mm = pe.matmul(psW[64 * h:64 * h + BLK, W.bank(name), 128 * c:128 * (c + 1)],
                                           cc(KM, c)[:, CH * b:CH * b + BLK], RB[0][:, c, :, BLK * b:BLK * (b + 1)],
                                           start=True, stop=True, skip_group_check=True)
                    mm.then_inc(w_full, 1)
                if ffn:
                    ffn.stats(0)

                def keys(p):
                    X.wait_free(pe, it, f"kt{p}", first)
                    for c in range(KC):
                        mm = pe.transpose(psX[:, 128 * c:128 * (c + 1)], cc(KM, c)[:, 128 * p:128 * (p + 1)], IDENT)
                    mm.then_inc(x_full, 1)

                def from_state(p):
                    if p:
                        pe.wait_ge(y_copied, 2 * it + 1)
                    elif not first:
                        pe.wait_ge(x_dve, X.read(it - 1, "kv3"))
                    for c in range(KC):
                        for h in range(2):
                            b = 2 * p + h
                            pe.matmul(psY[:, 128 * c + CH * h:128 * c + CH * (h + 1)], S[:, b, c, :],
                                      cc(RM, c)[:, CH * b:CH * (b + 1)], start=(c == 0 and h == 0), stop=False,
                                      skip_group_check=True)

                def from_chunk(p):
                    pe.wait_ge(ab_diag, 2 * it + p + 1)
                    pe.wait_ge(w_act, W.read(it, f"l32_{p}"))
                    for c in range(KC):
                        for h in range(HPG):
                            mm = pe.matmul(psY[rows(h), 128 * c:128 * (c + 1)], V[:, p, 128 * c + HD * h:128 * c + HD * (h + 1)],
                                           AB[:, HPG * c + h, :], start=False, stop=True, skip_group_check=True)
                    mm.then_inc(y_full, 1)

                pe.wait_ge(m_dve, M.read(it, "mg1"))
                pe.wait_ge(k_scaled, NPL * it + 6)
                keys(0)
                pe.wait_ge(r_scaled, NPL * it + 6)
                pe.wait_ge(p_act, P.read(it, "v1"))
                pe.wait_ge(su_pool, 2)
                if not first:
                    pe.wait_ge(s_ready, B * it)
                from_state(0)
                keys(1)
                from_chunk(0)
                if ffn:
                    ffn.up(1, 0)
                from_state(1)
                if ffn:
                    ffn.up(1, 1)
                from_chunk(1)
                pe.wait_ge(x_act, X.read(it, "kt1"))
                for b in range(B):
                    if b == 1:
                        pe.wait_ge(y_copied, 2 * it + 2)
                    elif b > 1:
                        pe.wait_ge(x_dve, X.read(it, f"kv{b - 2}"))
                    r = slice(CH * (b % 2), CH * (b % 2 + 1))
                    for c in range(KC):
                        mm = pe.matmul((psX, psY)[b % 2][:, 128 * c:128 * (c + 1)], KT[r, b // 2, 128 * c:128 * (c + 1)],
                                       V[r, b // 2, 128 * c:128 * (c + 1)], start=True, stop=True, skip_group_check=True)
                    mm.then_inc(x_full, 1)
                    if ffn and b < 2:
                        ffn.up(1, 2 + b)
                    elif ffn and b == 2:
                        ffn.down(1, 0)
                pe.wait_ge(y_squared, 2 * it + 2)
                P.wait_free(pe, it, "var", first)
                for p in range(PAIRS):
                    for c in range(KC):
                        o = HEADS * p + HPG * c
                        mm = pe.matmul(psP[:, P.bank("var"), o:o + HPG], cc(YSQ, c)[:, 128 * p:128 * (p + 1)], HEAD_MEAN,
                                       start=True, stop=True, skip_group_check=True)
                mm.then_inc(p_full, 1)
                if ffn:
                    ffn.down(1, 1)
                    ffn.down(1, 2)
                pe.wait_ge(rs_inv, 2 * it + 2)
                for g in range(2):
                    P.wait_free(pe, it, f"rb{g}", first)
                    for c in range(2):
                        for p in range(PAIRS):
                            mm = pe.transpose(psP[:, P.bank(f"rb{g}"), COLS * c + 128 * p:COLS * c + 128 * (p + 1)],
                                              RSX[:, p, 128 * (2 * g + c):128 * (2 * g + c + 1)], IDENT)
                    mm.then_inc(p_full, 1)
                pe.wait_ge(xm_ready, it + 2)
                pe.wait_ge(x_dve, X.read(it, "kv3"))
                for name, lo, n in (("w1a", 0, 4 * MIXR), ("w1b", 4 * MIXR, MIXR)):
                    wait_free(name)
                    tanh_argument(M_BANKS[M.bank(name)][0:n, 0:COLS], lo, n).then_inc(m_full, 1)
                pe.wait_ge(z_ready, 2 * it + 2)
                for p in range(PAIRS):
                    P.wait_free(pe, it, f"wo{p}", first)
                    for k in range(KC):
                        mm = pe.matmul(psP[:, P.bank(f"wo{p}"), :], cc(YSB, k)[:, 128 * p:128 * (p + 1)], WALL[:, W_O, k, :],
                                       start=(k == 0), stop=(k == KC - 1))
                    mm.then_inc(p_full, 1)
                if ffn:
                    ffn.stats(1)
                mix(it, 0, "mw", wait_free)
                if ffn:
                    ffn.down(1, 3)

            def feed_forward(j, before):
                first = before is None
                def tokens():
                    for p in range(PAIRS):
                        pe.wait_ge(x1_ready, 2 * j + p + 1)
                        W.wait_free(pe, j, f"xt{p}", first)
                        for c in range(KC):
                            mm = pe.transpose(psW[:, W.bank(f"xt{p}"), 128 * c:128 * (c + 1)], X1[:, p, 128 * c:128 * (c + 1)], IDENT)
                        mm.then_inc(w_full, 1)

                def up(p, g):
                    if g == 0:
                        pe.wait_ge(w_dve, W.read(j, f"xt{p}"))
                    name = f"fc{g}_{p}"
                    F.wait_free(pe, j, name, first)
                    for m in range(4):
                        for k in range(KC):
                            for part, x in enumerate((XHI, XLO)):
                                mm = pe.matmul(psF[:, F.bank(name), 128 * m:128 * (m + 1)],
                                               WFC[:, k, 128 * (4 * g + m):128 * (4 * g + m + 1)], x[:, p, k, :],
                                               start=(k == 0 and part == 0), stop=(k == KC - 1 and part == 1))
                    mm.then_inc(f_full, 1)

                def stats(p):
                    pe.wait_ge(sums_folded, 2 * j + p + 1)
                    F.wait_free(pe, j, f"st_{p}", first)
                    for i in range(2):
                        mm = pe.matmul(psF[:, F.bank(f"st_{p}"), i:i + 1], GR[:, i, :], ONES[:, 0:1], start=True, stop=True)
                    mm.then_inc(f_full, 1)

                def down(p, part):
                    pe.wait_ge(hlo_ready, 8 * j + 4 * p + part + 1)
                    if part == 0:
                        F.wait_free(pe, j, f"pj_{p}", first)
                    for m in range(MH // 4 * part, MH // 4 * (part + 1)):
                        for h in (HHI, HLO):
                            mm = pe.matmul(psF[:, F.bank(f"pj_{p}"), :], h[:, m, :], WPJ[:, m, :],
                                           start=(m == 0 and h is HHI), stop=(m == MH - 1 and h is HLO))
                    mm.then_inc(f_full if part == 3 else down_step, 1)

                def alone():
                    tokens()
                    for p in range(PAIRS):
                        for g in range(4):
                            up(p, g)
                        for part in range(4):
                            down(p, part)
                        stats(p)
                return FeedForward(tokens=tokens, up=up, stats=stats, down=down, alone=alone)

            over_tiles(pe, tile, feed_forward)

        @block.scalar
        def _(act):
            act.wait_ge(su_dve, 6)
            act.wait_ge(su_pool, 2)
            act.wait_ge(tm_first, 1)
            act.activation(TMA[:, :], psX[:, 0:COLS], ACT.Tanh).then_inc(tm_ready, 1)
            act.wait_ge(tm_first, 2)
            act.activation(TMB[:, :], psY[0:MIXR, 0:COLS], ACT.Tanh).then_inc(tm_ready, 1)

            def copy(o, i):
                return act.activation(o, i, ACT.Copy)

            def tile(it, first, ffn):
                act.wait_ge(p_full, P.full(it, "td1"))
                act.activation(TZ[:, :], psP[0:DECR, P.bank("td1"), 0:COLS], ACT.Tanh).then_inc(p_act, 1)
                if not first:
                    act.wait_ge(tot_ready, NPL * it)
                    act.wait_ge(r_scaled, NPL * it)
                    act.wait_ge(k_scaled, NPL * it)
                    act.wait_ge(s_ready, B * it)
                for g in range(2):
                    act.wait_ge(p_full, P.full(it, f"td2{g}"))
                    for c in range(2):
                        k = 2 * g + c
                        e = act.activation(cc(D, k), psP[:, P.bank(f"td2{g}"), COLS * c:COLS * (c + 1)], ACT.Exp,
                                           bias=PAR[:, k, DECAY:DECAY + 1])
                    e.then_inc(p_act, 1)
                act.wait_ge(p_act, P.read(it, "td21"))
                act.activation(D, D, ACT.Exp, scale=-1.0).then_inc(d_ready, 1)
                if ffn:
                    ffn.tokens()
                if not first:
                    act.wait_ge(x_full, X.full(it - 1, "kv3"))
                    act.wait_ge(p_dve, P.read(it - 1, "wo1"))
                for g in range(2):
                    act.wait_ge(p_full, P.full(it, f"k{g}"))
                    src = psP[:, P.bank(f"k{g}"), :]
                    copy(halves(K1[:, 512 * g:512 * (g + 1)], 1)[0], halves(src, 1)[0]).then_inc(k1_even, 1)
                    copy(KM[:, 512 * g:512 * (g + 1)], src).then_inc(p_act, 1)
                for p in range(PAIRS):
                    act.wait_ge(p_full, P.full(it, f"v{p}"))
                    if ffn and p == 0:
                        ffn.up(0, 0)
                    copy(V[:, p, :], psP[:, P.bank(f"v{p}"), :]).then_inc(p_act, 1)
                for g in range(2):
                    act.wait_ge(p_full, P.full(it, f"r{g}"))
                    if ffn and g == 0:
                        ffn.up(0, 1)
                    copy(RM[:, 512 * g:512 * (g + 1)], psP[:, P.bank(f"r{g}"), :]).then_inc(p_act, 1)
                act.wait_ge(p_act, P.read(it, "r1"))
                for p in range(PAIRS):
                    if not first:
                        act.wait_ge(w_full, W.full(it - 1, "l32_1" if p == 0 else "l16"))
                    for h in range(HPG):
                        e = copy(RB[p][rows(h), :, h, 1:128:2],
                                 RM[rows(h), :].rearrange("p (c t) -> p c t", c=KC)[:, :, 128 * p + 1:128 * (p + 1):2])
                    e.then_inc(rb_act, 1)
                if ffn:
                    ffn.up(0, 2)
                def gate(g):
                    act.wait_ge(p_full, P.full(it, f"g{g}"))
                    act.activation(G[:, 512 * g:512 * (g + 1)], psP[:, P.bank(f"g{g}"), :], ACT.Tanh, scale=0.5).then_inc(gate_tanh, 1)

                if not first:
                    act.wait_ge(z_ready, 2 * it)
                gate(0)
                for i, n in enumerate(LEVELS + (BLK,)):
                    act.wait_ge(r_scaled, NPL * it + i + 1)
                    act.wait_ge(w_full, W.full(it, W_SEQ[i][0]))
                    for h in range(HPG - 1):
                        dst, src = level_queries(i, n, h)
                        e = copy(dst, src)
                    e.then_inc(rb_act, 1)
                    if i == 0:
                        if ffn:
                            ffn.up(0, 3)
                        gate(1)

                def matrices(p):
                    if not first or p:
                        act.wait_ge(y_full, 2 * it + p)
                    if p == 0:
                        act.wait_ge(w_dve, W.read(it, "l16"))
                    for q in range(4):
                        r = slice(BLK * q, BLK * (q + 1))
                        e = copy(AB[r, :, BLK * q:BLK * (q + 1)],
                                 A[r, 512 * p:512 * (p + 1)].rearrange("p (h t) -> p h t", h=HEADS))
                    e.then_inc(ab_diag, 1)
                    act.wait_ge(w_full, W.full(it, f"l32_{p}"))
                    for h in range(2):
                        r = slice(64 * h, 64 * h + BLK)
                        e = copy(AB[r, :, 64 * h + BLK:64 * h + 2 * BLK],
                                 psW[r, W.bank(f"l32_{p}"), :].rearrange("p (h t) -> p h t", h=HEADS))
                    e.then_inc(w_act, 1)

                def squares(p):
                    act.wait_ge(y_copied, 2 * it + p + 1)
                    act.activation(YSQ.rearrange("p (c t) -> p c t", c=KC)[:, :, 128 * p:128 * (p + 1)],
                                   YSB.rearrange("p (c t) -> p c t", c=KC)[:, :, 128 * p:128 * (p + 1)], ACT.Square).then_inc(y_squared, 1)

                matrices(0)
                for q in range(PAIRS):
                    act.wait_ge(x_full, X.full(it, f"kt{q}"))
                    copy(KT[:, q, :], psX[:, :]).then_inc(x_act, 1)
                matrices(1)
                squares(0)
                if ffn:
                    ffn.up(1, 0)
                    ffn.up(1, 1)
                squares(1)
                if ffn:
                    for g in range(2, 4):
                        ffn.up(1, g)
                act.wait_ge(p_full, P.full(it, "var"))
                act.activation(RS[:, :, :, :], psP[:, P.bank("var"), 0:PAIRS * HEADS].rearrange("p (q c h) -> p q c h", q=PAIRS, c=KC),
                               ACT.Sqrt, bias=EPS[:, 0:1]).then_inc(p_act, 1)
                act.wait_ge(m_full, M.full(it, "w1a"))
                act.activation(TMA[:, :], M_BANKS[M.bank("w1a")][:, 0:COLS], ACT.Tanh).then_inc(tm_ready, 1)
                act.wait_ge(m_full, M.full(it, "w1b"))
                act.activation(TMB[:, :], M_BANKS[M.bank("w1b")][0:MIXR, 0:COLS], ACT.Tanh).then_inc(tm_ready, 1)

            def feed_forward(j, before):
                first = before is None

                def tokens():
                    for p in range(PAIRS):
                        act.wait_ge(w_full, W.full(j, f"xt{p}"))
                        copy(XHI[:, p, :, :], psW[:, W.bank(f"xt{p}"), :].rearrange("p (c t) -> p c t", c=KC)).then_inc(xhi_ready, 1)

                def up(p, g):
                    u = 4 * p + g
                    act.wait_ge(f_full, F.full(j, f"fc{g}_{p}"))
                    if u >= 2 or not first:
                        act.wait_ge(gw_ready, 8 * j + u - 1)
                        act.wait_ge(sums_added, 8 * j + u - 1)
                    act.activation(GF[:, u % 2, :], psF[:, F.bank(f"fc{g}_{p}"), :], ACT.Gelu).then_inc(f_act, 1)
                    act.wait_ge(f_act, 8 * j + u + 1)
                    act.activation(GSQ[:, u % 2, :], GF[:, u % 2, :], ACT.Square).then_inc(g_squared, 1)

                def alone():
                    tokens()
                    for p in range(PAIRS):
                        for g in range(4):
                            up(p, g)
                return FeedForward(tokens=tokens, up=up, alone=alone)

            over_tiles(act, tile, feed_forward)

        @block.gpsimd
        def _(pool):
            pool.wait_ge(setup_step, 9)
            for n, k in enumerate(POOL_PARTS):
                arena, i = (ARENA1, ARENA2)[k // 4], k // 4
                if n:
                    pool.wait_ge(quantised, POOL_PARTS[n - 1] + 1)
                pool.wait_ge(raw_in[k], 16)
                pool.tensor_scalar(BELOW[1], arena[:, 2048 * (k % 4):2048 * (k % 4 + 1)], SC[:, 20 + i:21 + i], None,
                                   ALU.is_lt).then_inc(below_ready, 1)
            pool.wait_ge(quantised, 4)
            pool.memset(ARENA1[:, 0:6144], 0.0).then_inc(su_pool, 1)
            pool.wait_ge(quantised, 8)
            pool.memset(ARENA2[:, 0:2048], 0.0).then_inc(su_pool, 1)
            pool.wait_ge(su_dve, 6)
            pool.wait_ge(su_pool, 2)

            def inverse_root(v):
                return pool.tensor_tensor(v, v, MINUS_HALF.broadcast_to([128, v.shape[1]]), ALU.pow)

            def tile(it, first, ffn):
                pool.wait_ge(xt_in, 16 * (it + 1))
                for f, name in ((1, "mk1"), (2, "mv1"), (3, "mr1"), (4, "mg1")):
                    pool.wait_ge(m_dve, M.read(it, name))
                    v = XF[f % 2].rearrange("p (q t) -> p q t", t=CH)
                    pool.tensor_tensor(v, v, xcur, ALU.add).then_inc(xf_ready, 1)
                    if f == 2 and ffn:
                        ffn.late()
                    if f == 3:
                        pool.wait_ge(p_act, P.read(it, "k1"))
                        pool.tensor_tensor(halves(K1, 1)[1].rearrange("p (c q) n -> p c (q n)", c=KC),
                                           halves(KM, 1)[1].rearrange("p (c q) n -> p c (q n)", c=KC),
                                           PAR[:, :, U:U + 1].broadcast_to([128, KC, COLS // 2]), ALU.mult).then_inc(k1_odd, 1)
                        if ffn:
                            ffn.up(0, 0)
                if ffn:
                    ffn.up(0, 1)
                    ffn.bias()
                    ffn.up(0, 2)
                    ffn.up(0, 3)
                    ffn.finish()

                def decay(b):
                    pool.wait_ge(y_full, 2 * it + b // 2 + 1)
                    tot = TOT[64].rearrange("p (c b) -> p b c", b=B)[:, b, :]
                    pool.tensor_tensor(S[:, b, :, :], S[:, b, :, :], grow(tot, 128), ALU.mult).then_inc(s_decayed, 1)

                def update(b):
                    pool.wait_ge(s_decayed, B * it + b + 1)
                    pool.wait_ge(x_dve, X.read(it, f"kv{b}"))
                    pool.tensor_tensor(S[:, b, :, :], S[:, b, :, :], KVM[:, b % 2, :].rearrange("p (c n) -> p c n", c=KC),
                                       ALU.add).then_inc(s_ready, 1)

                pool.wait_ge(tot_ready, NPL * it + 6)
                decay(0)
                decay(1)
                if ffn:
                    ffn.up(1, 0)
                    ffn.up(1, 1)
                decay(2)
                decay(3)
                for b in range(B):
                    update(b)
                    if ffn and b < 2:
                        ffn.up(1, 2 + b)
                pool.wait_ge(p_dve, P.read(it, "g0"))
                pool.wait_ge(y_affine, KC * it + 2)
                pool.tensor_tensor(YSB[:, 0:512], YSB[:, 0:512], G[:, 0:512], ALU.mult).then_inc(z_ready, 1)
                pool.wait_ge(mv_ready, 2 * (it + 1))
                inverse_root(RSTD[:, :]).then_inc(rstd_ready, 1)

            def feed_forward(j, before):
                first = before is None
                def up(p, g):
                    u = 4 * p + g
                    for acc, src, ready, n in ((GA, GF, f_act, 1), (QA, GSQ, g_squared, 2)):
                        pool.wait_ge(ready, 8 * j + u + 1)
                        if g == 0:
                            if p or not first:
                                pool.wait_ge(sums_folded, 2 * j + p)
                            e = pool.tensor_tensor(acc[:, :], src[:, u % 2, :], ZERO.broadcast_to([128, 512]), ALU.add)
                        else:
                            if n == 1:
                                pool.wait_ge(sums_added, 8 * j + u)
                            e = pool.tensor_tensor(acc[:, :], acc[:, :], src[:, u % 2, :], ALU.add)
                    e.then_inc(sums_added, 1)

                def bias():
                    if not first:
                        pool.wait_ge(out_stored, 16 * PAIRS * j)
                    for p in range(PAIRS):
                        pool.wait_ge(x1_ready, PAIRS * j + p + 1)
                        pool.tensor_tensor(OUT[:, p, :], X1[:, p, :], BSUM[:, :], ALU.add).then_inc(x1_biased, 1)

                def finish(j, p):
                    pool.wait_ge(st_step, 4 * (PAIRS * j + p) + 3)
                    inverse_root(FV[:, p:p + 1]).then_inc(root_taken, 1)
                    pool.wait_ge(o_step, 3 * (PAIRS * j + p) + 3)
                    inverse_root(OSD[:, p:p + 1]).then_inc(root_taken, 1)

                def late():
                    if not first:
                        finish(before, 1)

                def alone():
                    late()
                    bias()
                    for p in range(PAIRS):
                        for g in range(4):
                            up(p, g)
                        finish(j, p)
                return FeedForward(up=up, bias=bias, finish=lambda: finish(j, 0), late=late, alone=alone)

            over_tiles(pool, tile, feed_forward)

        @block.vector
        def _(dve):
            def after_wait(i):
                dve.memset(PAUSE[:, i:i + 1], 0.0)

            dve.wait_ge(const_in, 16 * 4)
            for i, arena in enumerate((ARENA1, ARENA2)):
                for k in range(4):
                    dve.wait_ge(raw_in[4 * i + k], 16)
                    e = dve.tensor_reduce(RED[:, 128 * i + 32 * k:128 * i + 32 * (k + 1)],
                                          arena[:, 2048 * k:2048 * (k + 1)].rearrange("p (q n) -> p q n", n=64), AX.X, ALU.add,
                                          apply_absolute_value=True)
                e.then_inc(setup_step, 1)
                dve.wait_ge(setup_step, i + 1)
                dve.tensor_reduce(SC[:, 8 + i:9 + i], RED[:, 128 * i:128 * (i + 1)], AX.X, ALU.add).then_inc(su_dve, 1)
            dve.tensor_reduce(SC[:, 10:12], FWB[:, :, :], AX.X, ALU.max, apply_absolute_value=True).then_inc(su_dve, 1)
            dve.wait_ge(su_pe, 3)
            dve.tensor_reduce(SC[0:2, 12:13], psX[0:2, 0:128], AX.X, ALU.max).then_inc(setup_step, 1)
            dve.wait_ge(setup_step, 3)
            dve.tensor_scalar(SC[0:2, 14:16], IDENT[0:2, 0:2], SC[0:2, 12:13], None, ALU.mult).then_inc(su_dve, 1)
            dve.wait_ge(su_pe, 4)
            dve.tensor_scalar(AMAX, psY[:, 0:2], 1e-30, None, ALU.max).then_inc(setup_step, 1)
            dve.wait_ge(setup_step, 4)
            dve.reciprocal(SC[:, 2:4], AMAX).then_inc(setup_step, 1)
            dve.wait_ge(setup_step, 5)
            dve.tensor_scalar(FWB[:, 0, :], FWB[:, 0, :], SC[:, 2:3], None, ALU.mult)
            dve.tensor_scalar(FWB[:, 1, :], FWB[:, 1, :], SC[:, 3:4], None, ALU.mult).then_inc(setup_step, 1)
            for i in range(2):
                dve.wait_ge(su_pe, i + 1)
                dve.tensor_scalar(SC[:, 16 + i:17 + i], psP[:, i, 0:1], 1.0 / (C * HID), GAMMA_EPS, ALU.mult, ALU.add).then_inc(setup_step, 1)
            dve.wait_ge(setup_step, 8)
            dve.tensor_scalar(SC[:, 18:20], SC[:, 16:18], 0.5, None, ALU.mult)
            dve.tensor_scalar(SC[:, 20:22], SC[:, 16:18], -0.5, None, ALU.mult).then_inc(setup_step, 1)
            dve.wait_ge(setup_step, 9)
            n = 9
            for k in range(8):
                arena, dst, i = (ARENA1, ARENA2)[k // 4], (WFC, WPJ)[k // 4], k // 4
                part = slice(2048 * (k % 4), 2048 * (k % 4 + 1))
                if k in POOL_PARTS:
                    dve.wait_ge(below_ready, POOL_PARTS.index(k) + 1)
                else:
                    if k:
                        dve.wait_ge(quantised, k)
                    dve.tensor_scalar(BELOW[0], arena[:, part], SC[:, 20 + i:21 + i], None, ALU.is_lt).then_inc(setup_step, 1)
                    n += 1
                    dve.wait_ge(setup_step, n)
                dve.scalar_tensor_tensor(out=dst[:, :, :].rearrange("p a n -> p (a n)")[:, part], in0=arena[:, part],
                                         scalar=SC[:, 18 + i:19 + i], in1=BELOW[k in POOL_PARTS], op0=ALU.is_gt,
                                         op1=ALU.subtract).then_inc(quantised, 1)
            dve.tensor_copy(VHI[:, :, :], FWB[:, :, :]).then_inc(setup_step, 1)
            n += 1
            dve.wait_ge(setup_step, n)
            dve.tensor_tensor(VLO[:, :, :], FWB[:, :, :], VHI[:, :, :], ALU.subtract).then_inc(su_dve, 1)
            dve.wait_ge(values_in, 16)
            wv = WALL[:, W_V, :, :].rearrange("p k (h j) -> p (k h) j", j=HD)
            dve.tensor_reduce(VMEAN, wv, AX.X, ALU.add).then_inc(setup_step, 1)
            n += 1
            dve.wait_ge(setup_step, n)
            dve.tensor_scalar(VMEAN, VMEAN, 1.0 / HD, None, ALU.mult).then_inc(setup_step, 1)
            n += 1
            dve.wait_ge(setup_step, n)
            dve.tensor_tensor(wv, wv, grow(VMEAN, HD), ALU.subtract)
            dve.tensor_scalar(PAR[:, :, LN_G:LN_B + 1], PAR[:, :, LN_G:LN_B + 1], 0.5, None, ALU.mult).then_inc(su_dve, 1)
            dve.wait_ge(su_dve, 6)
            dve.wait_ge(quantised, 8)

            def differences(it):
                dve.wait_ge(xt_in, 16 * (it + 1))
                dve.tensor_tensor(XX[:, :, :], xprev, xcur, ALU.subtract).then_inc(xx_ready, 1)

            def mixed_by_x(it):
                dve.wait_ge(xx_ready, it + 1)
                for k in range(KC):
                    q = slice(B * k, B * (k + 1))
                    e = dve.scalar_tensor_tensor(out=cc(XF[1], k).rearrange("p (q t) -> p q t", t=CH), in0=XX[:, q, :],
                                                 scalar=PAR[:, k, MAA_X:MAA_X + 1], in1=xcur[:, q, :], op0=ALU.mult, op1=ALU.add)
                e.then_inc(xm_ready, 1)

            def mix(t, f, name, before):
                if before:
                    dve.wait_ge(p_full, P.full(t, before))
                for g in range(2):
                    dve.wait_ge(m_full, M.full(t, f"{name}{g}"))
                    for c in range(2):
                        k = 2 * g + c
                        e = dve.scalar_tensor_tensor(
                            out=cc(XF[f % 2], k), in0=M_BANKS[M.bank(f"{name}{g}")][:, COLS * c:COLS * (c + 1)],
                            scalar=PAR[:, k, MIX_PAR[f]:MIX_PAR[f] + 1],
                            in1=XX[:, B * k:B * (k + 1), :].rearrange("p q t -> p (q t)"), op0=ALU.add, op1=ALU.mult)
                    e.then_inc(m_dve, 1)

            def decay_input(t, before):
                mix(t, 0, "mw", before)
                dve.wait_ge(m_dve, M.read(t, "mw1"))
                v = XF[0].rearrange("p (q t) -> p q t", t=CH)
                dve.tensor_tensor(v, v, xcur, ALU.add).then_inc(xf_ready, 1)

            differences(0)
            mixed_by_x(0)
            dve.wait_ge(su_pe, 6)
            dve.tensor_copy(WSUM[:, :], psW[:, 0, :])
            dve.tensor_scalar(BSUM[:, :], psW[:, 1, :], AMAX[:, 1:2], None, ALU.mult).then_inc(su_dve, 1)
            decay_input(-1, None)

            def tile(it, first, ffn):
                dve.wait_ge(tm_ready, M.read(it - 1, "w1b"))
                mix(it, 1, "mk", None)
                if ffn:
                    ffn.normalise()
                mix(it, 2, "mv", "td1")
                if ffn:
                    ffn.late()
                    ffn.tokens()
                mix(it, 3, "mr", "k1")
                if ffn:
                    ffn.up(0, 0)
                mix(it, 4, "mg", "v1")
                if ffn:
                    ffn.up(0, 1)
                def queries(i, n):
                    dve.wait_ge(r_scaled, NPL * it + i + 1)
                    dve.wait_ge(w_full, W.full(it, W_SEQ[i][0]))
                    dst, src = level_queries(i, n, HPG - 1)
                    dve.tensor_copy(dst, src).then_inc(rb_dve, 1)

                def scale(i, n):
                    tl, tr = TOT[n].rearrange("p (q two) -> p two q", two=2)[:, 0, :], TOT[n].rearrange("p (q two) -> p two q", two=2)[:, 1, :]
                    right = halves(RM, n)[1]
                    dve.wait_ge(rb_act, 7 * it + i + 2)
                    dve.wait_ge(rb_dve, 7 * it + i + 2)
                    dve.tensor_tensor(right, right, grow(tl, n), ALU.mult).then_inc(r_scaled, 1)
                    if 0 < i < NPL - 1:
                        queries(i, 2 * n)
                    if i == 0:
                        dve.wait_ge(k1_odd, it + 1)
                    else:
                        dve.wait_ge(w_full, W.full(it, f"l{n}" if n < 32 else "l32_1"))
                    left = halves(KM, n)[0]
                    dve.tensor_tensor(left, left, grow(tr, n), ALU.mult).then_inc(k_scaled, 1)
                    dve.tensor_tensor(TOT[2 * n], tl, tr, ALU.mult).then_inc(tot_ready, 1)
                    dve.wait_ge(tot_ready, NPL * it + i + 1)
                    dve.wait_ge(r_scaled, NPL * it + i + 1)
                    dve.wait_ge(k_scaled, NPL * it + i + 1)

                dve.wait_ge(p_act, P.read(it, "r1"))
                for p in range(PAIRS):
                    if not first:
                        dve.wait_ge(w_full, W.full(it - 1, "l32_1" if p == 0 else "l16"))
                    for h in range(HPG):
                        e = dve.tensor_tensor(RB[p][rows(h), :, h, 0:128:2],
                                               RM[rows(h), :].rearrange("p (c t) -> p c t", c=KC)[:, :, 128 * p:128 * (p + 1):2],
                                               PAR[rows(h), :, U:U + 1].broadcast_to([HD, KC, 64]), ALU.mult)
                    e.then_inc(rb_dve, 1)
                dve.wait_ge(d_ready, it + 1)
                scale(0, 1)
                queries(0, 2)
                if not first:
                    dve.wait_ge(p_dve, P.read(it - 1, "rb1"))
                    dve.wait_ge(ab_diag, 2 * it)
                for p in range(PAIRS):
                    dve.wait_ge(w_full, W.full(it, f"l1_{p}"))
                    dve.tensor_tensor(A[:, 512 * p:512 * (p + 1)].rearrange("p (h t) -> p h t", t=BLK),
                                      psW[:, W.bank(f"l1_{p}"), :].rearrange("p (h t) -> p h t", t=BLK),
                                      MASK1.unsqueeze(1).broadcast_to([128, HEADS, BLK]), ALU.mult).then_inc(w_dve, 1)
                dve.wait_ge(w_dve, W.read(it, "l1_1"))
                if ffn:
                    ffn.up(0, 2)
                    ffn.up(0, 3)
                for i, n in enumerate(LEVELS):
                    scale(i + 1, n)
                    av = A.rearrange("p (h q two n) -> p h q two n", two=2, n=n, h=2 * HEADS)[:, :, :, 1, :]
                    nq = 16 // n
                    data = psW[:, W.bank(f"l{n}"), :].rearrange("p (h q n) -> p h q n", h=2 * HEADS, n=n)
                    mask = CM[:, 16 * i:16 * (i + 1)].rearrange("p (q n) -> p q n", n=n).unsqueeze(1).broadcast_to([128, 2 * HEADS, nq, n])
                    after_wait(i)
                    dve.copy_predicated(av, mask, data).then_inc(w_dve, 1)
                    dve.wait_ge(w_dve, W.read(it, f"l{n}"))
                if ffn:
                    ffn.stats(0)
                scale(5, 32)
                if ffn:
                    ffn.finish()
                for g in range(2):
                    dve.wait_ge(gate_tanh, 2 * it + g + 1)
                    dve.scalar_tensor_tensor(out=G[:, 512 * g:512 * (g + 1)], in0=G[:, 512 * g:512 * (g + 1)], scalar=1.0,
                                             in1=psP[:, P.bank(f"g{g}"), :], op0=ALU.add, op1=ALU.mult).then_inc(p_dve, 1)
                for p in range(PAIRS):
                    dve.wait_ge(y_full, 2 * it + p + 1)
                    dve.tensor_copy(YSB.rearrange("p (c t) -> p c t", c=KC)[:, :, 128 * p:128 * (p + 1)],
                                    psY[:, :].rearrange("p (c t) -> p c t", c=KC)).then_inc(y_copied, 1)
                    if ffn and p == 0:
                        ffn.normed()
                        ffn.up(1, 0)
                        ffn.up(1, 1)
                for b in range(B):
                    dve.wait_ge(x_full, X.full(it, f"kv{b}"))
                    if b >= 2 or not first:
                        dve.wait_ge(s_ready, B * it + b - 1)
                    dve.tensor_tensor(KVM[:, b % 2, :].rearrange("p (c n) -> p c n", c=KC), (psX, psY)[b % 2][:, :].rearrange("p (c n) -> p c n", c=KC),
                                      BLKMASK.unsqueeze(1).broadcast_to([128, KC, 128]), ALU.mult).then_inc(x_dve, 1)
                    if ffn and b < 2:
                        ffn.up(1, 2 + b)
                dve.wait_ge(m_dve, M.read(it, "mg1"))
                differences(it + 1)
                dve.wait_ge(p_full, P.full(it, "var"))
                mixed_by_x(it + 1)
                dve.wait_ge(p_act, P.read(it, "var"))
                dve.reciprocal(RS[:, :, :, :], RS[:, :, :, :]).then_inc(rs_inv, 1)
                dve.wait_ge(rs_inv, 2 * it + 1)
                dve.wait_ge(ab_diag, 2 * it + 2)
                dve.tensor_copy(RSX.rearrange("p q (h j) -> p (q h) j", j=HD),
                                grow(RS[:, :, :, :].rearrange("p q c h -> p (q c h)"), HD)).then_inc(rs_inv, 1)
                if ffn:
                    ffn.stats(1)
                dve.wait_ge(y_copied, 2 * it + 2)
                for g in range(2):
                    dve.wait_ge(p_full, P.full(it, f"rb{g}"))
                    v = YSB[:, 512 * g:512 * (g + 1)]
                    dve.tensor_tensor(v, v, psP[:, P.bank(f"rb{g}"), :], ALU.mult).then_inc(p_dve, 1)
                    dve.wait_ge(p_dve, P.read(it, f"rb{g}"))
                    for k in (2 * g, 2 * g + 1):
                        dve.tensor_scalar(cc(YSB, k), cc(YSB, k), PAR[:, k, LN_G:LN_G + 1], PAR[:, k, LN_B:LN_B + 1],
                                          ALU.mult, ALU.add).then_inc(y_affine, 1)
                dve.wait_ge(y_affine, KC * it + 4)
                dve.wait_ge(p_dve, P.read(it, "g1"))
                dve.tensor_tensor(YSB[:, 512:1024], YSB[:, 512:1024], G[:, 512:1024], ALU.mult).then_inc(z_ready, 1)
                dve.wait_ge(xtok_in, 16 * (it + 1))
                if not first:
                    dve.wait_ge(x1_biased, 2 * it)
                for p in range(PAIRS):
                    dve.wait_ge(p_full, P.full(it, f"wo{p}"))
                    dve.tensor_tensor(X1[:, p, :], psP[:, P.bank(f"wo{p}"), :], XTOK[:, p, :], ALU.add).then_inc(p_dve, 1)
                    dve.wait_ge(p_dve, P.read(it, f"wo{p}"))
                    dve.bn_stats(BNS[:, p, :], X1[:, p, :]).then_inc(bn_done, 1)
                decay_input(it, "wo1")
                dve.wait_ge(bn_done, 2 * it + 2)
                after_wait(4)
                dve.bn_aggr(MV[:, 0, :], BNS[:, 0, :])
                dve.bn_aggr(MV[:, 1, :], BNS[:, 1, :]).then_inc(mv_ready, 1)
                dve.wait_ge(mv_ready, 2 * it + 1)
                dve.tensor_scalar(RSTD[:, :], MV[:, :, 1], LN_EPS, None, ALU.add).then_inc(mv_ready, 1)

            def feed_forward(j, before):
                first = before is None
                def normalise():
                    dve.wait_ge(rstd_ready, j + 1)
                    for p in range(PAIRS):
                        dve.tensor_scalar(X1[:, p, :], X1[:, p, :], MV[:, p, 0:1], RSTD[:, p:p + 1],
                                          ALU.subtract, ALU.mult).then_inc(x1_ready, 1)

                def tokens():
                    for p in range(PAIRS):
                        dve.wait_ge(xhi_ready, 2 * j + p + 1)
                        dve.tensor_tensor(XLO[:, p, :, :], psW[:, W.bank(f"xt{p}"), :].rearrange("p (c t) -> p c t", c=KC),
                                          XHI[:, p, :, :], ALU.subtract).then_inc(w_dve, 1)

                def up(p, g):
                    u = 4 * p + g
                    dve.wait_ge(f_act, 8 * j + u + 1)
                    if p or not first:
                        if g == 3:
                            dve.wait_ge(f_full, F.full(j if p else j - 1, f"pj_{1 - p}"))
                        else:
                            dve.wait_ge(down_step, 6 * j + 3 * p - 2 + g)
                    if u or not first:
                        dve.wait_ge(hlo_ready, 8 * j + u)
                    dve.tensor_tensor(GW[:, :].rearrange("p (m t) -> p m t", m=4), GF[:, u % 2, :].rearrange("p (m t) -> p m t", m=4),
                                      grow(FWB[:, 0, 4 * g:4 * (g + 1)], 128), ALU.mult).then_inc(gw_ready, 1)
                    dve.wait_ge(gw_ready, 8 * j + u + 1)
                    gw = GW[:, :].rearrange("p (m t) -> p m t", m=4)
                    dve.tensor_copy(HHI[:, 4 * g:4 * (g + 1), :], gw).then_inc(hhi_ready, 1)
                    dve.wait_ge(hhi_ready, 8 * j + u + 1)
                    dve.tensor_tensor(HLO[:, 4 * g:4 * (g + 1), :], gw, HHI[:, 4 * g:4 * (g + 1), :], ALU.subtract).then_inc(hlo_ready, 1)

                def stats(p):
                    dve.wait_ge(sums_added, 8 * j + 4 * p + 4)
                    dve.tensor_reduce(GR[:, 0, :], GA[:, :].rearrange("p (m t) -> p t m", m=4), AX.X, ALU.add)
                    dve.tensor_reduce(GR[:, 1, :], QA[:, :].rearrange("p (m t) -> p t m", m=4), AX.X, ALU.add).then_inc(sums_folded, 1)

                def finish(j, p):
                    st, s = ST[:, p, :], 4 * (PAIRS * j + p)
                    dve.wait_ge(f_full, F.full(j, f"st_{p}"))
                    dve.tensor_scalar(st[:, 0:2], psF[:, F.bank(f"st_{p}"), 0:2], 1.0 / HID, None, ALU.mult).then_inc(f_stats, 1)
                    dve.wait_ge(f_stats, F.read(j, f"st_{p}"))
                    dve.tensor_scalar(st[:, 2:3], st[:, 0:1], -1.0, None, ALU.mult).then_inc(st_step, 1)
                    dve.wait_ge(st_step, s + 1)
                    pj = psF[:, F.bank(f"pj_{p}"), :]
                    dve.scalar_tensor_tensor(out=pj, in0=WSUM[:, :], scalar=st[:, 2:3], in1=pj, op0=ALU.mult, op1=ALU.add)
                    dve.scalar_tensor_tensor(out=st[:, 3:4], in0=st[:, 0:1], scalar=st[:, 2:3], in1=st[:, 1:2],
                                             op0=ALU.mult, op1=ALU.add).then_inc(st_step, 1)
                    dve.wait_ge(st_step, s + 2)
                    dve.tensor_scalar(FV[:, p:p + 1], st[:, 3:4], 0.0, LN_EPS, ALU.max, ALU.add).then_inc(st_step, 1)
                    dve.wait_ge(root_taken, 2 * (PAIRS * j + p) + 1)
                    dve.tensor_scalar(FSC[:, p:p + 1], FV[:, p:p + 1], AMAX[:, 0:1], None, ALU.mult).then_inc(st_step, 1)
                    dve.wait_ge(st_step, s + 4)
                    dve.wait_ge(x1_biased, PAIRS * j + p + 1)
                    dve.scalar_tensor_tensor(out=OUT[:, p, :], in0=pj, scalar=FSC[:, p:p + 1], in1=OUT[:, p, :],
                                             op0=ALU.mult, op1=ALU.add).then_inc(f_product, 1)

                def normed(j, p):
                    dve.wait_ge(f_product, F.read(j, f"pj_{p}"))
                    dve.bn_stats(FBN[:, p, :], OUT[:, p, :]).then_inc(o_step, 1)
                    dve.wait_ge(o_step, 3 * (PAIRS * j + p) + 1)
                    after_wait(5 + p)
                    dve.bn_aggr(FMV[:, p, :], FBN[:, p, :]).then_inc(o_step, 1)
                    dve.wait_ge(o_step, 3 * (PAIRS * j + p) + 2)
                    dve.tensor_scalar(OSD[:, p:p + 1], FMV[:, p, 1:2], LN_EPS, None, ALU.add).then_inc(o_step, 1)
                    dve.wait_ge(root_taken, 2 * (PAIRS * j + p) + 2)
                    dve.tensor_scalar(OUT[:, p, :], OUT[:, p, :], FMV[:, p, 0:1], OSD[:, p:p + 1],
                                      ALU.subtract, ALU.mult).then_inc(out_ready, 1)

                def late():
                    if not first:
                        finish(before, 1)
                        normed(before, 1)

                def alone():
                    normalise()
                    tokens()
                    late()
                    for p in range(PAIRS):
                        for g in range(4):
                            up(p, g)
                        stats(p)
                        finish(j, p)
                        normed(j, p)
                return FeedForward(normalise=normalise, tokens=tokens, up=up, stats=stats, finish=lambda: finish(j, 0), normed=lambda: normed(j, 0),
                                   late=late, alone=alone)

            over_tiles(dve, tile, feed_forward)


def _constants():
    p = np.arange(128)
    ident = np.eye(128)
    blk = (p[:, None] // HD == p[None, :] // HD) * 1.0
    ones = np.ones((128, 128))
    head_mean = (p[:, None] // HD == np.arange(HPG)[None, :]) / HD
    s, t = p[:, None] % BLK, np.arange(BLK)[None, :]
    mask1 = ((s == t) | ((s % 2 == 0) & (t == s + 1))) * 1.0
    eps = np.tile(np.array([[GN_EPS, LN_EPS, 0.0, -0.5]]), (128, 1))
    f = np.concatenate([ident, blk, ones, head_mean, mask1, eps], 1).astype(np.float32)
    masks = []
    for n in LEVELS:
        r = np.arange(16)[None, :]
        masks.append((s // (2 * n) == r // n) & (s % (2 * n) < n))
    return f, np.concatenate(masks, 1).astype(np.uint32)


def kernel(**inputs):
    import concourse.bacc as _bacc
    from concourse.bass_utils import run_bass_kernel_spmd as _run

    g = {k.replace("L0_attn_", "a_").replace("L0_ffn_", "f_"): np.asarray(v) for k, v in inputs.items()}

    def by_part(w):
        return w.reshape(-1, 128, w.shape[-1]).transpose(1, 0, 2)

    x = g["a_x"]
    padded = np.pad(x, ((0, 0), (1, 0), (0, 0)))
    cuts = np.stack([padded[:, i * CH:i * CH + CH + 1] for i in range(TILES)])
    cuts = np.concatenate([cuts, np.zeros_like(cuts[:1])])
    x_ch = cuts.reshape(TILES + 1, B, CH + 1, KC, 128).transpose(0, 4, 3, 1, 2).reshape(TILES + 1, 128, KC * B, CH + 1)
    x_tok = x.reshape(PAIRS, 2, TILES, CH, C).transpose(2, 1, 3, 0, 4).reshape(TILES, 128, PAIRS, C)
    w_all = np.stack([by_part(g[n].T) for n in ("a_Wr", "a_Wk", "a_Wv", "a_Wg", "a_Wo")], 1)
    par = np.stack([g[n].reshape(KC, 128).T for n in
                    ("a_time_maa_x", "a_time_maa_w", "a_time_maa_k", "a_time_maa_v", "a_time_maa_r", "a_time_maa_g",
                     "a_time_decay", "a_u", "a_ln_g", "a_ln_b")], 2)
    c_f32, c_mask = _constants()
    arrays = {
        "x_ch": x_ch, "x_tok": x_tok, "w_all": w_all,
        "w1": by_part(g["a_maa_w1"]), "w2a": g["a_maa_w2"][0:4].reshape(128, C), "w2b": g["a_maa_w2"][4],
        "td1": by_part(g["a_td_w1"]), "td2": g["a_td_w2"], "par": par,
        "wfc": by_part(g["f_W_fc"].T).reshape(128, -1), "wpj": by_part(g["f_W_proj"].T).reshape(128, -1),
        "ffn_wb": np.stack([g["f_ln_w"].reshape(MH, 128).T, g["f_ln_b"].reshape(MH, 128).T], 1),
        "c_f32": c_f32, "c_mask": c_mask,
    }
    arrays = {k: np.ascontiguousarray(v) for k, v in arrays.items()}
    nc = _bacc.Bacc("TRN2", target_bir_lowering=False, num_devices=1)
    args = [nc.dram_tensor(k, a.shape, mybir.dt.from_np(a.dtype), kind="ExternalInput").ap() for k, a in arrays.items()]
    args.append(nc.dram_tensor("out", (TILES, 128, PAIRS, C), F32, kind="ExternalOutput").ap())
    rwkv_ffn_kernel(nc, *args)
    r = _run(nc, [arrays], core_ids=[0])
    out = r.results[0]["out"]
    return np.ascontiguousarray(out.reshape(TILES, 2, CH, PAIRS, C).transpose(3, 1, 0, 2, 4).reshape(B, T, C))
```
